# Optimizing a Trainium2 kernel written in Bass

```python
import numpy as np
import jax
import jax.numpy as jnp

def _softmax(x, axis=-1):
    return jax.nn.softmax(x, axis=axis)

def _gelu(x):
    return jax.nn.gelu(x, approximate=True)

def _silu(x):
    return jax.nn.silu(x)

def _sigmoid(x):
    return jax.nn.sigmoid(x)

def _layernorm(x, axis=-1, eps=1e-05):
    m = jnp.mean(x, axis=axis, keepdims=True)
    v = jnp.var(x, axis=axis, keepdims=True)
    return (x - m) / jnp.sqrt(v + eps)

def _scatter_add(tgt, idx, src, axis=0):
    return tgt.at[idx].add(src)

def _segment_sum(src, seg, n):
    return jax.ops.segment_sum(src, seg, n)
kernel_name = 'mk_gnn_ffn_d1_gnn_r8_05fa95'

def setup_inputs(seed: int=0):
    np.random.seed(seed)
    _w = jnp.asarray

    def _rec_inputs():
        import jax
        import jax.numpy as jnp
        _gk = jax.random.key(seed)
        x = -0.0003713 + 1 * jax.random.normal(jax.random.fold_in(_gk, 1), (6250, 256), jnp.float32)
        src = jax.random.randint(jax.random.fold_in(_gk, 2), (100000,), 0, 6250, jnp.int32)
        dst = jnp.minimum((6250 * jax.random.uniform(jax.random.fold_in(_gk, 3), (100000,)) ** 2.0).astype(jnp.int32), 49999)
        _o = jnp.argsort(dst, stable=True)
        src = src[_o]
        dst = dst[_o]
        return (x, src, dst)
    x, src, dst = _rec_inputs()

    def _L0_gnn_setup():
        import jax, jax.numpy as jnp
        import numpy as np
        N = 6250
        E = 200000
        F_IN = 256
        F_OUT = 256
        ALPHA = 0.2
        key = jax.random.key(seed)
        ks = jax.random.split(key, 7)
        x = jax.random.normal(ks[0], (N, F_IN), dtype=jnp.float32)
        row = jax.random.randint(ks[1], (E,), 0, N, dtype=jnp.int32)
        col = jax.random.randint(ks[2], (E,), 0, N, dtype=jnp.int32)
        W_w = jax.random.normal(ks[3], (F_IN, F_OUT), dtype=jnp.float32) / np.sqrt(F_IN).astype(np.float32)
        W_b = jax.random.normal(ks[4], (F_OUT,), dtype=jnp.float32) * 0.01
        a_w = jax.random.normal(ks[5], (2 * F_OUT,), dtype=jnp.float32) / np.sqrt(2 * F_OUT).astype(np.float32)
        a_b = jax.random.normal(ks[6], (1,), dtype=jnp.float32) * 0.01
        return {'x': x, 'W_w': W_w, 'W_b': W_b, 'a_w': a_w, 'a_b': a_b, 'row': row, 'col': col}
    _L0_gnn_all = _L0_gnn_setup()
    _L0_gnn_in = {k: v for k, v in _L0_gnn_all.items() if k in ('W_w', 'W_b', 'a_w', 'a_b')}
    del _L0_gnn_all

    def _L0_ffn_setup():
        import jax, jax.numpy as jnp
        import numpy as np
        TOP_K = 2
        key = jax.random.key(seed)
        ks = jax.random.split(key, 4)
        B, L, D, H, E = (8, 512, 256, 1024, 8)
        s = 0.02
        return {'x': jax.random.normal(ks[0], (B, L, D), jnp.float32), 'Wg': jax.random.normal(ks[1], (D, E), jnp.float32) * s, 'bg': jnp.zeros((E,), jnp.float32), 'W1': jax.random.normal(ks[2], (E, D, H), jnp.float32) * s, 'b1': jnp.zeros((E, H), jnp.float32), 'W2': jax.random.normal(ks[3], (E, H, D), jnp.float32) * s, 'b2': jnp.zeros((E, D), jnp.float32)}
    _L0_ffn_all = _L0_ffn_setup()
    _L0_ffn_in = {k: v for k, v in _L0_ffn_all.items() if k in ('Wg', 'bg', 'W1', 'b1', 'W2', 'b2')}
    del _L0_ffn_all
    return {'x': x, 'src': src, 'dst': dst, 'L0_gnn_W_w': _L0_gnn_in['W_w'], 'L0_gnn_W_b': _L0_gnn_in['W_b'], 'L0_gnn_a_w': _L0_gnn_in['a_w'], 'L0_gnn_a_b': _L0_gnn_in['a_b'], 'L0_ffn_Wg': _L0_ffn_in['Wg'], 'L0_ffn_bg': _L0_ffn_in['bg'], 'L0_ffn_W1': _L0_ffn_in['W1'], 'L0_ffn_b1': _L0_ffn_in['b1'], 'L0_ffn_W2': _L0_ffn_in['W2'], 'L0_ffn_b2': _L0_ffn_in['b2']}

def reference(x, src, dst, L0_gnn_W_w, L0_gnn_W_b, L0_gnn_a_w, L0_gnn_a_b, L0_ffn_Wg, L0_ffn_bg, L0_ffn_W1, L0_ffn_b1, L0_ffn_W2, L0_ffn_b2):
    import jax
    import jax.numpy as jnp

    def _L0_gnn_ref(x, W_w, W_b, a_w, a_b, row, col):
        import jax, jax.numpy as jnp
        import numpy as np
        N = 6250
        E = 200000
        F_IN = 256
        F_OUT = 256
        ALPHA = 0.2
        Wh = x @ W_w + W_b
        f_dst_part = Wh @ a_w[:F_OUT]
        f_row_part = Wh @ a_w[F_OUT:]
        e = f_dst_part[col] + f_row_part[row] + a_b[0]
        e = jnp.where(e > 0, e, ALPHA * e)
        m = jax.ops.segment_max(e, row, num_segments=N)
        ex = jnp.exp(e - m[row])
        denom = jax.ops.segment_sum(ex, row, num_segments=N)
        att = ex / denom[row]
        h_prime = jax.ops.segment_sum(att[:, None] * Wh[col], row, num_segments=N)
        return jax.nn.relu(h_prime)

    def _L0_ffn_ref(x, Wg, bg, W1, b1, W2, b2):
        import jax, jax.numpy as jnp
        import numpy as np
        TOP_K = 2
        B, L, D = x.shape
        E = W1.shape[0]
        xf = x.reshape(-1, D)
        gate_logits = xf @ Wg + bg
        top_w, top_i = jax.lax.top_k(gate_logits, TOP_K)
        top_w = jax.nn.softmax(top_w, axis=-1)
        w_dense = jnp.sum(jax.nn.one_hot(top_i, E, dtype=xf.dtype) * top_w[..., None], axis=1)
        out = jnp.zeros_like(xf)
        for e in range(E):
            h = jax.nn.gelu(xf @ W1[e] + b1[e], approximate=False)
            out = out + w_dense[:, e:e + 1] * (h @ W2[e] + b2[e])
        return out.reshape(B, L, D)
    x = x + _L0_gnn_ref(_layernorm(x, axis=-1), L0_gnn_W_w, L0_gnn_W_b, L0_gnn_a_w, L0_gnn_a_b, src, dst)
    x = x + _L0_ffn_ref(_layernorm(x, axis=-1)[None], L0_ffn_Wg, L0_ffn_bg, L0_ffn_W1, L0_ffn_b1, L0_ffn_W2, L0_ffn_b2)[0]
    return x

_drawn_inputs = setup_inputs


def setup_inputs(seed=0):
    import zlib

    import numpy as np

    out = dict(_drawn_inputs(seed))
    spreads = {'L0_ffn_bg': (0.0, 0.1), 'L0_ffn_b1': (0.0, 0.312), 'L0_ffn_b2': (0.0, 0.1)}
    factors = {'L0_gnn_W_b': 5.9}
    for name, (base, spread) in spreads.items():
        noise = np.random.default_rng([zlib.crc32(name.encode()), seed]).standard_normal(out[name].shape)
        drawn = base * np.exp(spread * noise) if base else spread * noise
        out[name] = jnp.asarray(drawn.astype(out[name].dtype))
    for name, factor in factors.items():
        out[name] = (out[name] * factor).astype(out[name].dtype)
    return out
```

```python
from contextlib import ExitStack

import numpy as np
import concourse.bass as bass
import concourse.mybir as mybir
from concourse.alu_op_type import AluOpType as ALU

FP32, BF16, FP16 = mybir.dt.float32, mybir.dt.bfloat16, mybir.dt.float16
I32, U16 = mybir.dt.int32, mybir.dt.uint16
ACT = mybir.ActivationFunctionType
X = mybir.AxisListType.X

P = 128
N, F, E = 6250, 256, 100000
NT = -(-N // P)
LAST = N - (NT - 1) * P
KT = F // P
EPS = 1e-5
SLOPE = 0.2
FAR = -1e30

HALVES = 2
EP = 125
ET = E // HALVES // EP
SLOTS = (E // HALVES + NT * (P - 1)) // P
G = 4
SLOTS = -(-SLOTS // (2 * G)) * 2 * G
GROUPS = SLOTS // G
TW = F + 2
COUNT, SCORE = F, F + 1
AW = F + 1

NE, H = 8, 1024
HC = H // P
TOPK = 2
XT = (N * TOPK + NE * (P - 1)) // P
XT += XT % 2


class Steps:

    def __init__(self, eng, sem):
        self.eng, self.sem, self.base, self.n = eng, sem, 0, 0

    def done(self, ins):
        ins.then_inc(self.sem, 1)
        self.n += 1

    def settle(self):
        self.eng.wait_ge(self.sem, self.base + self.n)

    def then(self, ins):
        self.done(ins)
        self.settle()


def repeat(eng, steps, count, per, body):
    start = steps.base + steps.n
    with eng.Fori(0, count) as it:
        steps.base, steps.n = it * per + start, 0
        body(it)
        assert steps.n == per, (steps.n, per)
    steps.base, steps.n = start + count * per, 0


def flat(ap):
    return ap.rearrange("p a b -> p (a b)")


def over_middle(ap, n):
    return ap.unsqueeze(1).broadcast_to([ap.shape[0], n, ap.shape[1]])


def over_last(ap, n):
    return ap.unsqueeze(2).broadcast_to([ap.shape[0], ap.shape[1], n])


def gnn_moe_kernel(nc, x, src, dst, W_w, W_b, a_w, a_b, Wg, bg, W1, b1, W2, b2, out):
    with ExitStack() as ctx:
        def sb(name, shape, dt=FP32, stack=ctx):
            return stack.enter_context(nc.sbuf_tensor(name, shape, dt))

        table = nc.dram_tensor("table", (NT * P, TW), FP32, kind="Internal").ap()
        xs = nc.dram_tensor("expert_in", (XT * P, F), FP32, kind="Internal").ap()
        ys = nc.dram_tensor("expert_out", (XT * P, F), FP32, kind="Internal").ap()

        x1 = nc.dram_tensor("residual", (NT * P, F), FP32, kind="Internal").ap()

        c = {}
        c["ident"] = sb("ident", [P, P])
        c["ident16"] = sb("ident16", [P, P], BF16)
        c["before"] = sb("before", [P, P])
        c["ones"] = sb("ones", [P, P])
        c["iota32"] = sb("iota32", [P, SLOTS], I32)
        c["iota"] = sb("iota", [P, SLOTS])
        c["iota16"] = sb("iota16", [P, SLOTS], FP16)
        c["eps"] = sb("eps", [P, 1])
        c["valid"] = sb("valid", [P, 1])
        row_score = sb("row_score", [P, NT])
        row_scoreT = sb("row_scoreT", [NT, P])
        g = {}
        g["pos"] = sb("pos", [P, TOPK, NT], I32)
        g["weight"] = sb("weight", [P, TOPK, NT])
        g["expert32"] = sb("expert32", [P, XT], I32)
        with ExitStack() as sums:
            acc = sb("acc", [P, NT + 1, AW], FP32, sums)
            constants(nc, c, acc)
            projection(nc, c, x, W_w, W_b, a_w, a_b, table, xs, row_score, row_scoreT)
            with ExitStack() as rounds:
                s = {}
                for name, shape, dt in [
                    ("cols", [P, SLOTS], I32),
                    ("rows", [P, SLOTS], FP32),
                    ("tile32", [P, SLOTS], I32),
                    ("fresh", [P, SLOTS], FP32),
                    ("rscore", [P, SLOTS], FP32),
                    ("floor", [P, SLOTS], FP32),
                    ("mx", [P, 1 + SLOTS], FP32),
                    ("lastsel", [NT, SLOTS], FP32),
                    ("absent", [NT, 1], FP32),
                ]:
                    s[name] = sb(name, shape, dt, rounds)
                for q in range(HALVES):
                    route_edges(nc, c, s, q, src, dst, row_scoreT)
                    attention(nc, c, s, q, table, acc)
            gate(nc, c, g, x, acc, Wg, bg, xs, x1)
        experts(nc, c, g, xs, ys, W1, b1, W2, b2)
        combine(nc, g, x1, ys, out)


def constants(nc, c, acc):
    with nc.semaphore("filled") as filled, nc.semaphore("cast") as cast, nc.Block() as block:
        @block.gpsimd
        def _(pool):
            pool.iota(c["iota32"][:, :], [[1, SLOTS]], base=0, channel_multiplier=0).then_inc(filled, 1)
            pool.memset(c["ones"][:, :], 1.0).then_inc(filled, 1)
            pool.memset(c["ident"][:, :], 0.0).then_inc(filled, 1)
            pool.memset(c["eps"][:, :], EPS)
            pool.wait_ge(filled, 3)
            pool.affine_select(out=c["ident"][:, :], in_=c["ident"][:, :], compare_op=ALU.not_equal, fill=1.0,
                               base=0, pattern=[[-1, P]], channel_multiplier=1).then_inc(filled, 1)
            pool.affine_select(out=c["before"][:, :], in_=c["ones"][:, :], compare_op=ALU.is_gt, fill=0.0,
                               base=0, pattern=[[1, P]], channel_multiplier=-1)
            pool.affine_select(out=c["valid"][:, :], in_=c["ones"][:, 0:1], compare_op=ALU.is_gt, fill=0.0,
                               base=LAST, pattern=[[1, 1]], channel_multiplier=-1)

        @block.vector
        def _(dve):
            dve.memset(acc[:, :, :], 0.0)
            dve.wait_ge(filled, 4)
            dve.tensor_copy(c["iota"][:, :], c["iota32"][:, :])
            dve.tensor_copy(c["iota16"][:, :], c["iota32"][:, :])
            dve.tensor_copy(c["ident16"][:, :], c["ident"][:, :])


def projection(nc, c, x, W_w, W_b, a_w, a_b, table, xs, row_score, row_scoreT):
    ctx = ExitStack()
    with ctx:
        sb = lambda n, s, d=FP32: ctx.enter_context(nc.sbuf_tensor(n, s, d))
        ps = lambda n, s, d=FP32: ctx.enter_context(nc.psum_tensor(n, s, d))
        sem = lambda n: ctx.enter_context(nc.semaphore(n))
        xa = sb("p_x", [P, NT, F])
        wh = sb("p_wh", [P, NT, TW])
        stats = sb("p_stats", [P, NT, 6])
        mv = sb("p_mv", [P, NT, 2])
        rstd = sb("p_rstd", [P, NT])
        xn = sb("p_xn", [P, 2, F])
        xT = sb("p_xT", [P, 2, KT, P])
        wx = sb("p_wx", [P, KT, TW])
        bx = sb("p_bx", [P, TW])
        av = sb("p_av", [P, 2, F])
        ab = sb("p_ab", [P, 1])
        junk = sb("p_junk", [P, F])
        zeros = sb("p_zeros", [P, F])
        low = sb("p_low", [P, 1])
        lowT = sb("p_lowT", [1, 1])
        lift = sb("p_lift", [P, 1])
        pT = [ps(f"p_pT{i}", [P, KT, P]) for i in range(2)]
        pW = [ps(f"p_pW{i}", [P, TW]) for i in range(2)]
        pL = ps("p_pL", [P, 512])
        loaded, weights, vec, cleared = sem("x_loaded"), sem("w_loaded"), sem("p_vec"), sem("p_cleared")
        spread, rooted, ready = sem("var_ready"), sem("std_ready"), sem("xn_ready")
        turned, kept, multiplied, added = sem("xT_psum"), sem("xT_sbuf"), sem("wh_psum"), sem("wh_sbuf")
        low_ready, low_turned, low_one, low_all = sem("low_ready"), sem("low_turned"), sem("low_one"), sem("low_all")
        shifted, rowT, stored, zeroed = sem("shifted"), sem("rowT"), sem("stored"), sem("zeroed")
        block = ctx.enter_context(nc.Block())

        @block.sync
        def _(sp):
            sp.dma_start(xa[:, 0:NT - 1, :], x[0:(NT - 1) * P, :].rearrange("(b p) f -> p b f", p=P)).then_inc(loaded, 16)
            sp.wait_ge(cleared, 1)
            sp.dma_start(xa[0:LAST, NT - 1, :], x[(NT - 1) * P:N, :]).then_inc(loaded, 16)
            sp.wait_ge(shifted, 1)
            sp.dma_start(table.rearrange("(b p) f -> p b f", p=P), wh[:, :, :]).then_inc(stored, 16)
            sp.wait_ge(stored, 16)

        @block.gpsimd
        def _(pool):
            pool.memset(xa[:, NT - 1, :], 0.0).then_inc(cleared, 1)
            pool.memset(zeros[:, :], 0.0).then_inc(cleared, 1)

        @block.scalar
        def _(act):
            act.dma_start(wx[:, :, 0:F], W_w.rearrange("(k p) f -> p k f", p=P)).then_inc(weights, 16)
            act.dma_start(bx[:, 0:F], W_b.rearrange("(a f) -> a f", a=1).partition_broadcast(P).rearrange("p a f -> p (a f)")).then_inc(weights, 16)
            act.dma_start(av[:, 0, :], a_w[F:2 * F].rearrange("(a f) -> a f", a=1).partition_broadcast(P).rearrange("p a f -> p (a f)")).then_inc(weights, 16)
            act.dma_start(av[:, 1, :], a_w[0:F].rearrange("(a f) -> a f", a=1).partition_broadcast(P).rearrange("p a f -> p (a f)")).then_inc(weights, 16)
            act.dma_start(ab[:, :], a_b.rearrange("(a f) -> a f", a=1).partition_broadcast(P).rearrange("p a f -> p (a f)")).then_inc(weights, 16)
            act.wait_ge(spread, 1)
            act.activation(rstd[:, :], mv[:, :, 1], ACT.Sqrt, bias=c["eps"][:, :]).then_inc(rooted, 1)
            act.wait_ge(cleared, 2)
            act.dma_start(xs.rearrange("(p t) f -> p t f", p=P), over_middle(zeros[:, :], XT)).then_inc(zeroed, 16)

            for b in (0, 1):
                act.wait_ge(turned, b + 1)
                act.activation(xT[:, b, :, :], pT[b][:, :, :], ACT.Copy).then_inc(kept, 1)
            with act.Fori(1, NT // 2) as it:
                for i in range(2):
                    act.wait_ge(turned, it * 2 + i + 1)
                    act.wait_ge(multiplied, it * 2 + i - 1)
                    act.activation(xT[:, i, :, :], pT[i][:, :, :], ACT.Copy).then_inc(kept, 1)
            act.wait_ge(turned, NT)
            act.wait_ge(multiplied, NT - 2)
            act.activation(xT[:, 0, :, :], pT[0][:, :, :], ACT.Copy).then_inc(kept, 1)
            act.wait_ge(zeroed, 16)

        @block.vector
        def _(dve):
            st = Steps(dve, vec)
            dve.wait_ge(weights, 80)
            for i in range(2):
                for k in range(KT):
                    st.then(dve.tensor_tensor_reduce(out=junk[:, :], in0=wx[:, k, 0:F], in1=av[:, i, :], scale=1.0, scalar=0.0,
                                                     op0=ALU.mult, op1=ALU.add, accum_out=wx[:, k, COUNT + i:COUNT + i + 1]))
                st.then(dve.tensor_tensor_reduce(out=junk[:, :], in0=bx[:, 0:F], in1=av[:, i, :], scale=1.0, scalar=0.0,
                                                 op0=ALU.mult, op1=ALU.add, accum_out=bx[:, COUNT + i:COUNT + i + 1]))
            st.then(dve.tensor_tensor(bx[:, COUNT:COUNT + 1], bx[:, COUNT:COUNT + 1], ab[:, :], ALU.add))
            dve.wait_ge(loaded, 32)

            def spread_of(b):
                st.then(dve.bn_stats(stats[:, bass.ds(b, 1), :].rearrange("p a f -> p (a f)"), xa[:, bass.ds(b, 1), :].rearrange("p a f -> p (a f)")))
            repeat(dve, st, NT, 1, spread_of)
            st.then(dve.tensor_tensor(mv[:, :, 0], stats[:, :, 1], stats[:, :, 4], ALU.add))
            st.then(dve.tensor_tensor(rstd[:, :], stats[:, :, 1], stats[:, :, 4], ALU.subtract))
            st.then(dve.tensor_tensor(mv[:, :, 1], stats[:, :, 2], stats[:, :, 5], ALU.add))
            st.then(dve.tensor_scalar(mv[:, :, 0], mv[:, :, 0], 0.5, None, ALU.mult))
            st.then(dve.tensor_tensor(rstd[:, :], rstd[:, :], rstd[:, :], ALU.mult))
            st.then(dve.tensor_scalar(rstd[:, :], rstd[:, :], 0.25, None, ALU.mult))
            st.then(dve.scalar_tensor_tensor(mv[:, :, 1], mv[:, :, 1], 1.0 / F, rstd[:, :], ALU.mult, ALU.add))
            dve.sem_inc(spread, 1)
            dve.wait_ge(rooted, 1)
            st.then(dve.reciprocal(rstd[:, :], rstd[:, :]))

            def norm(b, i, first):
                if not first:
                    dve.wait_ge(turned, b - 1)
                dve.tensor_scalar(xn[:, i, :], xa[:, bass.ds(b, 1), :].rearrange("p a f -> p (a f)"), mv[:, bass.ds(b, 1), 0], rstd[:, bass.ds(b, 1)],
                                  ALU.subtract, ALU.mult).then_inc(ready, 1)

            def add_bias(b, i):
                dve.wait_ge(multiplied, b + 1)
                dve.tensor_tensor(wh[:, bass.ds(b, 1), :].rearrange("p a f -> p (a f)"), pW[i][:, :], bx[:, :], ALU.add).then_inc(added, 1)
            norm(0, 0, True)
            norm(1, 1, True)
            with dve.Fori(0, NT // 2 - 1) as it:
                for i in range(2):
                    norm(it * 2 + i + 2, i, False)
                    add_bias(it * 2 + i, i)
            norm(NT - 1, 0, False)
            add_bias(NT - 3, 0)
            add_bias(NT - 2, 1)
            add_bias(NT - 1, 0)
            dve.wait_ge(added, NT)
            dve.tensor_reduce(low[:, :], wh[:, :, SCORE], X, ALU.min).then_inc(low_ready, 1)
            dve.wait_ge(low_turned, 1)
            dve.tensor_reduce(lowT[:, :], pL[0:1, 0:P], X, ALU.min).then_inc(low_one, 1)
            dve.wait_ge(low_all, 1)
            st.then(dve.tensor_scalar(lift[:, :], pL[:, P:P + 1], -1.0, 1.0, ALU.mult, ALU.add))
            st.then(dve.tensor_scalar(row_score[:, :], wh[:, :, COUNT], lift[:, :], None, ALU.subtract))
            st.then(dve.tensor_scalar(wh[:, :, SCORE], wh[:, :, SCORE], lift[:, :], None, ALU.add))
            st.then(dve.memset(wh[:, :, COUNT], 1.0))
            dve.sem_inc(shifted, 1)
            dve.wait_ge(rowT, 1)
            dve.tensor_copy(row_scoreT[:, :], pL[0:NT, 2 * P:3 * P])

        @block.tensor
        def _(pe):
            def turn(b, i, first):
                pe.wait_ge(ready, b + 1)
                if not first:
                    pe.wait_ge(kept, b - 1)
                for k in range(KT):
                    ins = pe.transpose(pT[i][:, k, :], xn[:, i, k * P:(k + 1) * P], c["ident"][:, :])
                ins.then_inc(turned, 1)

            def multiply(b, i, first):
                pe.wait_ge(kept, b + 1)
                if not first:
                    pe.wait_ge(added, b - 1)
                for k in range(KT):
                    ins = pe.matmul(pW[i][:, :], xT[:, i, k, :], wx[:, k, :], start=k == 0, stop=k == KT - 1)
                ins.then_inc(multiplied, 1)
            turn(0, 0, True)
            turn(1, 1, True)
            multiply(0, 0, True)
            turn(2, 0, False)
            multiply(1, 1, True)
            with pe.Fori(1, NT // 2) as it:
                for i in range(2):
                    turn(it * 2 + i + 1, (i + 1) % 2, False)
                    multiply(it * 2 + i, i, False)
            multiply(NT - 1, 0, False)
            pe.wait_ge(low_ready, 1)
            pe.transpose(pL[0:1, 0:P], low[:, :], c["ident"][:, :]).then_inc(low_turned, 1)
            pe.wait_ge(low_one, 1)
            pe.matmul(pL[:, P:P + 1], c["ones"][0:1, :], lowT[:, :], start=True, stop=True).then_inc(low_all, 1)
            pe.wait_ge(shifted, 1)
            pe.transpose(pL[0:NT, 2 * P:3 * P], row_score[:, :], c["ident"][:, :]).then_inc(rowT, 1)


class Route:

    def __init__(self, ctx, nc, c, tag, parts, nb, nt, tiles):
        self.nc, self.c, self.parts, self.nb, self.nt, self.tiles = nc, c, parts, nb, nt, tiles
        sb = lambda n, s, d=FP32: ctx.enter_context(nc.sbuf_tensor(f"{tag}_{n}", s, d))
        ps = lambda n, s: ctx.enter_context(nc.psum_tensor(f"{tag}_{n}", s, FP32))
        self.onehot = sb("onehot", [parts, nb, nt], FP16)
        self.rank = sb("rank", [parts, nb, nt], FP16)
        self.upto = sb("upto", [parts, nb])
        self.own = sb("own", [parts, nb])
        self.base = sb("base", [parts, nb])
        self.t32 = sb("t32", [P, nb], I32)
        self.need = sb("need", [P, nb])
        self.end = sb("end", [P, nb])
        self.begin = sb("begin", [P, nb])
        self.endc = sb("endc", [nb, 1])
        self.beginc = sb("beginc", [nb, 1])
        self.past = sb("past", [nb, tiles])
        self.member = sb("member", [nb, tiles])
        self.kind = sb("kind", [P, tiles])
        self.p_n = ps("p_n", [P, 512])
        self.p_kind = ps("p_kind", [P, tiles])
        self.to_t = ctx.enter_context(nc.semaphore(f"{tag}_to_tensor"))
        self.to_v = ctx.enter_context(nc.semaphore(f"{tag}_to_vector"))

    def vector(self, dve, st):
        nb, nt, parts = self.nb, self.nt, self.parts
        st.then(dve.tensor_tensor_scan(flat(self.rank[:, :, :]), flat(self.onehot[:, :, :]), flat(self.onehot[:, :, :]), 0.0, ALU.add, ALU.max))
        st.then(dve.tensor_copy(self.upto[:, :], self.rank[:, :, nt - 1]))
        st.then(dve.tensor_copy(self.own[:, :], self.upto[:, :]))
        st.then(dve.tensor_tensor(self.own[:, 1:nb], self.upto[:, 1:nb], self.upto[:, 0:nb - 1], ALU.subtract))
        dve.sem_inc(self.to_t, 1)
        dve.wait_ge(self.to_v, 1)
        st.then(dve.tensor_scalar(self.t32[:, :], self.p_n[:, 0:nb], float(P - 1), None, ALU.add))
        st.then(dve.tensor_scalar(self.t32[:, :], self.t32[:, :], P.bit_length() - 1, None, ALU.logical_shift_right))
        st.then(dve.tensor_copy(self.need[:, :], self.t32[:, :]))
        st.then(dve.tensor_tensor_scan(self.end[:, :], self.need[:, :], self.need[:, :], 0.0, ALU.add, ALU.max))
        st.then(dve.tensor_tensor(self.begin[:, :], self.end[:, :], self.need[:, :], ALU.subtract))
        st.then(dve.tensor_tensor(self.base[:, :], self.own[:, :], self.upto[:, :], ALU.subtract))
        st.then(dve.scalar_tensor_tensor(self.base[:, :], self.base[:, :], -1.0, self.p_n[0:parts, P:P + nb], ALU.add, ALU.add))
        st.then(dve.scalar_tensor_tensor(self.base[:, :], self.begin[0:parts, :], float(P), self.base[:, :], ALU.mult, ALU.add))
        dve.sem_inc(self.to_t, 1)
        dve.wait_ge(self.to_v, 2)
        st.then(dve.tensor_copy(self.endc[:, :], self.p_n[0:nb, 2 * P:2 * P + 1]))
        st.then(dve.tensor_copy(self.beginc[:, :], self.p_n[0:nb, 3 * P:3 * P + 1]))
        st.then(dve.tensor_scalar(self.past[:, :], self.c["iota"][0:nb, 0:self.tiles], self.endc[:, :], None, ALU.is_ge))
        st.then(dve.scalar_tensor_tensor(self.member[:, :], self.c["iota"][0:nb, 0:self.tiles], self.beginc[:, :], self.past[:, :], ALU.is_ge, ALU.subtract))
        dve.sem_inc(self.to_t, 1)
        dve.wait_ge(self.to_v, 3)
        st.then(dve.tensor_copy(self.kind[:, :], self.p_kind[:, :]))

    def tensor(self, pe):
        nb, parts = self.nb, self.parts
        pe.wait_ge(self.to_t, 1)
        pe.matmul(self.p_n[:, 0:nb], self.c["ones"][0:parts, :], self.own[:, :], start=True, stop=True)
        pe.matmul(self.p_n[0:parts, P:P + nb], self.c["before"][0:parts, 0:parts], self.own[:, :], start=True, stop=True).then_inc(self.to_v, 1)
        pe.wait_ge(self.to_t, 2)
        pe.transpose(self.p_n[0:nb, 2 * P:3 * P], self.end[:, :], self.c["ident"][:, :])
        pe.transpose(self.p_n[0:nb, 3 * P:4 * P], self.begin[:, :], self.c["ident"][:, :]).then_inc(self.to_v, 1)
        pe.wait_ge(self.to_t, 3)
        pe.matmul(self.p_kind[:, :], self.c["ones"][0:nb, :], self.past[:, :], start=True, stop=True).then_inc(self.to_v, 1)


def route_edges(nc, c, s, q, src, dst, row_scoreT):
    ctx = ExitStack()
    with ctx:
        sb = lambda n, s, d=FP32: ctx.enter_context(nc.sbuf_tensor(f"r{q}_{n}", s, d))
        ps = lambda n, s, d=FP32: ctx.enter_context(nc.psum_tensor(f"r{q}_{n}", s, d))
        sem = lambda n: ctx.enter_context(nc.semaphore(f"r{q}_{n}"))
        row32, col32 = sb("row32", [EP, ET], I32), sb("col32", [EP, ET], I32)
        low32, tmp32 = sb("low32", [EP, ET], I32), sb("tmp32", [EP, ET], I32)
        tile16 = sb("tile16", [EP, ET], FP16)
        high, low = sb("high", [EP, ET]), sb("low", [EP, ET])
        pos = sb("pos", [EP, ET])
        slot, lane = sb("slot", [EP, ET]), sb("lane", [EP, ET])
        R = Route(ctx, nc, c, f"r{q}_e", EP, NT, ET, SLOTS)
        B = 4
        lane_high, lane_low = sb("lane_high", [EP, B, P], FP16), sb("lane_low", [EP, B, P], FP16)
        in_slot = sb("in_slot", [EP, B, SLOTS], FP16)
        none = sb("none", [EP, P], FP16)
        slot_i32, slot_f = sb("slot_i32", [P, SLOTS], I32), sb("slot_f", [P, SLOTS])
        mxT, lastT = sb("mxT", [P, 4, P]), sb("lastT", [P, 4, NT])
        floorT = sb("floorT", [NT, P])
        p_high, p_low = ps("p_high", [P, SLOTS]), ps("p_low", [P, SLOTS])
        p_score, p_floor = ps("p_score", [P, SLOTS]), ps("p_floor", [P, SLOTS])
        p_a, p_b = ps("p_a", [P, 512]), ps("p_b", [P, 512])
        loaded, vec, begun, made, placed = sem("loaded"), sem("vec"), sem("begun"), sem("made"), sem("placed")
        scores, floors, floors_in, cuts, cuts_in, zeroed, summed, put = (sem(n) for n in (
            "scores", "floors", "floors_in", "cuts", "cuts_in", "zeroed", "summed", "put"))
        CW = SLOTS // 4
        block = ctx.enter_context(nc.Block())

        @block.sync
        def _(sp):
            half = slice(q * EP * ET, (q + 1) * EP * ET)
            sp.dma_start(row32[:, :], src[half].rearrange("(p t) -> p t", p=EP)).then_inc(loaded, 16)
            sp.dma_start(col32[:, :], dst[half].rearrange("(p t) -> p t", p=EP)).then_inc(loaded, 16)
            sp.wait_ge(loaded, 32)

        @block.vector
        def _(dve):
            st = Steps(dve, vec)
            dve.memset(none[:, :], 0.0).then_inc(zeroed, 1)
            if q:
                dve.wait_ge(cuts, 1)
                st.then(dve.tensor_copy(mxT[0:CW, :, :], p_a[0:CW, :].rearrange("p (a b) -> p a b", a=4)))
                st.then(dve.tensor_copy(lastT[0:CW, :, :], p_b[0:CW, 0:4 * NT].rearrange("p (a b) -> p a b", a=4)))
                dve.sem_inc(cuts_in, 1)
                dve.wait_ge(summed, 1)
                st.then(dve.tensor_scalar(floorT[:, :], p_floor[0:NT, 0:P], s["absent"][:, :], None, ALU.add))
                dve.sem_inc(floors_in, 1)
            dve.wait_ge(loaded, 32)
            st.done(dve.tensor_scalar(low32[:, :], row32[:, :], P - 1, None, ALU.bitwise_and))
            st.done(dve.tensor_scalar(tmp32[:, :], col32[:, :], 7, 7, ALU.bitwise_and, ALU.logical_shift_left))
            st.then(dve.tensor_scalar(row32[:, :], row32[:, :], 7, None, ALU.logical_shift_right))
            st.done(dve.tensor_copy(tile16[:, :], row32[:, :]))
            st.done(dve.scalar_tensor_tensor(low[:, :], tmp32[:, :], 1.0, low32[:, :], ALU.add, ALU.add))
            st.then(dve.tensor_scalar(col32[:, :], col32[:, :], 3, None, ALU.logical_shift_right))
            st.then(dve.tensor_copy(high[:, :], col32[:, :]))
            st.then(dve.tensor_tensor(R.onehot[:, :, :], over_middle(tile16[:, :], NT), over_last(c["iota16"][0:EP, 0:NT], ET), ALU.is_equal))
            R.vector(dve, st)
            place = R.onehot[:, :, :].bitcast(U16)

            def pick(b):
                st.done(dve.scalar_tensor_tensor(place[:, b, :], R.rank[:, b, :], R.base[:, b:b + 1], R.onehot[:, b, :], ALU.add, ALU.mult))
            for b in range(NT):
                pick(b)
            st.settle()
            st.then(dve.tensor_reduce(pos[:, :], place.rearrange("p b t -> p t b"), X, ALU.add))
            st.then(dve.tensor_copy(tmp32[:, :], pos[:, :]))
            st.then(dve.tensor_scalar(low32[:, :], tmp32[:, :], P - 1, None, ALU.bitwise_and))
            st.then(dve.tensor_scalar(tmp32[:, :], tmp32[:, :], 7, None, ALU.logical_shift_right))
            st.done(dve.tensor_copy(lane[:, :], low32[:, :]))
            st.then(dve.tensor_copy(slot[:, :], tmp32[:, :]))

            def masks(t, j):
                dve.tensor_scalar(lane_high[:, j, :], c["iota16"][0:EP, 0:P], lane[:, bass.ds(t, 1)], high[:, bass.ds(t, 1)], ALU.is_equal, ALU.mult)
                dve.tensor_scalar(lane_low[:, j, :], c["iota16"][0:EP, 0:P], lane[:, bass.ds(t, 1)], low[:, bass.ds(t, 1)], ALU.is_equal, ALU.mult)
                dve.tensor_scalar(in_slot[:, j, :], c["iota16"][0:EP, :], slot[:, bass.ds(t, 1)], None, ALU.is_equal).then_inc(made, 1)
            for j in range(B):
                masks(j, j)
            with dve.Fori(1, ET // B) as it:
                for j in range(B):
                    dve.wait_ge(placed, (it - 1) * B + j + 1)
                    masks(it * B + j, j)
            kind = R.kind
            st.done(dve.tensor_copy(s["tile32"][:, :], kind[:, :]))
            st.done(dve.memset(s["fresh"][:, 0:1], FAR))
            st.then(dve.tensor_tensor(s["fresh"][:, 1:SLOTS], kind[:, 1:SLOTS], kind[:, 0:SLOTS - 1], ALU.not_equal))
            st.then(dve.tensor_scalar(s["fresh"][:, 1:SLOTS], s["fresh"][:, 1:SLOTS], FAR, None, ALU.mult))
            dve.wait_ge(scores, 1)
            st.then(dve.tensor_copy(s["rscore"][:, :], p_score[:, :]))
            if q:
                dve.wait_ge(floors, 1)
                st.then(dve.tensor_copy(s["floor"][:, :], p_floor[:, :]))
            else:
                st.then(dve.memset(s["floor"][:, :], FAR))
            st.then(dve.memset(s["mx"][:, 0:1], 0.0))
            if q + 1 < HALVES:
                st.then(dve.tensor_scalar(R.beginc[:, :], R.endc[:, :], R.beginc[:, :], FAR, ALU.is_equal, ALU.mult))
                st.then(dve.tensor_copy(s["absent"][:, :], R.beginc[:, :]))
                st.then(dve.tensor_scalar(R.endc[:, :], R.endc[:, :], -1.0, None, ALU.add))
                st.then(dve.scalar_tensor_tensor(s["lastsel"][:, :], c["iota"][0:NT, :], R.endc[:, :], R.member[:, :], ALU.is_equal, ALU.mult))
            dve.wait_ge(put, 1)
            st.then(dve.tensor_scalar(s["cols"][:, :], p_low[:, :], -1.0, None, ALU.add))
            st.done(dve.tensor_scalar(slot_i32[:, :], s["cols"][:, :], P - 1, None, ALU.bitwise_and))
            st.then(dve.tensor_scalar(s["cols"][:, :], s["cols"][:, :], 7, None, ALU.arith_shift_right))
            st.done(dve.tensor_scalar(slot_f[:, :], s["cols"][:, :], 0.0, None, ALU.max))
            st.done(dve.tensor_scalar(s["rows"][:, :], p_low[:, :], 0.0, 1000.0, ALU.is_equal, ALU.mult))
            st.settle()
            st.done(dve.scalar_tensor_tensor(s["cols"][:, :], p_high[:, :], 8.0, slot_f[:, :], ALU.mult, ALU.add))
            st.then(dve.tensor_tensor(s["rows"][:, :], s["rows"][:, :], slot_i32[:, :], ALU.add))

        @block.tensor
        def _(pe):
            if q:
                for k in range(4):
                    pe.transpose(p_a[0:CW, k * P:(k + 1) * P], s["mx"][:, 1 + k * CW:1 + (k + 1) * CW], c["ident"][:, :])
                    ins = pe.transpose(p_b[0:CW, k * NT:(k + 1) * NT], s["lastsel"][:, k * CW:(k + 1) * CW], c["ident"][0:NT, 0:NT])
                ins.then_inc(cuts, 1)
                pe.wait_ge(cuts_in, 1)
                for k in range(4):
                    ins = pe.matmul(p_floor[0:NT, 0:P], lastT[0:CW, k, :], mxT[0:CW, k, :], start=k == 0, stop=k == 3)
                ins.then_inc(summed, 1)
            R.tensor(pe)
            pe.matmul(p_score[:, :], row_scoreT[:, :], R.member[:, :], start=True, stop=True).then_inc(scores, 1)
            if q:
                pe.wait_ge(floors_in, 1)
                pe.matmul(p_floor[:, :], floorT[:, :], R.member[:, :], start=True, stop=True).then_inc(floors, 1)
            pe.wait_ge(zeroed, 1)
            pe.wait_ge(made, 1)
            for p in (p_high, p_low):
                pe.matmul(p[:, :], none[:, :], in_slot[:, 0, :], start=True, stop=False)

            def place(t, j):
                pe.wait_ge(made, t + 1)
                pe.matmul(p_high[:, :], lane_high[:, j, :], in_slot[:, j, :], start=False, stop=False)
                pe.matmul(p_low[:, :], lane_low[:, j, :], in_slot[:, j, :], start=False, stop=False).then_inc(placed, 1)
            with pe.Fori(0, ET // B) as it:
                for j in range(B):
                    place(it * B + j, j)
            for p in (p_high, p_low):
                ins = pe.matmul(p[:, :], none[:, :], in_slot[:, B - 1, :], start=False, stop=True)
            ins.then_inc(put, 1)


def attention(nc, c, s, q, table, acc):
    ctx = ExitStack()
    with ctx:
        sb = lambda n, s, d=FP32: ctx.enter_context(nc.sbuf_tensor(f"a{q}_{n}", s, d))
        ps = lambda n, s, d=FP32: ctx.enter_context(nc.psum_tensor(f"a{q}_{n}", s, d))
        sem = lambda n: ctx.enter_context(nc.semaphore(f"a{q}_{n}"))
        index = [sb(f"index{i}", [P, G], I32) for i in range(2)]
        rows = sb("gathered", [P, 2 * G, TW])
        onehot = sb("onehot", [P, 2, G, P])
        raised = sb("raised", [P, 2, G, P])
        member = sb("member", [P, 2, G, P])
        weight = sb("weight", [P, 2, G, P])
        tile_mx, row_e = sb("tile_mx", [P, G]), sb("row_e", [P, G])
        drop = sb("drop", [P, 2, G])
        factor = sb("factor", [P, 2, G])
        row_info = sb("row_info", [P, 2, G, 2])
        e1, e2, e3 = sb("e1", [P, G]), sb("e2", [P, G]), sb("e3", [P, G])
        expo, w = sb("expo", [P, 2, G]), sb("w", [P, 2, G])
        p_turn = [ps(f"p_turn{i}", [P, G, P]) for i in range(2)]
        p_slot = ps("p_slot", [P, G, 2])
        p_sum = [ps(f"p_sum{j}", [P, 512]) for j in range(G)]
        staged, issued = sem("staged"), sem("issued")
        gathered = [sem(f"gathered{j}") for j in range(2 * G)]
        masked, raised_s, turned, reduced, informed, dropped = (sem(n) for n in (
            "masked", "raised", "turned", "reduced", "informed", "dropped"))
        membered, spread, exponents, exps, weighed, factored, summed, added, vec = (sem(n) for n in (
            "membered", "spread", "exponents", "exps", "weighed", "factored", "summed", "added", "vec"))
        block = ctx.enter_context(nc.Block())

        @block.gpsimd
        def _(pool):
            def gather(it, i, first):
                g = it * 2 + i
                if not first:
                    pool.wait_ge(summed, (g - 2) * G + G)
                    pool.nop()
                pool.tensor_copy(index[i][:, :], s["cols"][:, bass.ds(g * G, G)]).then_inc(staged, 1)
                pool.wait_ge(staged, g + 1)
                pool.sem_inc(issued, 1)
                for j in range(G):
                    pool.indirect_dma_start(rows[:, i * G + j, :], None, table, bass.IndirectOffsetOnAxis(ap=index[i][:, j:j + 1], axis=0)
                                            ).then_inc(gathered[i * G + j], 16)
            for i in range(2):
                gather(0, i, True)
            with pool.Fori(1, GROUPS // 2) as it:
                for i in range(2):
                    gather(it, i, False)

        @block.scalar
        def _(act):
            def raise_scores(it, i, reused):
                g = it * 2 + i
                for j in range(G):
                    act.wait_ge(gathered[i * G + j], it * 16 + 16)
                act.wait_ge(masked, g * G + G)
                if reused:
                    act.wait_ge(turned, g - 1)
                act.nop()
                for j in range(G):
                    ins = act.activation(raised[:, i, j, :], onehot[:, i, j, :], ACT.Copy, scale=rows[:, i * G + j, SCORE:SCORE + 1])
                ins.then_inc(raised_s, 1)

            def group(it, i, first, last):
                g = it * 2 + i
                act.wait_ge(reduced, g + 1)
                act.activation(member[:, i, :, :], p_turn[i][:, :, :], ACT.Sign).then_inc(membered, 1)
                act.wait_ge(dropped, g + 1)
                act.activation(factor[:, i, :], drop[:, i, :], ACT.Exp).then_inc(factored, 1)
                if not last:
                    raise_scores(it if i == 0 else it + 1, 1 - i, not first)
                act.wait_ge(exponents, g + 1)
                act.activation(w[:, i, :], expo[:, i, :], ACT.Exp).then_inc(exps, 1)
                act.wait_ge(exps, g + 1)
                act.nop()
                for j in range(G):
                    ins = act.activation(weight[:, i, j, :], onehot[:, i, j, :], ACT.Copy, scale=w[:, i, j:j + 1])
                ins.then_inc(weighed, 1)
            raise_scores(0, 0, False)
            group(0, 0, True, False)
            group(0, 1, False, False)
            with act.Fori(1, GROUPS // 2 - 1) as it:
                for i in range(2):
                    group(it, i, False, False)
            group(GROUPS // 2 - 1, 0, False, False)
            group(GROUPS // 2 - 1, 1, False, True)

        @block.tensor
        def _(pe):
            def turn(g, i):
                pe.wait_ge(raised_s, g + 1)
                for j in range(G):
                    ins = pe.transpose(p_turn[i][:, j, :], raised[:, i, j, :], c["ident"][:, :])
                ins.then_inc(turned, 1)

            def group(it, i, last):
                g = it * 2 + i
                pe.wait_ge(informed, g + 1)
                pe.wait_ge(membered, g + 1)
                for j in range(G):
                    ins = pe.matmul(p_slot[:, j, :], member[:, i, j, :], row_info[:, i, j, :], start=True, stop=True)
                ins.then_inc(spread, 1)
                if not last:
                    turn(g + 1, 1 - i)
                pe.wait_ge(weighed, g + 1)
                for j in range(G):
                    pe.matmul(p_sum[j][:, 0:AW], weight[:, i, j, :], rows[:, i * G + j, 0:AW], start=True, stop=True).then_inc(summed, 1)
            turn(0, 0)
            with pe.Fori(0, GROUPS // 2 - 1) as it:
                for i in range(2):
                    group(it, i, False)
            group(GROUPS // 2 - 1, 0, False)
            group(GROUPS // 2 - 1, 1, True)

        @block.vector
        def _(dve):
            st = Steps(dve, vec)

            def masks(g, i):
                for j in range(G):
                    dve.tensor_scalar(onehot[:, i, j, :], c["iota16"][:, 0:P], s["rows"][:, bass.ds(g * G + j, 1)], None,
                                      ALU.is_equal).then_inc(masked, 1)

            def add(g, i):
                for j in range(G):
                    tile = dve.value_load(s["tile32"][0:1, bass.ds(g * G + j, 1)], min_val=0, max_val=NT)
                    dve.wait_ge(summed, g * G + j + 1)
                    if j == 0:
                        dve.wait_ge(factored, g + 1)
                    if not (isinstance(g, int) and g == 0 and j == 0):
                        dve.wait_ge(added, g * G + j)
                    here = acc[:, bass.ds(tile, 1), :].rearrange("p a f -> p (a f)")
                    dve.scalar_tensor_tensor(here, here, factor[:, i, j:j + 1], p_sum[j][:, 0:AW], ALU.mult, ALU.add).then_inc(added, 1)

            def group(it, i, first, last):
                g = it * 2 + i
                now = bass.ds(g * G, G)
                mx_now, mx_before = s["mx"][:, bass.ds(g * G + 1, G)], s["mx"][:, bass.ds(g * G, G)]
                dve.wait_ge(turned, g + 1)
                st.then(dve.tensor_reduce(tile_mx[:, :], p_turn[i][:, :, :], X, ALU.max))
                dve.sem_inc(reduced, 1)
                st.then(dve.tensor_tensor(row_e[:, :], tile_mx[:, :], s["rscore"][:, now], ALU.add))
                st.then(dve.scalar_tensor_tensor(row_e[:, :], row_e[:, :], SLOPE, row_e[:, :], ALU.mult, ALU.max))
                st.then(dve.tensor_tensor(row_e[:, :], row_e[:, :], s["floor"][:, now], ALU.max))
                st.then(dve.tensor_tensor_scan(mx_now, s["fresh"][:, now], row_e[:, :], s["mx"][:, bass.ds(g * G, 1)], ALU.add, ALU.max))
                if not first:
                    dve.wait_ge(spread, g)
                dve.tensor_scalar(row_info[:, i, :, 1], mx_now, -1.0, None, ALU.mult)
                dve.tensor_copy(row_info[:, i, :, 0], s["rscore"][:, now]).then_inc(informed, 1)
                st.then(dve.tensor_tensor(drop[:, i, :], mx_before, s["fresh"][:, now], ALU.add))
                st.then(dve.tensor_tensor(drop[:, i, :], drop[:, i, :], s["floor"][:, now], ALU.max))
                st.then(dve.tensor_tensor(drop[:, i, :], drop[:, i, :], mx_now, ALU.subtract))
                dve.sem_inc(dropped, 1)
                if not last:
                    if not first:
                        dve.wait_ge(weighed, g)
                    masks(g + 1, 1 - i)
                if not first:
                    add(g - 1, 1 - i)
                dve.wait_ge(spread, g + 1)
                st.then(dve.tensor_tensor(e1[:, :], rows[:, i * G:(i + 1) * G, SCORE], p_slot[:, :, 0], ALU.add))
                st.then(dve.scalar_tensor_tensor(e2[:, :], e1[:, :], SLOPE, e1[:, :], ALU.mult, ALU.max))
                st.then(dve.tensor_tensor(e3[:, :], e2[:, :], p_slot[:, :, 1], ALU.add))
                dve.tensor_scalar(expo[:, i, :], e3[:, :], 0.0, None, ALU.min).then_inc(exponents, 1)
            masks(0, 0)
            group(0, 0, True, False)
            per = st.n
            group(0, 1, False, False)
            assert st.n == 2 * per

            def pair(it):
                group(it + 1, 0, False, False)
                group(it + 1, 1, False, False)
            repeat(dve, st, GROUPS // 2 - 2, 2 * per, pair)
            group(GROUPS // 2 - 1, 0, False, False)
            group(GROUPS // 2 - 1, 1, False, True)
            add(GROUPS - 1, 1)
            dve.wait_ge(added, GROUPS * G)


def gate(nc, c, g, x, acc, Wg, bg, xs, x1):
    ctx = ExitStack()
    with ctx:
        sb = lambda n, s, d=FP32: ctx.enter_context(nc.sbuf_tensor(f"g_{n}", s, d))
        ps = lambda n, s, d=FP32: ctx.enter_context(nc.psum_tensor(f"g_{n}", s, d))
        sem = lambda n: ctx.enter_context(nc.semaphore(f"g_{n}"))
        xa = sb("x", [P, NT, F])
        xn = sb("xn", [P, 2, F])
        inv = sb("inv", [P, NT])
        stats, mean, var, rstd = sb("stats", [P, NT, 6]), sb("mean", [P, NT]), sb("var", [P, NT]), sb("rstd", [P, NT])
        xT = sb("xT", [P, 2, KT, P])
        wg, bgb = sb("wg", [P, KT, NE]), sb("bgb", [P, NE])
        logits = sb("logits", [P, NT, NE])
        top = [sb(f"top{k}", [P, NT]) for k in range(TOPK)]
        which = sb("which", [P, NT])
        same = sb("same", [P, NT, NE])
        hot = [sb(f"hot{k}", [P, NT, NE]) for k in range(TOPK)]
        ratio = sb("ratio", [P, NT])
        place = sb("place", [P, NT, NE])
        iotaE = sb("iotaE", [P, NE])
        posf = sb("posf", [P, NT])
        R = Route(ctx, nc, c, "g_r", P, NE, NT, XT)
        pT = [ps(f"pT{i}", [P, KT, P]) for i in range(2)]
        pG = [ps(f"pG{i}", [P, 512]) for i in range(2)]
        loaded, weights, cleared, vec, spread, rooted = (sem(n) for n in ("loaded", "weights", "cleared", "vec", "spread", "rooted"))
        ready, turned, kept, multiplied, added, differ, expd, placed, scattered = (sem(n) for n in (
            "ready", "turned", "kept", "multiplied", "added", "differ", "expd", "placed", "scattered"))
        resident, saved, copied = sem("resident"), sem("saved"), sem("copied")
        block = ctx.enter_context(nc.Block())

        @block.sync
        def _(sp):
            sp.dma_start(xa[:, 0:NT - 1, :], x[0:(NT - 1) * P, :].rearrange("(b p) f -> p b f", p=P)).then_inc(loaded, 16)
            sp.wait_ge(cleared, 1)
            sp.dma_start(xa[0:LAST, NT - 1, :], x[(NT - 1) * P:N, :]).then_inc(loaded, 16)
            sp.dma_start(wg[:, :, :], Wg.rearrange("(k p) f -> p k f", p=P)).then_inc(weights, 16)
            sp.dma_start(bgb[:, :], bg.rearrange("(a f) -> a f", a=1).partition_broadcast(P).rearrange("p a f -> p (a f)")).then_inc(weights, 16)
            sp.wait_ge(resident, 1)
            sp.dma_start(x1.rearrange("(b p) f -> p b f", p=P), acc[:, 0:NT, 0:F]).then_inc(saved, 16)
            sp.wait_ge(weights, 32)
            sp.wait_ge(saved, 16)

        @block.gpsimd
        def _(pool):
            pool.memset(xa[:, NT - 1, :], 0.0).then_inc(cleared, 1)

            def keep(b, i):
                pool.wait_ge(ready, b + 1)
                pool.nop()
                pool.tensor_copy(xa[:, bass.ds(b, 1), :].rearrange("p a f -> p (a f)"), xn[:, i, :]).then_inc(copied, 1)
            with pool.Fori(0, NT // 2) as it:
                for i in range(2):
                    keep(it * 2 + i, i)
            keep(NT - 1, 0)
            pool.wait_ge(copied, NT)
            pool.wait_ge(placed, 1)
            for b in range(NT):
                n = P if b < NT - 1 else LAST
                for k in range(TOPK):
                    pool.indirect_dma_start(xs, bass.IndirectOffsetOnAxis(ap=g["pos"][0:n, k, b:b + 1], axis=0),
                                            xa[0:n, b, :], None).then_inc(scattered, 16)
            pool.wait_ge(scattered, 16 * TOPK * NT)

        @block.scalar
        def _(act):
            act.wait_ge(spread, 1)
            act.activation(rstd[:, :], var[:, :], ACT.Sqrt, bias=c["eps"][:, :]).then_inc(rooted, 1)
            for b in (0, 1):
                act.wait_ge(turned, b + 1)
                act.activation(xT[:, b, :, :], pT[b][:, :, :], ACT.Copy).then_inc(kept, 1)
            with act.Fori(1, NT // 2) as it:
                for i in range(2):
                    act.wait_ge(turned, it * 2 + i + 1)
                    act.wait_ge(multiplied, it * 2 + i - 1)
                    act.activation(xT[:, i, :, :], pT[i][:, :, :], ACT.Copy).then_inc(kept, 1)
            act.wait_ge(turned, NT)
            act.wait_ge(multiplied, NT - 2)
            act.activation(xT[:, 0, :, :], pT[0][:, :, :], ACT.Copy).then_inc(kept, 1)
            act.wait_ge(differ, 1)
            act.activation(ratio[:, :], ratio[:, :], ACT.Exp).then_inc(expd, 1)

        @block.tensor
        def _(pe):
            def turn(b, i, first):
                pe.wait_ge(ready, b + 1)
                if not first:
                    pe.wait_ge(kept, b - 1)
                for k in range(KT):
                    ins = pe.transpose(pT[i][:, k, :], xn[:, i, k * P:(k + 1) * P], c["ident"][:, :])
                ins.then_inc(turned, 1)

            def multiply(b, i, first):
                pe.wait_ge(kept, b + 1)
                if not first:
                    pe.wait_ge(added, b - 1)
                for k in range(KT):
                    ins = pe.matmul(pG[i][:, 0:NE], xT[:, i, k, :], wg[:, k, :], start=k == 0, stop=k == KT - 1)
                ins.then_inc(multiplied, 1)
            pe.wait_ge(weights, 32)
            turn(0, 0, True)
            turn(1, 1, True)
            multiply(0, 0, True)
            turn(2, 0, False)
            multiply(1, 1, True)
            with pe.Fori(1, NT // 2) as it:
                for i in range(2):
                    turn(it * 2 + i + 1, (i + 1) % 2, False)
                    multiply(it * 2 + i, i, False)
            multiply(NT - 1, 0, False)
            R.tensor(pe)

        @block.vector
        def _(dve):
            st = Steps(dve, vec)
            dve.wait_ge(loaded, 32)
            st.then(dve.tensor_scalar(inv[:, :], acc[:, 0:NT, F], 1e-30, None, ALU.max))
            st.then(dve.reciprocal(inv[:, :], inv[:, :]))

            def residual(b):
                at = lambda a, n=F: a[:, bass.ds(b, 1), 0:n].rearrange("p a f -> p (a f)")
                st.then(dve.tensor_scalar(at(acc), at(acc), inv[:, bass.ds(b, 1)], 0.0, ALU.mult, ALU.max))
                st.then(dve.tensor_tensor(at(acc), at(acc), at(xa), ALU.add))
                st.done(dve.bn_stats(at(stats, 6), at(acc)))
            repeat(dve, st, NT, 3, residual)
            st.settle()
            dve.sem_inc(resident, 1)
            st.then(dve.tensor_tensor(mean[:, :], stats[:, :, 1], stats[:, :, 4], ALU.add))
            st.then(dve.tensor_tensor(rstd[:, :], stats[:, :, 1], stats[:, :, 4], ALU.subtract))
            st.then(dve.tensor_tensor(var[:, :], stats[:, :, 2], stats[:, :, 5], ALU.add))
            st.then(dve.tensor_scalar(mean[:, :], mean[:, :], 0.5, None, ALU.mult))
            st.then(dve.tensor_tensor(rstd[:, :], rstd[:, :], rstd[:, :], ALU.mult))
            st.then(dve.tensor_scalar(rstd[:, :], rstd[:, :], 0.25, None, ALU.mult))
            st.then(dve.scalar_tensor_tensor(var[:, :], var[:, :], 1.0 / F, rstd[:, :], ALU.mult, ALU.add))
            dve.sem_inc(spread, 1)
            dve.wait_ge(rooted, 1)
            st.then(dve.reciprocal(rstd[:, :], rstd[:, :]))

            dve.wait_ge(weights, 32)

            def norm(b, i, first):
                if not first:
                    dve.wait_ge(turned, b - 1)
                    dve.wait_ge(copied, b - 1)
                here = acc[:, bass.ds(b, 1), 0:F].rearrange("p a f -> p (a f)")
                dve.tensor_scalar(xn[:, i, :], here, mean[:, bass.ds(b, 1)], rstd[:, bass.ds(b, 1)],
                                  ALU.subtract, ALU.mult).then_inc(ready, 1)

            def add_bias(b, i):
                dve.wait_ge(multiplied, b + 1)
                dve.tensor_tensor(logits[:, bass.ds(b, 1), :].rearrange("p a f -> p (a f)"), pG[i][:, 0:NE], bgb[:, :], ALU.add).then_inc(added, 1)
            norm(0, 0, True)
            norm(1, 1, True)
            with dve.Fori(0, NT // 2 - 1) as it:
                for i in range(2):
                    norm(it * 2 + i + 2, i, False)
                    add_bias(it * 2 + i, i)
            norm(NT - 1, 0, False)
            add_bias(NT - 3, 0)
            add_bias(NT - 2, 1)
            add_bias(NT - 1, 0)
            dve.wait_ge(added, NT)
            st.then(dve.tensor_copy(iotaE[:, :], c["iota"][:, 0:NE]))
            experts_of = over_middle(iotaE[:, :], NT)
            for k in range(TOPK):
                st.then(dve.tensor_reduce(top[k][:, :], logits[:, :, :], X, ALU.max))
                st.then(dve.tensor_tensor(same[:, :, :], logits[:, :, :], over_last(top[k][:, :], NE), ALU.is_equal))
                st.then(dve.tensor_scalar(same[:, :, :], same[:, :, :], -float(NE), float(NE), ALU.mult, ALU.add))
                st.then(dve.tensor_tensor(same[:, :, :], same[:, :, :], experts_of, ALU.add))
                st.then(dve.tensor_reduce(which[:, :], same[:, :, :], X, ALU.min))
                st.then(dve.tensor_tensor(hot[k][:, :, :], over_last(which[:, :], NE), experts_of, ALU.is_equal))
                if k == 0:
                    st.then(dve.scalar_tensor_tensor(flat(logits[:, :, :]), flat(hot[k][:, :, :]), FAR, flat(logits[:, :, :]), ALU.mult, ALU.add))
                st.then(dve.tensor_scalar(hot[k][:, NT - 1, :], hot[k][:, NT - 1, :], c["valid"][:, :], None, ALU.mult))
            st.then(dve.tensor_tensor(ratio[:, :], top[1][:, :], top[0][:, :], ALU.subtract))
            dve.sem_inc(differ, 1)
            st.then(dve.tensor_tensor(R.onehot[:, :, :], hot[0][:, :, :].rearrange("p b e -> p e b"), hot[1][:, :, :].rearrange("p b e -> p e b"), ALU.add))
            R.vector(dve, st)
            for k in range(TOPK):
                ep = place[:, :, :].rearrange("p b e -> p e b")
                hotk = hot[k][:, :, :].rearrange("p b e -> p e b")
                st.then(dve.tensor_tensor(ep, R.rank[:, :, :], over_last(R.base[:, :], NT), ALU.add))
                st.then(dve.tensor_tensor(ep, ep, hotk, ALU.mult))
                st.then(dve.tensor_reduce(posf[:, :], place[:, :, :], X, ALU.add))
                st.then(dve.tensor_copy(g["pos"][:, k, :], posf[:, :]))
            dve.sem_inc(placed, 1)
            st.then(dve.tensor_scalar(g["expert32"][:, :], R.kind[:, :], float(NE - 1), None, ALU.min))
            dve.wait_ge(expd, 1)
            st.then(dve.tensor_scalar(posf[:, :], ratio[:, :], 1.0, None, ALU.add))
            st.then(dve.reciprocal(g["weight"][:, 0, :], posf[:, :]))
            st.then(dve.tensor_tensor(g["weight"][:, 1, :], g["weight"][:, 0, :], ratio[:, :], ALU.mult))


def experts(nc, c, g, xs, ys, W1, b1, W2, b2):
    ctx = ExitStack()
    with ctx:
        sb = lambda n, s, d=FP32: ctx.enter_context(nc.sbuf_tensor(f"e_{n}", s, d))
        ps = lambda n, s, d=FP32: ctx.enter_context(nc.psum_tensor(f"e_{n}", s, d))
        sem = lambda n: ctx.enter_context(nc.semaphore(f"e_{n}"))
        w1h, w1l = sb("w1h", [P, NE * KT, H], BF16), sb("w1l", [P, NE * KT, H], BF16)
        w2h, w2l = sb("w2h", [P, NE * HC, F], BF16), sb("w2l", [P, NE * HC, F], BF16)
        WB = 3
        CH = 2048
        stage = sb("stage", [P, WB, CH])
        b1c = sb("b1c", [P, NE, HC])
        b2b = sb("b2b", [P, NE, F])
        b1r = sb("b1r", [NE * HC, P])
        xt = sb("xt", [P, 4, F])
        xh, xl = sb("xh", [P, 2, KT, P], BF16), sb("xl", [P, 2, KT, P], BF16)
        hf = sb("hf", [P, 2, HC, P])
        hh, hl = sb("hh", [P, 2, HC, P], BF16), sb("hl", [P, 2, HC, P], BF16)
        yt = sb("yt", [P, 2, F])
        pT = [ps(f"pT{i}", [P, KT, P]) for i in range(2)]
        pH = [ps(f"pH{i}", [P, HC, P]) for i in range(2)]
        pY = [ps(f"pY{i}", [P, F]) for i in range(2)]
        wload = [sem(f"wload{i}") for i in range(WB)]
        high, rest, biases, b1turned, b1kept = (sem(n) for n in ("high", "rest", "biases", "b1turned", "b1kept"))
        xload = [sem(f"xload{i}") for i in range(4)]
        turned, xhigh, xrest, hidden, gelued, hhigh, hrest, out_s, biased = (sem(n) for n in (
            "turned", "xhigh", "xrest", "hidden", "gelued", "hhigh", "hrest", "out", "biased"))
        stored = [sem(f"stored{i}") for i in range(2)]
        per = H * KT // CH
        chunks = 2 * NE * per
        w1v = W1.rearrange("e (k p) h -> e p k h", p=P)
        w2v = W2.rearrange("e (k p) f -> e p k f", p=P)
        block = ctx.enter_context(nc.Block())

        def chunk(n):
            e = n // 2
            if n % 2 == 0:
                return w1v[e], w1h[:, e * KT:(e + 1) * KT, :], w1l[:, e * KT:(e + 1) * KT, :], H
            return w2v[e], w2h[:, e * HC:(e + 1) * HC, :], w2l[:, e * HC:(e + 1) * HC, :], F
        assert per == 1 and HC * F == CH

        @block.sync
        def _(sp):
            for n in range(chunks):
                if n >= WB:
                    sp.wait_ge(rest, n - WB + 1)
                d, _, _, width = chunk(n)
                sp.dma_start(stage[:, n % WB, :].rearrange("p (k f) -> p k f", f=width), d).then_inc(wload[n % WB], 16)
            for j in range(4):
                sp.dma_start(xt[:, j, :], xs[j * P:(j + 1) * P, :]).then_inc(xload[j], 16)

            def load(it, j):
                t = it * 4 + j
                sp.wait_ge(turned, t - 3)
                sp.nop()
                sp.dma_start(xt[:, j, :], xs[bass.ds(t * P, P), :]).then_inc(xload[j], 16)
            with sp.Fori(1, XT // 4) as it:
                for j in range(4):
                    load(it, j)
            for j in range(XT % 4):
                load(XT // 4, j)

        @block.gpsimd
        def _(pool):
            def store(it, i):
                t = it * 2 + i
                pool.wait_ge(biased, t + 1)
                pool.nop()
                pool.dma_start(ys[bass.ds(t * P, P), :], yt[:, i, :]).then_inc(stored[i], 16)
            with pool.Fori(0, XT // 2) as it:
                for i in range(2):
                    store(it, i)
            for i in range(2):
                pool.wait_ge(stored[i], 16 * (XT // 2))

        @block.scalar
        def _(act):
            act.dma_start(b1r[:, :], b1.rearrange("e (k p) -> (e k) p", p=P)).then_inc(biases, 16)
            act.dma_start(b2b[:, :, :], b2.rearrange("(a e) f -> a e f", a=1).partition_broadcast(P).rearrange("p a e f -> p (a e) f")).then_inc(biases, 16)
            for n in range(chunks):
                act.wait_ge(wload[n % WB], 16 * (n // WB + 1))
                _, h, _, _ = chunk(n)
                act.activation(flat(h), stage[:, n % WB, :], ACT.Copy).then_inc(high, 1)
            act.wait_ge(b1turned, 1)
            act.activation(flat(b1c[:, :, :]), pY[0][:, 0:NE * HC], ACT.Copy).then_inc(b1kept, 1)

            def x_high(t, i, first):
                act.wait_ge(turned, t + 1)
                if not first:
                    act.wait_ge(hidden, t - 1)
                act.activation(xh[:, i, :, :], pT[i][:, :, :], ACT.Copy).then_inc(xhigh, 1)

            def gelu(t, i, first):
                e = act.value_load(g["expert32"][0:1, bass.ds(t, 1)], min_val=0, max_val=NE - 1)
                act.wait_ge(hidden, t + 1)
                if not first:
                    act.wait_ge(hrest, t - 1)
                act.nop()
                for k in range(HC):
                    act.activation(hf[:, i, k, :], pH[i][:, k, :], ACT.Gelu,
                                   bias=b1c[:, bass.ds(e, 1), k]).then_inc(gelued, 1)
            act.wait_ge(b1kept, 1)
            x_high(0, 0, True)
            x_high(1, 1, True)
            gelu(0, 0, True)
            x_high(2, 0, False)
            gelu(1, 1, True)
            with act.Fori(1, XT // 2 - 1) as it:
                for i in range(2):
                    x_high(it * 2 + i + 1, 1 - i, False)
                    gelu(it * 2 + i, i, False)
            x_high(XT - 1, 1, False)
            gelu(XT - 2, 0, False)
            gelu(XT - 1, 1, False)

        @block.vector
        def _(dve):
            for n in range(chunks):
                dve.wait_ge(high, n + 1)
                _, h, low, _ = chunk(n)
                dve.tensor_tensor(flat(low), stage[:, n % WB, :], flat(h), ALU.subtract).then_inc(rest, 1)
            dve.wait_ge(biases, 32)

            def x_rest(t, i, first):
                dve.wait_ge(xhigh, t + 1)
                if not first:
                    dve.wait_ge(hidden, t - 1)
                dve.tensor_tensor(xl[:, i, :, :], pT[i][:, :, :], xh[:, i, :, :], ALU.subtract).then_inc(xrest, 1)

            def split(t, i, first):
                if not first:
                    dve.wait_ge(out_s, t - 1)
                for half in range(2):
                    ks = slice(half * HC // 2, (half + 1) * HC // 2)
                    dve.wait_ge(gelued, t * HC + (half + 1) * HC // 2)
                    dve.tensor_copy(hh[:, i, ks, :], hf[:, i, ks, :]).then_inc(hhigh, 1)
                    dve.wait_ge(hhigh, t * 2 + half + 1)
                    ins = dve.tensor_tensor(hl[:, i, ks, :], hf[:, i, ks, :], hh[:, i, ks, :], ALU.subtract)
                ins.then_inc(hrest, 1)

            def add_bias(t, it, i, first):
                e = dve.value_load(g["expert32"][0:1, bass.ds(t, 1)], min_val=0, max_val=NE - 1)
                dve.wait_ge(out_s, t + 1)
                if not first:
                    dve.wait_ge(stored[i], it * 16)
                dve.tensor_tensor(yt[:, i, :], pY[i][:, :], b2b[:, bass.ds(e, 1), :].rearrange("p a f -> p (a f)"), ALU.add).then_inc(biased, 1)
            x_rest(0, 0, True)
            x_rest(1, 1, True)
            split(0, 0, True)
            x_rest(2, 0, False)
            split(1, 1, True)
            add_bias(0, 0, 0, True)
            x_rest(3, 1, False)
            split(2, 0, False)
            add_bias(1, 0, 1, True)
            with dve.Fori(1, XT // 2 - 2) as it:
                for i in range(2):
                    x_rest(it * 2 + i + 2, i, False)
                    split(it * 2 + i + 1, 1 - i, False)
                    add_bias(it * 2 + i, it, i, False)
            x_rest(XT - 2, 0, False)
            split(XT - 3, 1, False)
            add_bias(XT - 4, XT // 2 - 2, 0, False)
            x_rest(XT - 1, 1, False)
            split(XT - 2, 0, False)
            add_bias(XT - 3, XT // 2 - 2, 1, False)
            split(XT - 1, 1, False)
            add_bias(XT - 2, XT // 2 - 1, 0, False)
            add_bias(XT - 1, XT // 2 - 1, 1, False)

        @block.tensor
        def _(pe):
            pe.wait_ge(biases, 32)
            pe.transpose(pY[0][:, 0:NE * HC], b1r[:, :], c["ident"][0:NE * HC, 0:NE * HC]).then_inc(b1turned, 1)
            pe.wait_ge(rest, chunks)
            pe.wait_ge(b1kept, 1)

            def turn(t, it, j, i, first):
                pe.wait_ge(xload[j], it * 16 + 16)
                if not first:
                    pe.wait_ge(xrest, t - 1)
                for k in range(KT):
                    ins = pe.transpose(pT[i][:, k, :], xt[:, j, k * P:(k + 1) * P], c["ident"][:, :])
                ins.then_inc(turned, 1)

            def layer1(t, i, first):
                e = pe.value_load(g["expert32"][0:1, bass.ds(t, 1)], min_val=0, max_val=NE - 1)
                pe.wait_ge(xrest, t + 1)
                if not first:
                    pe.wait_ge(gelued, (t - 1) * HC)
                for m in range(HC):
                    cols = slice(m * P, (m + 1) * P)
                    for k in range(KT):
                        wh = w1h[:, bass.ds(e * KT + k, 1), cols].rearrange("p a f -> p (a f)")
                        wl = w1l[:, bass.ds(e * KT + k, 1), cols].rearrange("p a f -> p (a f)")
                        pe.matmul(pH[i][:, m, :], wh, xh[:, i, k, :], start=k == 0, stop=False)
                        pe.matmul(pH[i][:, m, :], wh, xl[:, i, k, :], start=False, stop=False)
                        ins = pe.matmul(pH[i][:, m, :], wl, xh[:, i, k, :], start=False, stop=k == KT - 1)
                ins.then_inc(hidden, 1)

            def layer2(t, i, first):
                e = pe.value_load(g["expert32"][0:1, bass.ds(t, 1)], min_val=0, max_val=NE - 1)
                pe.wait_ge(hrest, t + 1)
                if not first:
                    pe.wait_ge(biased, t - 1)
                for m in range(HC):
                    wh = w2h[:, bass.ds(e * HC + m, 1), :].rearrange("p a f -> p (a f)")
                    wl = w2l[:, bass.ds(e * HC + m, 1), :].rearrange("p a f -> p (a f)")
                    pe.matmul(pY[i][:, :], hh[:, i, m, :], wh, start=m == 0, stop=False)
                    pe.matmul(pY[i][:, :], hh[:, i, m, :], wl, start=False, stop=False)
                    ins = pe.matmul(pY[i][:, :], hl[:, i, m, :], wh, start=False, stop=m == HC - 1)
                ins.then_inc(out_s, 1)
            turn(0, 0, 0, 0, True)
            turn(1, 0, 1, 1, True)
            layer1(0, 0, True)
            turn(2, 0, 2, 0, False)
            layer1(1, 1, True)
            layer2(0, 0, True)
            turn(3, 0, 3, 1, False)
            layer1(2, 0, False)
            layer2(1, 1, True)
            LOOPS = (XT - 4) // 4
            with pe.Fori(1, 1 + LOOPS) as it:
                for j in range(4):
                    t = it * 4 + j
                    turn(t, it, j, j % 2, False)
                    layer1(t - 1, (j + 1) % 2, False)
                    layer2(t - 2, j % 2, False)
            for t in range(4 + 4 * LOOPS, XT + 2):
                if t < XT:
                    turn(t, t // 4, t % 4, t % 2, False)
                if t - 1 < XT:
                    layer1(t - 1, (t - 1) % 2, False)
                layer2(t - 2, t % 2, False)


def combine(nc, g, x1, ys, out):
    ctx = ExitStack()
    with ctx:
        sb = lambda n, s, d=FP32: ctx.enter_context(nc.sbuf_tensor(f"c_{n}", s, d))
        sem = lambda n: ctx.enter_context(nc.semaphore(f"c_{n}"))
        B = 7
        xr = sb("x", [P, NT, F])
        y = sb("y", [P, B, TOPK, F])
        xload, stored = sem("xload"), sem("stored")
        gathered = [sem(f"gathered{j}") for j in range(B)]
        half, mixed = sem("half"), sem("mixed")
        block = ctx.enter_context(nc.Block())

        @block.sync
        def _(sp):
            sp.dma_start(xr[:, :, :], x1.rearrange("(b p) f -> p b f", p=P)).then_inc(xload, 16)
            for r in range(NT // B):
                sp.wait_ge(mixed, (r + 1) * B)
                full = B if r < NT // B - 1 else B - 1
                b = r * B
                sp.dma_start(out[b * P:(b + full) * P, :].rearrange("(b p) f -> p b f", p=P), xr[:, b:b + full, :]).then_inc(stored, 16)
            sp.dma_start(out[(NT - 1) * P:N, :], xr[0:LAST, NT - 1, :]).then_inc(stored, 16)
            sp.wait_ge(stored, 16 * (NT // B + 1))

        @block.gpsimd
        def _(pool):
            for b in range(NT):
                if b >= B:
                    pool.wait_ge(mixed, b - B + 1)
                for k in range(TOPK):
                    pool.indirect_dma_start(y[:, b % B, k, :], None, ys, bass.IndirectOffsetOnAxis(ap=g["pos"][:, k, b:b + 1], axis=0)
                                            ).then_inc(gathered[b % B], 16)

        @block.vector
        def _(dve):
            dve.wait_ge(xload, 16)
            with dve.Fori(0, NT // B) as it:
                for j in range(B):
                    b = it * B + j
                    here = xr[:, bass.ds(b, 1), :].rearrange("p a f -> p (a f)")
                    dve.wait_ge(gathered[j], it * 32 + 32)
                    dve.scalar_tensor_tensor(here, y[:, j, 0, :], g["weight"][:, 0, bass.ds(b, 1)], here, ALU.mult, ALU.add).then_inc(half, 1)
                    dve.wait_ge(half, b + 1)
                    dve.scalar_tensor_tensor(here, y[:, j, 1, :], g["weight"][:, 1, bass.ds(b, 1)], here, ALU.mult, ALU.add).then_inc(mixed, 1)


_INS = ["x", "src", "dst", "L0_gnn_W_w", "L0_gnn_W_b", "L0_gnn_a_w", "L0_gnn_a_b", "L0_ffn_Wg", "L0_ffn_bg",
        "L0_ffn_W1", "L0_ffn_b1", "L0_ffn_W2", "L0_ffn_b2"]


def kernel(**inputs):
    import concourse.bacc as _bacc
    from concourse.bass_utils import run_bass_kernel_spmd as _run

    nc = _bacc.Bacc("TRN2", target_bir_lowering=False, num_devices=1)
    arrays, args = {}, []
    for name in _INS:
        a = np.ascontiguousarray(inputs[name])
        arrays[f"in_{name}_dram"] = a
        args.append(nc.dram_tensor(f"in_{name}_dram", a.shape, mybir.dt.from_np(a.dtype), kind="ExternalInput").ap())
    args.append(nc.dram_tensor("out_0_dram", (N, F), FP32, kind="ExternalOutput").ap())
    gnn_moe_kernel(nc, *args)
    return _run(nc, [arrays], core_ids=[0]).results[0]["out_0_dram"]
```

```python
from contextlib import ExitStack

import numpy as np
import concourse.bass as bass
import concourse.mybir as mybir
from concourse.alu_op_type import AluOpType as ALU

FP32, BF16, FP16 = mybir.dt.float32, mybir.dt.bfloat16, mybir.dt.float16
I32 = mybir.dt.int32
ACT = mybir.ActivationFunctionType
X = mybir.AxisListType.X

P = 128
N, F, E = 6250, 256, 100000
NT = -(-N // P)
LAST = N - (NT - 1) * P
U = 7
assert NT % U == 0 and NT % 8 == 1
KT = F // P
EPS = 1e-5
SLOPE = 0.2
FAR = -1e30

EP = 125
ET = E // EP
BY_DMA = 352
G = 3
GROUPS = (E + NT * (G * P - 1)) // (G * P)
GROUPS += GROUPS % 2
PAIRS = GROUPS // 2
RING = 6
SLOTS = G * GROUPS
TW = F + 2
COUNT, SCORE = F, F + 1
AW = F + 1

NE, H = 8, 1024
HC = H // P
TOPK = 2
XG = 2
XT = (N * TOPK + NE * (XG * P - 1)) // (XG * P)
XT += XT % 2
XSLOTS = XT * XG
XR = 3


class Steps:

    def __init__(self, eng, sem):
        self.eng, self.sem, self.base, self.n = eng, sem, 0, 0

    def done(self, ins):
        ins.then_inc(self.sem, 1)
        self.n += 1

    def settle(self):
        self.eng.wait_ge(self.sem, self.base + self.n)

    def then(self, ins):
        self.done(ins)
        self.settle()


def repeat(eng, steps, count, per, body):
    start = steps.base + steps.n
    with eng.Fori(0, count) as it:
        steps.base, steps.n = it * per + start, 0
        body(it)
        assert steps.n == per, (steps.n, per)
    steps.base, steps.n = start + count * per, 0


def flat(ap):
    return ap.rearrange("p a b -> p (a b)")


def wait(eng, on, value):
    if not isinstance(value, int) or value > 0:
        eng.wait_ge(on, value)


def load_x(eng, x, xr, xload, k):
    b0, b1 = k * U, min((k + 1) * U, NT - 1)
    eng.dma_start(xr[:, k % XR, 0:b1 - b0, :], x[b0 * P:b1 * P, :].rearrange("(b p) f -> p b f", p=P)).then_inc(xload[k % XR], 16)


def row(ap, b):
    return ap[:, bass.ds(b, 1), :].rearrange("p b a -> p (b a)")


def over_middle(ap, n):
    return ap.unsqueeze(1).broadcast_to([ap.shape[0], n, ap.shape[1]])


def over_last(ap, n):
    return ap.unsqueeze(2).broadcast_to([ap.shape[0], ap.shape[1], n])


def gnn_moe_kernel(nc, x, src, dst, W_w, W_b, a_w, a_b, Wg, bg, W1, b1, W2, b2, out):
    with ExitStack() as ctx:
        def sb(name, shape, dt=FP32, stack=ctx):
            return stack.enter_context(nc.sbuf_tensor(name, shape, dt))

        table = nc.dram_tensor("table", (NT * P, TW), FP32, kind="Internal").ap()
        xn_rows = nc.dram_tensor("expert_in", (NT * P, F), FP32, kind="Internal").ap()
        ys = nc.dram_tensor("expert_out", (TOPK * NT * P + XSLOTS * P, F), FP32, kind="Internal").ap()
        spots = nc.dram_tensor("spots", (P * SLOTS, 1), I32, kind="Internal").ap()
        x1 = nc.dram_tensor("residual", (NT * P, F), FP32, kind="Internal").ap()

        c = {}
        c["ident"] = sb("ident", [P, P])
        c["before"] = sb("before", [P, P])
        c["ones"] = sb("ones", [P, P])
        c["iota"] = sb("iota", [P, SLOTS])
        c["iota16"] = sb("iota16", [P, SLOTS], FP16)
        c["eps"] = sb("eps", [P, 1])
        c["valid"] = sb("valid", [P, 1])
        row_score = sb("row_score", [P, NT])
        row_scoreT = sb("row_scoreT", [NT, P])
        lift = sb("lift", [P, 1])
        constants(nc, c)
        g = {}
        g["take"] = sb("take", [P, XSLOTS], I32)
        g["give"] = sb("give", [P, XSLOTS], I32)
        g["weight"] = sb("weight", [P, TOPK, NT])
        g["expert32"] = sb("expert32", [P, XT], I32)
        with ExitStack() as sums:
            e = {name: sb(name, [EP, ET], I32, sums) for name in ("row", "col")}
            projection(nc, c, x, W_w, W_b, a_w, a_b, src, dst, e, table, spots, row_score, row_scoreT, lift)
            s = {}
            for name, shape, dt in [
                ("cols", [P, SLOTS], I32),
                ("rows", [P, SLOTS], FP32),
                ("tile32", [P, GROUPS], I32),
                ("fresh", [P, GROUPS], FP32),
                ("rscore", [P, GROUPS], FP32),
            ]:
                s[name] = sb(name, shape, dt, sums)
            route_edges(nc, c, s, e, spots, row_scoreT)
            acc = sb("acc", [P, NT + 1, AW], FP32, sums)
            xr = sb("x_ahead", [P, XR, U, F], FP32, sums)
            xload = [sums.enter_context(nc.semaphore(f"x_ahead{k}")) for k in range(XR)]
            attention(nc, c, s, table, acc, lift, x, xr, xload)
            gate(nc, c, g, x, xr, xload, acc, Wg, bg, xn_rows, x1)
        experts(nc, c, g, xn_rows, ys, W1, b1, W2, b2)
        combine(nc, g, x1, ys, out)


def constants(nc, c):
    with nc.sbuf_tensor("iota32", [P, SLOTS], I32) as iota32, nc.semaphore("filled") as filled, nc.Block() as block:
        @block.gpsimd
        def _(pool):
            pool.iota(iota32[:, :], [[1, SLOTS]], base=0, channel_multiplier=0).then_inc(filled, 1)
            pool.memset(c["ones"][:, :], 1.0).then_inc(filled, 1)
            pool.memset(c["ident"][:, :], 0.0).then_inc(filled, 1)
            pool.memset(c["eps"][:, :], EPS)
            pool.wait_ge(filled, 3)
            pool.affine_select(out=c["ident"][:, :], in_=c["ident"][:, :], compare_op=ALU.not_equal, fill=1.0,
                               base=0, pattern=[[-1, P]], channel_multiplier=1).then_inc(filled, 1)
            pool.affine_select(out=c["before"][:, :], in_=c["ones"][:, :], compare_op=ALU.is_gt, fill=0.0,
                               base=0, pattern=[[1, P]], channel_multiplier=-1)
            pool.affine_select(out=c["valid"][:, :], in_=c["ones"][:, 0:1], compare_op=ALU.is_gt, fill=0.0,
                               base=LAST, pattern=[[1, 1]], channel_multiplier=-1)

        @block.vector
        def _(dve):
            dve.wait_ge(filled, 4)
            dve.tensor_copy(c["iota"][:, :], iota32[:, :])
            dve.tensor_copy(c["iota16"][:, :], iota32[:, :])


def projection(nc, c, x, W_w, W_b, a_w, a_b, src, dst, e, table, spots, row_score, row_scoreT, lift):
    ctx = ExitStack()
    with ctx:
        sb = lambda n, s, d=FP32: ctx.enter_context(nc.sbuf_tensor(n, s, d))
        ps = lambda n, s, d=FP32: ctx.enter_context(nc.psum_tensor(n, s, d))
        sem = lambda n: ctx.enter_context(nc.semaphore(n))
        xa = sb("p_x", [P, NT, F])
        wh = sb("p_wh", [P, NT, TW])
        whf = sb("p_whf", [P, 2, F])
        score = sb("p_score", [P, NT])
        halves = wh[:, :, 0:SCORE].bitcast(BF16)
        stats = sb("p_stats", [P, NT, 6])
        mv = sb("p_mv", [P, NT, 2])
        rstd = sb("p_rstd", [P, NT])
        xn = sb("p_xn", [P, 2, F])
        xT = sb("p_xT", [P, 2, KT, P])
        wx = sb("p_wx", [P, KT, TW])
        bx = sb("p_bx", [P, TW])
        av = sb("p_av", [P, 2, F])
        ab = sb("p_ab", [P, 1])
        junk = sb("p_junk", [P, F])
        ZQ = 3
        assert SLOTS % ZQ == 0
        zeros = sb("p_zeros", [P, SLOTS // ZQ], I32)
        low = sb("p_low", [P, 1])
        lowT = sb("p_lowT", [1, 1])
        pT = [ps(f"p_pT{i}", [P, KT, P]) for i in range(2)]
        pW = [ps(f"p_pW{i}", [P, TW]) for i in range(2)]
        pL = ps("p_pL", [P, 512])
        loaded = [sem(f"x_loaded{k}") for k in range(NT // U)]
        weights, vec, cleared = sem("w_loaded"), sem("p_vec"), sem("p_cleared")
        spread, rooted, ready = sem("var_ready"), sem("std_ready"), sem("xn_ready")
        turned, kept, multiplied, added = sem("xT_psum"), sem("xT_sbuf"), sem("wh_psum"), sem("wh_sbuf")
        low_ready, low_turned, low_one, low_all = sem("low_ready"), sem("low_turned"), sem("low_one"), sem("low_all")
        highs, lows, edges = sem("p_highs"), sem("p_lows"), sem("edges")
        shifted, rowT, stored, zeroed = sem("shifted"), sem("rowT"), sem("stored"), sem("zeroed")
        block = ctx.enter_context(nc.Block())

        @block.sync
        def _(sp):
            for k in range(NT // U):
                b0, b1 = k * U, min((k + 1) * U, NT - 1)
                sp.dma_start(xa[:, b0:b1, :], x[b0 * P:b1 * P, :].rearrange("(b p) f -> p b f", p=P)).then_inc(loaded[k], 16)
            sp.wait_ge(cleared, 1)
            sp.dma_start(xa[0:LAST, NT - 1, :], x[(NT - 1) * P:N, :]).then_inc(loaded[-1], 16)
            sp.dma_start(e["row"][:, :], src.rearrange("(p t) -> p t", p=EP)).then_inc(edges, 16)
            sp.dma_start(e["col"][:, :], dst.rearrange("(p t) -> p t", p=EP)).then_inc(edges, 16)
            sp.wait_ge(edges, 32)
            sp.wait_ge(cleared, 3)

            def store(b, n):
                sp.wait_ge(highs, b + n)
                sp.wait_ge(lows, b + n)
                sp.nop()
                sp.dma_start(table[bass.ds(b * P, n * P), :].rearrange("(b p) f -> p b f", p=P), wh[:, bass.ds(b, n), :]).then_inc(stored, 16)
            with sp.Fori(0, NT // 2) as it:
                store(it * 2, 2)
            store(NT - 1, 1)
            sp.wait_ge(stored, 16 * (NT // 2 + 1))

        @block.gpsimd
        def _(pool):
            pool.memset(xa[:, NT - 1, :], 0.0).then_inc(cleared, 1)
            pool.memset(zeros[:, :], 0).then_inc(cleared, 1)
            pool.memset(halves[:, :, 2 * COUNT:2 * COUNT + 1], 1.0)
            pool.memset(halves[:, :, 2 * COUNT + 1:2 * COUNT + 2], 0.0).then_inc(cleared, 1)

            def low_half(b, i):
                pool.wait_ge(highs, b + 1)
                pool.nop()
                pool.tensor_tensor(row(halves, b)[:, 0:F], whf[:, i, :], row(halves, b)[:, F:2 * F], ALU.subtract).then_inc(lows, 1)
            with pool.Fori(0, NT // 2) as it:
                for i in range(2):
                    low_half(it * 2 + i, i)
            low_half(NT - 1, 0)

        @block.scalar
        def _(act):
            act.dma_start(wx[:, :, 0:F], W_w.rearrange("(k p) f -> p k f", p=P)).then_inc(weights, 16)
            act.dma_start(bx[:, 0:F], W_b.rearrange("(a f) -> a f", a=1).partition_broadcast(P).rearrange("p a f -> p (a f)")).then_inc(weights, 16)
            act.dma_start(av[:, 0, :], a_w[F:2 * F].rearrange("(a f) -> a f", a=1).partition_broadcast(P).rearrange("p a f -> p (a f)")).then_inc(weights, 16)
            act.dma_start(av[:, 1, :], a_w[0:F].rearrange("(a f) -> a f", a=1).partition_broadcast(P).rearrange("p a f -> p (a f)")).then_inc(weights, 16)
            act.dma_start(ab[:, :], a_b.rearrange("(a f) -> a f", a=1).partition_broadcast(P).rearrange("p a f -> p (a f)")).then_inc(weights, 16)
            act.wait_ge(spread, 1)
            act.activation(rstd[:, :], mv[:, :, 1], ACT.Sqrt, bias=c["eps"][:, :]).then_inc(rooted, 1)
            act.wait_ge(cleared, 2)
            act.dma_start(spots.rearrange("(p q t) a -> p q (t a)", p=P, q=ZQ), over_middle(zeros[:, :], ZQ)).then_inc(zeroed, 16)

            def keep(b, i, first):
                act.wait_ge(turned, b + 1)
                if not first:
                    act.wait_ge(multiplied, b - 1)
                act.activation(xT[:, i, :, :], pT[i][:, :, :], ACT.Copy).then_inc(kept, 1)

            def high(b, i):
                act.wait_ge(added, b + 1)
                act.nop()
                act.activation(row(halves, b)[:, F:2 * F], whf[:, i, :], ACT.Copy).then_inc(highs, 1)
            keep(0, 0, True)
            keep(1, 1, True)
            with act.Fori(0, NT // 2 - 1) as it:
                for i in range(2):
                    keep(it * 2 + i + 2, i, False)
                    high(it * 2 + i, i)
            keep(NT - 1, 0, False)
            for b in range(NT - 3, NT):
                high(b, b % 2)
            act.wait_ge(zeroed, 16)

        @block.vector
        def _(dve):
            st = Steps(dve, vec)
            dve.wait_ge(weights, 80)
            for i in range(2):
                for k in range(KT):
                    st.then(dve.tensor_tensor_reduce(out=junk[:, :], in0=wx[:, k, 0:F], in1=av[:, i, :], scale=1.0, scalar=0.0,
                                                     op0=ALU.mult, op1=ALU.add, accum_out=wx[:, k, COUNT + i:COUNT + i + 1]))
                st.then(dve.tensor_tensor_reduce(out=junk[:, :], in0=bx[:, 0:F], in1=av[:, i, :], scale=1.0, scalar=0.0,
                                                 op0=ALU.mult, op1=ALU.add, accum_out=bx[:, COUNT + i:COUNT + i + 1]))
            st.then(dve.tensor_tensor(bx[:, COUNT:COUNT + 1], bx[:, COUNT:COUNT + 1], ab[:, :], ALU.add))
            for b in range(NT):
                if b % U == 0:
                    dve.wait_ge(loaded[b // U], 16 if b < NT - U else 32)
                st.done(dve.bn_stats(stats[:, b, :], xa[:, b, :]))
            st.settle()
            st.then(dve.tensor_tensor(mv[:, :, 0], stats[:, :, 1], stats[:, :, 4], ALU.add))
            st.then(dve.tensor_tensor(rstd[:, :], stats[:, :, 1], stats[:, :, 4], ALU.subtract))
            st.then(dve.tensor_tensor(mv[:, :, 1], stats[:, :, 2], stats[:, :, 5], ALU.add))
            st.then(dve.tensor_scalar(mv[:, :, 0], mv[:, :, 0], 0.5, None, ALU.mult))
            st.then(dve.tensor_tensor(rstd[:, :], rstd[:, :], rstd[:, :], ALU.mult))
            st.then(dve.tensor_scalar(rstd[:, :], rstd[:, :], 0.25, None, ALU.mult))
            st.then(dve.scalar_tensor_tensor(mv[:, :, 1], mv[:, :, 1], 1.0 / F, rstd[:, :], ALU.mult, ALU.add))
            dve.sem_inc(spread, 1)
            dve.wait_ge(rooted, 1)
            st.then(dve.reciprocal(rstd[:, :], rstd[:, :]))

            def norm(b, i, first):
                if not first:
                    dve.wait_ge(turned, b - 1)
                dve.tensor_scalar(xn[:, i, :], xa[:, bass.ds(b, 1), :].rearrange("p a f -> p (a f)"), mv[:, bass.ds(b, 1), 0], rstd[:, bass.ds(b, 1)],
                                  ALU.subtract, ALU.mult).then_inc(ready, 1)

            def add_bias(b, i, first=False):
                dve.wait_ge(multiplied, b + 1)
                if not first:
                    dve.wait_ge(lows, b - 1)
                dve.tensor_tensor(score[:, bass.ds(b, 1)], pW[i][:, COUNT:SCORE], bx[:, COUNT:SCORE], ALU.add)
                dve.tensor_tensor(row(wh, b)[:, SCORE:TW], pW[i][:, SCORE:TW], bx[:, SCORE:TW], ALU.add)
                dve.tensor_tensor(whf[:, i, :], pW[i][:, 0:F], bx[:, 0:F], ALU.add).then_inc(added, 1)
            norm(0, 0, True)
            norm(1, 1, True)
            for b in range(2):
                norm(b + 2, b, False)
                add_bias(b, b, True)
            with dve.Fori(1, NT // 2 - 1) as it:
                for i in range(2):
                    norm(it * 2 + i + 2, i, False)
                    add_bias(it * 2 + i, i)
            norm(NT - 1, 0, False)
            add_bias(NT - 3, 0)
            add_bias(NT - 2, 1)
            add_bias(NT - 1, 0)
            dve.wait_ge(added, NT)
            dve.tensor_reduce(low[:, :], wh[:, :, SCORE], X, ALU.min).then_inc(low_ready, 1)
            dve.wait_ge(low_turned, 1)
            dve.tensor_reduce(lowT[:, :], pL[0:1, 0:P], X, ALU.min).then_inc(low_one, 1)
            dve.wait_ge(low_all, 1)
            st.then(dve.tensor_scalar(lift[:, :], pL[:, P:P + 1], -1.0, 1.0, ALU.mult, ALU.add))
            st.then(dve.tensor_scalar(row_score[:, :], score[:, :], lift[:, :], None, ALU.subtract))
            dve.sem_inc(shifted, 1)
            dve.wait_ge(rowT, 1)
            dve.tensor_copy(row_scoreT[:, :], pL[0:NT, 2 * P:3 * P])

        @block.tensor
        def _(pe):
            def turn(b, i, first):
                pe.wait_ge(ready, b + 1)
                if not first:
                    pe.wait_ge(kept, b - 1)
                for k in range(KT):
                    ins = pe.transpose(pT[i][:, k, :], xn[:, i, k * P:(k + 1) * P], c["ident"][:, :])
                ins.then_inc(turned, 1)

            def multiply(b, i, first):
                pe.wait_ge(kept, b + 1)
                if not first:
                    pe.wait_ge(added, b - 1)
                for k in range(KT):
                    ins = pe.matmul(pW[i][:, :], xT[:, i, k, :], wx[:, k, :], start=k == 0, stop=k == KT - 1)
                ins.then_inc(multiplied, 1)
            turn(0, 0, True)
            turn(1, 1, True)
            multiply(0, 0, True)
            turn(2, 0, False)
            multiply(1, 1, True)
            with pe.Fori(1, NT // 2) as it:
                for i in range(2):
                    turn(it * 2 + i + 1, (i + 1) % 2, False)
                    multiply(it * 2 + i, i, False)
            multiply(NT - 1, 0, False)
            pe.wait_ge(low_ready, 1)
            pe.transpose(pL[0:1, 0:P], low[:, :], c["ident"][:, :]).then_inc(low_turned, 1)
            pe.wait_ge(low_one, 1)
            pe.matmul(pL[:, P:P + 1], c["ones"][0:1, :], lowT[:, :], start=True, stop=True).then_inc(low_all, 1)
            pe.wait_ge(shifted, 1)
            pe.transpose(pL[0:NT, 2 * P:3 * P], row_score[:, :], c["ident"][:, :]).then_inc(rowT, 1)


class Route:

    def __init__(self, ctx, nc, c, tag, parts, nb, nt, size, tiles):
        self.c, self.parts, self.nb, self.nt, self.size, self.tiles = c, parts, nb, nt, size, tiles
        self.per, self.shift = size // P, 11
        self.up = (1 << self.shift) // self.per + 1
        most = -(-parts * nt // P) + self.per
        assert all(n * self.up >> self.shift == n // self.per for n in range(most + 1)) and most * self.up < 1 << 24
        sb = lambda n, s, d=FP32: ctx.enter_context(nc.sbuf_tensor(f"{tag}_{n}", s, d))
        ps = lambda n, s: ctx.enter_context(nc.psum_tensor(f"{tag}_{n}", s, FP32))
        self.onehot = sb("onehot", [parts, nb, nt], FP16)
        self.rank = sb("rank", [parts, nb, nt], FP16)
        self.upto = sb("upto", [parts, nb])
        self.own = sb("own", [parts, nb])
        self.base = sb("base", [parts, nb])
        self.t32 = sb("t32", [P, nb], I32)
        self.need = sb("need", [P, nb])
        self.end = sb("end", [P, nb])
        self.begin = sb("begin", [P, nb])
        self.endc = sb("endc", [nb, 1])
        self.beginc = sb("beginc", [nb, 1])
        self.past = sb("past", [nb, tiles])
        self.member = sb("member", [nb, tiles])
        self.kind = sb("kind", [P, tiles])
        self.zero = sb("zero", [P, P]) if nb == NE else None
        self.p_n = ps("p_n", [P, 512])
        self.p_kind = ps("p_kind", [P, tiles])
        self.to_t = ctx.enter_context(nc.semaphore(f"{tag}_to_tensor"))
        self.to_v = ctx.enter_context(nc.semaphore(f"{tag}_to_vector"))

    def vector(self, dve, st):
        nb, nt, parts = self.nb, self.nt, self.parts
        st.then(dve.tensor_tensor_scan(flat(self.rank[:, :, :]), flat(self.onehot[:, :, :]), flat(self.onehot[:, :, :]), 0.0, ALU.add, ALU.max))
        st.then(dve.tensor_copy(self.upto[:, :], self.rank[:, :, nt - 1]))
        st.then(dve.tensor_copy(self.own[:, :], self.upto[:, :]))
        st.then(dve.tensor_tensor(self.own[:, 1:nb], self.upto[:, 1:nb], self.upto[:, 0:nb - 1], ALU.subtract))
        dve.sem_inc(self.to_t, 1)
        dve.wait_ge(self.to_v, 1)
        st.then(dve.tensor_scalar(self.t32[:, :], self.p_n[:, 0:nb], float(P - 1), None, ALU.add))
        st.then(dve.tensor_scalar(self.t32[:, :], self.t32[:, :], P.bit_length() - 1, None, ALU.logical_shift_right))
        st.then(dve.tensor_scalar(self.t32[:, :], self.t32[:, :], float(self.per - 1), float(self.up), ALU.add, ALU.mult))
        st.then(dve.tensor_scalar(self.t32[:, :], self.t32[:, :], self.shift, None, ALU.logical_shift_right))
        st.then(dve.tensor_copy(self.need[:, :], self.t32[:, :]))
        st.then(dve.tensor_tensor_scan(self.end[:, :], self.need[:, :], self.need[:, :], 0.0, ALU.add, ALU.max))
        st.then(dve.tensor_tensor(self.begin[:, :], self.end[:, :], self.need[:, :], ALU.subtract))
        st.then(dve.tensor_tensor(self.base[:, :], self.own[:, :], self.upto[:, :], ALU.subtract))
        st.then(dve.scalar_tensor_tensor(self.base[:, :], self.base[:, :], -1.0, self.p_n[0:parts, P:P + nb], ALU.add, ALU.add))
        st.then(dve.scalar_tensor_tensor(self.base[:, :], self.begin[0:parts, :], float(self.size), self.base[:, :], ALU.mult, ALU.add))
        dve.sem_inc(self.to_t, 1)
        dve.wait_ge(self.to_v, 2)
        st.then(dve.tensor_copy(self.endc[:, :], self.p_n[0:nb, 2 * P:2 * P + 1]))
        st.then(dve.tensor_copy(self.beginc[:, :], self.p_n[0:nb, 3 * P:3 * P + 1]))
        st.then(dve.tensor_scalar(self.past[:, :], self.c["iota"][0:nb, 0:self.tiles], self.endc[:, :], None, ALU.is_ge))
        st.then(dve.scalar_tensor_tensor(self.member[:, :], self.c["iota"][0:nb, 0:self.tiles], self.beginc[:, :], self.past[:, :], ALU.is_ge, ALU.subtract))
        dve.sem_inc(self.to_t, 1)
        dve.wait_ge(self.to_v, 3)
        st.then(dve.tensor_copy(self.kind[:, :], self.p_kind[:, :]))

    def tensor(self, pe):
        nb, parts = self.nb, self.parts
        pe.wait_ge(self.to_t, 1)
        pe.matmul(self.p_n[:, 0:nb], self.c["ones"][0:parts, :], self.own[:, :], start=True, stop=True)
        pe.matmul(self.p_n[0:parts, P:P + nb], self.c["before"][0:parts, 0:parts], self.own[:, :], start=True, stop=True).then_inc(self.to_v, 1)
        pe.wait_ge(self.to_t, 2)
        pe.transpose(self.p_n[0:nb, 2 * P:3 * P], self.end[:, :], self.c["ident"][:, :])
        pe.transpose(self.p_n[0:nb, 3 * P:4 * P], self.begin[:, :], self.c["ident"][:, :]).then_inc(self.to_v, 1)
        pe.wait_ge(self.to_t, 3)
        pe.matmul(self.p_kind[:, :], self.c["ones"][0:nb, :], self.past[:, :], start=True, stop=True).then_inc(self.to_v, 1)


def route_edges(nc, c, s, e, spots, row_scoreT):
    ctx = ExitStack()
    with ctx:
        sb = lambda n, s, d=FP32: ctx.enter_context(nc.sbuf_tensor(f"r_{n}", s, d))
        ps = lambda n, s, d=FP32: ctx.enter_context(nc.psum_tensor(f"r_{n}", s, d))
        sem = lambda n: ctx.enter_context(nc.semaphore(f"r_{n}"))
        row32, col32 = e["row"], e["col"]
        part32, part = sb("part32", [P, SLOTS], I32), sb("part", [P, SLOTS])
        low32, pos = part32[0:EP, 0:ET], part[0:EP, 0:ET]
        tmp32 = sb("tmp32", [EP, ET], I32)
        tile16 = sb("tile16", [EP, ET], FP16)
        high, low = sb("high", [EP, ET], FP16), sb("low", [EP, ET], FP16)
        value, address = row32, col32
        HALF = 16
        assert BY_DMA % (2 * HALF) == 0 and (ET - BY_DMA) % 4 == 0
        staged_value, staged_address = sb("staged_value", [EP, 2, HALF], I32), sb("staged_address", [EP, 2, HALF], I32)
        slot, lane = sb("slot", [EP, ET], FP16), sb("lane", [EP, ET], FP16)
        R = Route(ctx, nc, c, "r_e", EP, NT, ET, G * P, GROUPS)
        B = 4
        lane_high, lane_low = sb("lane_high", [EP, B, P], FP16), sb("lane_low", [EP, B, P], FP16)
        in_slot = flat(R.rank[:, :, :])[:, 0:B * SLOTS].rearrange("p (j s) -> p j s", j=B)
        none = sb("none", [EP, P], FP16)
        PB = 2
        POOLS = [b for b in range(NT) if b % 8 not in (2, 5, 7)]
        place = [s["rows"][0:EP, 0:ET], s["cols"][0:EP, 0:ET].bitcast(FP32)]
        picked, summed = sem("picked"), sem("summed")
        addressed, staged, issued, fetched = sem("addressed"), sem("staged"), sem("issued"), sem("fetched")
        written = [sem(f"written{i}") for i in range(2)]
        C0 = SLOTS // 2
        p_high = [ps(f"p_high{k}", [P, C0]) for k in range(2)]
        p_low = [ps(f"p_low{k}", [P, C0]) for k in range(2)]
        p_score = ps("p_score", [P, GROUPS])
        loaded, vec, made, placed, scores, zeroed, put = (sem(n) for n in (
            "loaded", "vec", "made", "placed", "scores", "zeroed", "put"))
        block = ctx.enter_context(nc.Block())

        @block.sync
        def _(sp):
            for i in range(2):
                sp.wait_ge(written[i], BY_DMA // 2 * 16)
            sp.wait_ge(addressed, 2)
            sp.dma_start(part32[:, :], spots.rearrange("(p t) a -> p (t a)", p=P)).then_inc(fetched, 16)
            sp.wait_ge(fetched, 16)

        @block.gpsimd
        def _(pool):
            for n in range(len(POOLS)):
                pool.wait_ge(picked, n + 1)
                if n == 0:
                    pool.tensor_copy(pos, place[0]).then_inc(summed, 1)
                else:
                    pool.wait_ge(summed, n)
                    pool.tensor_tensor(pos, pos, place[n % PB], ALU.add).then_inc(summed, 1)
            pool.wait_ge(addressed, 1)

            def scatter(it, i):
                first = ET - BY_DMA + (it * 2 + i) * HALF
                pool.tensor_copy(staged_value[:, i, :], value[:, bass.ds(first, HALF)]).then_inc(staged, 1)
                pool.tensor_copy(staged_address[:, i, :], address[:, bass.ds(first, HALF)]).then_inc(staged, 1)
                pool.wait_ge(staged, (it * 2 + i + 1) * 2)
                pool.sem_inc(issued, 1)
                for j in range(HALF):
                    pool.indirect_dma_start(spots, bass.IndirectOffsetOnAxis(ap=staged_address[:, i, j:j + 1], axis=0),
                                            staged_value[:, i, j:j + 1], None).then_inc(written[i], 16)
            for i in range(2):
                scatter(0, i)
            with pool.Fori(1, BY_DMA // (2 * HALF)) as it:
                for i in range(2):
                    pool.wait_ge(written[i], it * HALF * 16)
                    pool.nop()
                    scatter(it, i)

        @block.vector
        def _(dve):
            st = Steps(dve, vec)
            dve.memset(none[:, :], 0.0).then_inc(zeroed, 1)
            st.done(dve.tensor_scalar(low32, row32[:, :], P - 1, None, ALU.bitwise_and))
            st.done(dve.tensor_scalar(tmp32[:, :], col32[:, :], 7, 7, ALU.bitwise_and, ALU.logical_shift_left))
            st.then(dve.tensor_scalar(row32[:, :], row32[:, :], 7, None, ALU.logical_shift_right))
            st.then(dve.tensor_copy(tile16[:, :], row32[:, :]))
            st.then(dve.tensor_scalar(value[:, :], col32[:, :], 7, None, ALU.logical_shift_left))
            st.done(dve.scalar_tensor_tensor(low[:, :], tmp32[:, :], 1.0, low32, ALU.add, ALU.add))
            st.then(dve.tensor_scalar(col32[:, :], col32[:, :], 3, None, ALU.logical_shift_right))
            st.done(dve.scalar_tensor_tensor(value[:, :], value[:, :], 1.0, low32, ALU.add, ALU.add))
            st.done(dve.tensor_copy(high[:, :], col32[:, :]))
            for b in range(NT):
                st.done(dve.tensor_scalar(R.onehot[:, b, :], tile16[:, :], float(b), None, ALU.is_equal))
            st.settle()
            R.vector(dve, st)
            n, more, own = 0, low32.bitcast(FP32), tmp32[:, :].bitcast(FP32)
            st.then(dve.memset(more, 0.0))
            for b in range(NT):
                to = place[n % PB] if b in POOLS else own
                if b in POOLS and n >= PB:
                    dve.wait_ge(summed, n - PB + 1)
                ins = dve.scalar_tensor_tensor(to, R.rank[:, b, :], R.base[:, b:b + 1], R.onehot[:, b, :], ALU.add, ALU.mult)
                if b in POOLS:
                    ins.then_inc(picked, 1)
                    n += 1
                else:
                    st.then(ins)
                    st.then(dve.tensor_tensor(more, more, own, ALU.add))
            dve.wait_ge(summed, n)
            st.then(dve.tensor_tensor(pos, pos, more, ALU.add))
            st.then(dve.tensor_copy(tmp32[:, :], pos))
            st.then(dve.tensor_scalar(low32, tmp32[:, :], P - 1, None, ALU.bitwise_and))
            st.then(dve.tensor_scalar(tmp32[:, :], tmp32[:, :], 7, None, ALU.logical_shift_right))
            dve.scalar_tensor_tensor(address[:, :], low32, float(SLOTS), tmp32[:, :], ALU.mult, ALU.add).then_inc(addressed, 1)
            st.done(dve.tensor_copy(lane[:, :], low32))
            st.then(dve.tensor_copy(slot[:, :], tmp32[:, :]))
            dve.sem_inc(addressed, 1)

            def masks(t, j):
                dve.tensor_scalar(lane_high[:, j, :], c["iota16"][0:EP, 0:P], lane[:, bass.ds(t, 1)], high[:, bass.ds(t, 1)], ALU.is_equal, ALU.mult)
                dve.tensor_scalar(lane_low[:, j, :], c["iota16"][0:EP, 0:P], lane[:, bass.ds(t, 1)], low[:, bass.ds(t, 1)], ALU.is_equal, ALU.mult)
                dve.tensor_scalar(in_slot[:, j, :], c["iota16"][0:EP, :], slot[:, bass.ds(t, 1)], None, ALU.is_equal).then_inc(made, 1)
            for j in range(B):
                masks(j, j)
            with dve.Fori(1, (ET - BY_DMA) // B) as it:
                for j in range(B):
                    dve.wait_ge(placed, (it - 1) * B + j + 1)
                    masks(it * B + j, j)
            kind = R.kind
            st.done(dve.tensor_copy(s["tile32"][:, :], kind[:, :]))
            st.done(dve.memset(s["fresh"][:, 0:1], FAR))
            st.then(dve.tensor_tensor(s["fresh"][:, 1:GROUPS], kind[:, 1:GROUPS], kind[:, 0:GROUPS - 1], ALU.not_equal))
            st.then(dve.tensor_scalar(s["fresh"][:, 1:GROUPS], s["fresh"][:, 1:GROUPS], FAR, None, ALU.mult))
            dve.wait_ge(scores, 1)
            st.then(dve.tensor_copy(s["rscore"][:, :], p_score[:, :]))
            dve.wait_ge(put, 1)
            dve.wait_ge(fetched, 16)
            for k in range(2):
                w = slice(k * C0, (k + 1) * C0)
                st.then(dve.tensor_tensor(part[:, w], part32[:, w], p_low[k][:, :], ALU.add))
                st.then(dve.scalar_tensor_tensor(part[:, w], p_high[k][:, :], 8.0 * P, part[:, w], ALU.mult, ALU.add))
                st.then(dve.tensor_scalar(part32[:, w], part[:, w], -1.0, None, ALU.add))
                st.done(dve.tensor_scalar(s["cols"][:, w], part32[:, w], 7, None, ALU.arith_shift_right))
                st.then(dve.tensor_scalar(part32[:, w], part32[:, w], P - 1, None, ALU.bitwise_and))
                st.done(dve.tensor_scalar(s["rows"][:, w], part[:, w], 0.0, 1000.0, ALU.is_equal, ALU.mult))
                st.then(dve.tensor_scalar(s["cols"][:, w], s["cols"][:, w], 0, None, ALU.max))
                st.then(dve.tensor_tensor(s["rows"][:, w], s["rows"][:, w], part32[:, w], ALU.add))

        @block.tensor
        def _(pe):
            R.tensor(pe)
            pe.matmul(p_score[:, :], row_scoreT[:, :], R.member[:, :], start=True, stop=True).then_inc(scores, 1)
            pe.wait_ge(zeroed, 1)
            pe.wait_ge(made, 1)
            for p in (p_high, p_low):
                for k in range(2):
                    pe.matmul(p[k][:, :], none[:, :], in_slot[:, 0, k * C0:(k + 1) * C0], start=True, stop=False)

            def place(t, j):
                pe.wait_ge(made, t + 1)
                for p, value in ((p_high, lane_high), (p_low, lane_low)):
                    for k in range(2):
                        ins = pe.matmul(p[k][:, :], value[:, j, :], in_slot[:, j, k * C0:(k + 1) * C0], start=False, stop=False)
                ins.then_inc(placed, 1)
            with pe.Fori(0, (ET - BY_DMA) // B) as it:
                for j in range(B):
                    place(it * B + j, j)
            for p in (p_high, p_low):
                for k in range(2):
                    ins = pe.matmul(p[k][:, :], none[:, :], in_slot[:, B - 1, k * C0:(k + 1) * C0], start=False, stop=True)
            ins.then_inc(put, 1)


def attention(nc, c, s, table, acc, lift, x, xr, xload):
    ctx = ExitStack()
    with ctx:
        sb = lambda n, s, d=FP32: ctx.enter_context(nc.sbuf_tensor(f"a_{n}", s, d))
        ps = lambda n, s, d=FP32: ctx.enter_context(nc.psum_tensor(f"a_{n}", s, d))
        sem = lambda n: ctx.enter_context(nc.semaphore(f"a_{n}"))
        T = 2 * G
        index = sb("index", [P, RING * T], I32)
        run = sb("run", [P, 3, 2, AW])
        rows = sb("gathered", [P, RING * T, TW])
        lane = sb("lane", [P, RING * T])
        fresh, rscore = sb("fresh", [P, RING, 2]), sb("rscore", [P, RING, 2])
        lifted = sb("lifted", [P, 3, T])
        onehot = sb("onehot", [P, 3, T, P], BF16)
        raised = sb("raised", [P, 2, T, P])
        member = sb("member", [P, 2, T, P])
        high, low = sb("high", [P, 2, T, P], BF16), sb("low", [P, 2, T, P], BF16)
        tile_mx, sum_e, row_e = sb("tile_mx", [P, 2]), sb("sum_e", [P, 2]), sb("row_e", [P, 2])
        drop, factor = sb("drop", [P, 2, 2]), sb("factor", [P, RING, 2])
        row_info = sb("row_info", [P, 2, 2, 2])
        e1, e2, e3 = sb("e1", [P, T]), sb("e2", [P, T]), sb("e3", [P, T])
        expo, w, w_low = sb("expo", [P, 2, T]), sb("w", [P, 2, T]), sb("w_low", [P, T])
        w_high = sb("w_high", [P, 2, T], BF16)
        p_turn = ps("p_turn", [P, 2, 512])
        p_slot = [ps(f"p_slot{i}", [P, T, 2]) for i in range(2)]
        p_sum = [[ps(f"p_sum{i}{h}", [P, AW]) for h in range(2)] for i in range(2)]
        staged, issued = sem("staged"), sem("issued")
        gathered = [sem(f"gathered{d}") for d in range(RING)]
        masked, lifted_s, raised_s, turned, reduced, informed, dropped, cleared = (sem(n) for n in (
            "masked", "lifted_s", "raised_s", "turned", "reduced", "informed", "dropped", "cleared"))
        membered, spread, exponents, exps, halved, highs, lows, factored, summed, added, vec, kept = (sem(n) for n in (
            "membered", "spread", "exponents", "exps", "halved", "highs", "lows", "factored", "summed", "added", "vec", "kept"))
        block = ctx.enter_context(nc.Block())
        HALF = RING // 2
        RINGS, REST = PAIRS // RING, PAIRS % RING
        assert RING % 6 == 0 and REST >= 2 and RINGS >= 3

        def shift(it, d, n):
            it, d = (it + (d + n) // RING if (d + n) // RING else it), (d + n) % RING
            return (it, d) if not isinstance(it, int) or 0 <= it * RING + d < PAIRS else None

        def size(it, half):
            return min(HALF, PAIRS - it * RING - half * HALF) if isinstance(it, int) else HALF

        def walk(eng, period, steps=None):
            for d in range(RING):
                period(0, d)
            def ring(it):
                for d in range(RING):
                    period(it + 1, d)
            if steps is None:
                with eng.Fori(0, RINGS - 2) as it:
                    ring(it)
            else:
                repeat(eng, steps, RINGS - 2, 9 * RING + 6, ring)
            for d in range(RING):
                period(RINGS - 1, d)
            for d in range(REST):
                period(RINGS, d)

        @block.sync
        def _(sp):
            for k in range(XR):
                load_x(sp, x, xr, xload, k)

        @block.gpsimd
        def _(pool):
            def period(it, d):
                q = it * RING + d
                if d % HALF == 0:
                    n = size(it, d // HALF)
                    for e in range(d, d + n):
                        wait(pool, gathered[e], it * 16 * T)
                    pool.nop()
                    pool.tensor_copy(index[:, d * T:(d + n) * T], s["cols"][:, bass.ds(q * T, n * T)]).then_inc(staged, 1)
                    pool.wait_ge(staged, it * 2 + d // HALF + 1)
                wait(pool, summed, (q - RING + 1) * 2)
                pool.sem_inc(issued, 1)
                for j in range(d * T, (d + 1) * T):
                    pool.indirect_dma_start(rows[:, j, :], None, table, bass.IndirectOffsetOnAxis(ap=index[:, j:j + 1], axis=0)
                                            ).then_inc(gathered[d], 16)
            walk(pool, period)

        @block.scalar
        def _(act):
            def lift_scores(it, d):
                act.wait_ge(gathered[d], (it + 1) * 16 * T)
                act.activation(lifted[:, d % 3, :], rows[:, d * T:(d + 1) * T, SCORE], ACT.Identity, bias=lift[:, :]).then_inc(lifted_s, 1)

            def raise_scores(it, d):
                q = it * RING + d
                act.wait_ge(masked, q + 1)
                wait(act, turned, q - 1)
                act.wait_ge(lifted_s, q + 1)
                for j in range(T):
                    ins = act.activation(raised[:, d % 2, j, :], onehot[:, d % 3, j, :], ACT.Copy, scale=lifted[:, d % 3, j:j + 1])
                ins.then_inc(raised_s, 1)

            def members(it, d):
                q = it * RING + d
                act.wait_ge(reduced, q + 1)
                wait(act, spread, q - 1)
                act.activation(member[:, d % 2, :, :].rearrange("p (h j) m -> p h (j m)", h=2), p_turn[:, :, 0:G * P], ACT.Sign).then_inc(membered, 1)
                act.wait_ge(dropped, q + 1)
                act.activation(factor[:, d, :], drop[:, d % 2, :], ACT.Exp).then_inc(factored, 1)

            def weigh_high(it, d):
                q, i = it * RING + d, d % 2
                act.wait_ge(exponents, q + 1)
                act.activation(w[:, i, :], expo[:, i, :], ACT.Exp).then_inc(exps, 1)
                act.wait_ge(exps, q + 1)
                act.activation(w_high[:, i, :], w[:, i, :], ACT.Copy).then_inc(halved, 1)
                wait(act, summed, (q - 1) * 2)
                for j in range(T):
                    ins = act.activation(high[:, i, j, :], onehot[:, d % 3, j, :], ACT.Copy, scale=w[:, i, j:j + 1])
                ins.then_inc(highs, 1)

            def keep(it, d, h):
                g = (it * RING + d) * 2 + h
                tile = act.value_load(s["tile32"][0:1, bass.ds(g, 1)], min_val=0, max_val=NT)
                act.wait_ge(added, g + 1)
                wait(act, kept, g)
                act.nop()
                act.activation(row(acc, tile), run[:, d % 3, h, :], ACT.Copy).then_inc(kept, 1)

            def period(it, d):
                if shift(it, d, -3):
                    keep(*shift(it, d, -3), 0)
                weigh_high(it, d)
                if shift(it, d, -3):
                    keep(*shift(it, d, -3), 1)
                if shift(it, d, 2):
                    lift_scores(*shift(it, d, 2))
                if shift(it, d, 1):
                    members(*shift(it, d, 1))
                if shift(it, d, 2):
                    raise_scores(*shift(it, d, 2))
            lift_scores(0, 0)
            raise_scores(0, 0)
            lift_scores(0, 1)
            members(0, 0)
            raise_scores(0, 1)
            act.wait_ge(cleared, 3)
            walk(act, period)
            for n in (-3, -2, -1):
                for h in range(2):
                    keep(*shift(RINGS, REST, n), h)

        @block.tensor
        def _(pe):
            def turn(it, d):
                q = it * RING + d
                pe.wait_ge(raised_s, q + 1)
                wait(pe, membered, q)
                for j in range(T):
                    ins = pe.transpose(p_turn[:, j // G, j % G * P:(j % G + 1) * P], raised[:, d % 2, j, :], c["ident"][:, :])
                ins.then_inc(turned, 1)

            def spread_info(it, d):
                q, i = it * RING + d, d % 2
                pe.wait_ge(informed, q + 1)
                pe.wait_ge(membered, q + 1)
                wait(pe, exponents, q - 1)
                for j in range(T):
                    ins = pe.matmul(p_slot[i][:, j, :], member[:, i, j, :], row_info[:, i, j // G, :], start=True, stop=True)
                ins.then_inc(spread, 1)

            def sums(it, d):
                q, i = it * RING + d, d % 2
                pe.wait_ge(highs, q + 1)
                pe.wait_ge(lows, q + 1)
                wait(pe, added, (q - 1) * 2)
                for h in range(2):
                    for j in range(h * G, (h + 1) * G):
                        first, last = j == h * G, j == (h + 1) * G - 1
                        halves = rows[:, d * T + j, 0:SCORE].bitcast(BF16)
                        row_low, row_high = halves[:, 0:F], halves[:, F:F + AW]
                        pe.matmul(p_sum[i][h][:, :], high[:, i, j, :], row_high, start=first, stop=False)
                        pe.matmul(p_sum[i][h][:, 0:F], high[:, i, j, :], row_low, start=False, stop=False)
                        ins = pe.matmul(p_sum[i][h][:, :], low[:, i, j, :], row_high, start=False, stop=last)
                    ins.then_inc(summed, 1)

            def period(it, d):
                spread_info(it, d)
                if shift(it, d, 1):
                    turn(*shift(it, d, 1))
                if shift(it, d, -1):
                    sums(*shift(it, d, -1))
            turn(0, 0)
            walk(pe, period)
            sums(*shift(RINGS, REST, -1))

        @block.vector
        def _(dve):
            st = Steps(dve, vec)

            def stage(it, half):
                n, d0 = size(it, half), half * HALF
                q = it * RING + d0
                st.done(dve.tensor_copy(lane[:, d0 * T:(d0 + n) * T], s["rows"][:, bass.ds(q * T, n * T)]))
                st.done(dve.tensor_copy(flat(fresh[:, d0:d0 + n, :]), s["fresh"][:, bass.ds(q * 2, n * 2)]))
                st.then(dve.tensor_copy(flat(rscore[:, d0:d0 + n, :]), s["rscore"][:, bass.ds(q * 2, n * 2)]))

            def mask(d, j):
                return dve.tensor_scalar(onehot[:, d % 3, j, :], c["iota16"][:, 0:P], lane[:, d * T + j:d * T + j + 1], None, ALU.is_equal)

            def maxima(it, d, masks_too):
                q, i = it * RING + d, d % 2
                after = shift(it, d, 1) if masks_too else None
                if after:
                    wait(dve, highs, q - 1)
                    mask(after[1], 0)
                dve.wait_ge(turned, q + 1)
                st.done(dve.tensor_reduce(tile_mx[:, :], p_turn[:, :, 0:G * P], X, ALU.max))
                if after:
                    mask(after[1], 1)
                st.settle()
                dve.tensor_tensor(sum_e[:, :], tile_mx[:, :], rscore[:, d, :], ALU.add).then_inc(reduced, 1)
                if after:
                    mask(after[1], 2)
                dve.wait_ge(reduced, q + 1)
                st.done(dve.scalar_tensor_tensor(row_e[:, :], sum_e[:, :], SLOPE, sum_e[:, :], ALU.mult, ALU.max))
                wait(dve, spread, q - 1)
                st.done(dve.tensor_copy(row_info[:, i, :, 0], rscore[:, d, :]))
                if after:
                    mask(after[1], 3)
                st.settle()
                before, here = row_info[:, 1 - i, 1, 1:2], row_info[:, i, 0, 1:2]
                st.done(dve.scalar_tensor_tensor(here, before, fresh[:, d, 0:1], row_e[:, 0:1], ALU.add, ALU.max))
                if after:
                    mask(after[1], 4)
                st.settle()
                st.done(dve.scalar_tensor_tensor(drop[:, i, 0:1], before, fresh[:, d, 0:1], here, ALU.add, ALU.subtract))
                before, here = here, row_info[:, i, 1, 1:2]
                dve.scalar_tensor_tensor(here, before, fresh[:, d, 1:2], row_e[:, 1:2], ALU.add, ALU.max).then_inc(informed, 1)
                if after:
                    for j in range(5, T):
                        ins = mask(after[1], j)
                    ins.then_inc(masked, 1)
                dve.wait_ge(informed, q + 1)
                dve.scalar_tensor_tensor(drop[:, i, 1:2], before, fresh[:, d, 1:2], here, ALU.add, ALU.subtract).then_inc(dropped, 1)

            def exponent(it, d):
                q, i = it * RING + d, d % 2
                dve.wait_ge(spread, q + 1)
                st.then(dve.tensor_tensor(e1[:, :], lifted[:, d % 3, :], p_slot[i][:, :, 0], ALU.add))
                st.then(dve.scalar_tensor_tensor(e2[:, :], e1[:, :], SLOPE, e1[:, :], ALU.mult, ALU.max))
                st.then(dve.tensor_tensor(e3[:, :], e2[:, :], p_slot[i][:, :, 1], ALU.subtract))
                dve.tensor_scalar(expo[:, i, :], e3[:, :], 0.0, None, ALU.min).then_inc(exponents, 1)

            def weigh_low(it, d):
                q, i = it * RING + d, d % 2
                dve.wait_ge(halved, q + 1)
                st.then(dve.tensor_tensor(w_low[:, :], w[:, i, :], w_high[:, i, :], ALU.subtract))
                wait(dve, summed, (q - 1) * 2)
                for j in range(T):
                    ins = dve.tensor_scalar(low[:, i, j, :], onehot[:, d % 3, j, :], w_low[:, j:j + 1], None, ALU.mult)
                ins.then_inc(lows, 1)

            def add(it, d):
                q, i = it * RING + d, d % 2
                dve.wait_ge(factored, q + 1)
                wait(dve, kept, (q - 2) * 2)
                for h in range(2):
                    dve.wait_ge(summed, q * 2 + h + 1)
                    wait(dve, added, q * 2 + h)
                    before = run[:, d % 3, 0, :] if h else run[:, (d + 2) % 3, 1, :]
                    dve.scalar_tensor_tensor(run[:, d % 3, h, :], before, factor[:, d, h:h + 1], p_sum[i][h][:, :], ALU.mult, ALU.add).then_inc(added, 1)

            def period(it, d):
                if shift(it, d, -2):
                    add(*shift(it, d, -2))
                if d % HALF == 0:
                    ahead = shift(it, d, HALF)
                    if ahead and (d > 0 or not isinstance(it, int) or it > 0):
                        stage(ahead[0], ahead[1] // HALF)
                exponent(it, d)
                if shift(it, d, 1):
                    maxima(*shift(it, d, 1), True)
                weigh_low(it, d)
            dve.memset(row_info[:, :, :, :], 0.0).then_inc(cleared, 1)
            dve.memset(run[:, :, :, :], 0.0).then_inc(cleared, 1)
            dve.wait_ge(cleared, 2)
            dve.memset(acc[:, :, :], 0.0).then_inc(cleared, 1)
            stage(0, 0)
            stage(0, 1)
            for j in range(T):
                ins = mask(0, j)
            ins.then_inc(masked, 1)
            maxima(0, 0, True)
            walk(dve, period, st)
            add(*shift(RINGS, REST, -2))
            add(*shift(RINGS, REST, -1))
            dve.wait_ge(added, PAIRS * 2)


def gate(nc, c, g, x, xr, xload, acc, Wg, bg, xn_rows, x1):
    ctx = ExitStack()
    with ctx:
        sb = lambda n, s, d=FP32: ctx.enter_context(nc.sbuf_tensor(f"g_{n}", s, d))
        ps = lambda n, s, d=FP32: ctx.enter_context(nc.psum_tensor(f"g_{n}", s, d))
        sem = lambda n: ctx.enter_context(nc.semaphore(f"g_{n}"))
        RU = 4
        UNITS = (NT + 1) // 2
        PAIRED = TOPK * NT
        CHUNKS = NT // U
        xlast = sb("xlast", [P, F])
        xn = sb("xn", [P, RU, 2, F])
        inv = sb("inv", [P, NT])
        stats, mean, var, rstd = sb("stats", [P, NT, 6]), sb("mean", [P, NT]), sb("var", [P, NT]), sb("rstd", [P, NT])
        xT = sb("xT", [P, 2, 2, KT, P])
        wg, bgb = sb("wg", [P, KT, NE]), sb("bgb", [P, NE])
        logits = sb("logits", [P, NT, NE])
        top = [sb(f"top{k}", [P, NT]) for k in range(TOPK)]
        which = sb("which", [P, NT])
        same = sb("same", [P, NT, NE])
        hot = [sb(f"hot{k}", [P, NT, NE]) for k in range(TOPK)]
        ratio = sb("ratio", [P, NT])
        place = sb("place", [P, NT, NE])
        iotaE = sb("iotaE", [P, NE])
        posf = sb("posf", [P, NT])
        pos32, part32 = sb("pos32", [P, TOPK, NT], I32), sb("part32", [P, PAIRED], I32)
        lane, slot = sb("lane", [P, TOPK, NT]), sb("slot", [P, PAIRED])
        pair32, pair = sb("pair32", [P, PAIRED], I32), sb("pair", [P, PAIRED])
        spare32, spare = sb("spare32", [P, XSLOTS], I32), sb("spare", [P, XSLOTS])
        B = 7
        assert PAIRED % B == 0
        in_lane, in_slot = sb("in_lane", [P, B, P]), sb("in_slot", [P, B, XSLOTS])
        holds, empty, token = sb("holds", [P, XSLOTS]), sb("empty", [P, XSLOTS]), sb("token", [P, XSLOTS])
        R = Route(ctx, nc, c, "g_r", P, NE, NT, XG * P, XT)
        pT = [ps(f"pT{i}", [P, 2, KT, P]) for i in range(2)]
        pG = [ps(f"pG{i}", [P, 2, NE]) for i in range(2)]
        p_slot = ps("p_slot", [P, XSLOTS])
        weights, cleared, vec, spread, rooted, last_loaded = (sem(n) for n in ("weights", "cleared", "vec", "spread", "rooted", "last_loaded"))
        ready, turned, kept, multiplied, added, differ, expd = (sem(n) for n in (
            "ready", "turned", "kept", "multiplied", "added", "differ", "expd"))
        inverted, clipped, resident, x1_saved = sem("inverted"), sem("clipped"), sem("resident"), sem("x1_saved")
        numbered, made, used, put = sem("numbered"), sem("made"), sem("used"), sem("put")
        saved = [sem(f"saved{j}") for j in range(RU)]
        block = ctx.enter_context(nc.Block())

        def walk(period):
            for j in range(RU):
                period(0, j)

            def inner(eng):
                with eng.Fori(1, UNITS // RU) as it:
                    for j in range(RU):
                        period(it, j)
                period(UNITS // RU, 0)
            return inner

        def before(it, j, n):
            turns = (j - n) // RU
            it, j = (it + turns if turns else it), (j - n) % RU
            return (it, j) if not isinstance(it, int) or it >= 0 else None

        def width(it):
            return 1 if isinstance(it, int) and it == UNITS // RU else 2

        @block.sync
        def _(sp):
            sp.dma_start(wg[:, :, :], Wg.rearrange("(k p) f -> p k f", p=P)).then_inc(weights, 16)
            sp.dma_start(bgb[:, :], bg.rearrange("(a f) -> a f", a=1).partition_broadcast(P).rearrange("p a f -> p (a f)")).then_inc(weights, 16)
            sp.wait_ge(cleared, 1)
            sp.dma_start(xlast[0:LAST, :], x[(NT - 1) * P:N, :]).then_inc(last_loaded, 16)
            for k in range(CHUNKS):
                b0 = k * U
                sp.wait_ge(resident, k + 1)
                sp.dma_start(x1[b0 * P:(b0 + U) * P, :].rearrange("(b p) f -> p b f", p=P), acc[:, b0:b0 + U, 0:F]).then_inc(x1_saved, 16)
                if k + XR < CHUNKS:
                    load_x(sp, x, xr, xload, k + XR)

            def period(it, j):
                u, n = it * RU + j, width(it)
                sp.wait_ge(ready, u + 1)
                sp.nop()
                sp.dma_start(xn_rows[bass.ds(u * 2 * P, n * P), :].rearrange("(b p) f -> p b f", p=P), xn[:, j, 0:n, :]).then_inc(saved[j], 16)
            walk(period)(sp)
            sp.wait_ge(weights, 32)
            sp.wait_ge(x1_saved, 16 * CHUNKS)
            for j in range(RU):
                sp.wait_ge(saved[j], 16 * (UNITS // RU + (1 if j == 0 else 0)))

        @block.gpsimd
        def _(pool):
            pool.memset(xlast[:, :], 0.0).then_inc(cleared, 1)
            pool.iota(pair32[:, :], [[P, PAIRED]], base=1, channel_multiplier=1).then_inc(numbered, 1)
            pool.iota(spare32[:, :], [[P, XSLOTS]], base=PAIRED * P + 1, channel_multiplier=1).then_inc(numbered, 1)

        @block.scalar
        def _(act):
            act.wait_ge(inverted, 1)
            with act.Fori(0, CHUNKS) as it:
                for j in range(U):
                    here = row(acc, it * U + j)[:, 0:F]
                    ins = act.activation(here, here, ACT.Relu, scale=inv[:, bass.ds(it * U + j, 1)])
                ins.then_inc(clipped, 1)
            act.wait_ge(spread, 1)
            act.activation(rstd[:, :], var[:, :], ACT.Sqrt, bias=c["eps"][:, :]).then_inc(rooted, 1)

            def period(it, j):
                u, n = it * RU + j, width(it)
                act.wait_ge(turned, u + 1)
                wait(act, multiplied, u - 1)
                act.activation(xT[:, j % 2, 0:n, :, :], pT[j % 2][:, 0:n, :, :], ACT.Copy).then_inc(kept, 1)
            walk(period)(act)
            act.wait_ge(differ, 1)
            act.activation(ratio[:, :], ratio[:, :], ACT.Exp).then_inc(expd, 1)

        @block.tensor
        def _(pe):
            def turn(it, j):
                u = it * RU + j
                pe.wait_ge(ready, u + 1)
                wait(pe, kept, u - 1)
                for a in range(width(it)):
                    for k in range(KT):
                        ins = pe.transpose(pT[j % 2][:, a, k, :], xn[:, j, a, k * P:(k + 1) * P], c["ident"][:, :])
                ins.then_inc(turned, 1)

            def multiply(it, j):
                u = it * RU + j
                pe.wait_ge(kept, u + 1)
                wait(pe, added, u - 1)
                for a in range(width(it)):
                    for k in range(KT):
                        ins = pe.matmul(pG[j % 2][:, a, :], xT[:, j % 2, a, k, :], wg[:, k, :], start=k == 0, stop=k == KT - 1)
                ins.then_inc(multiplied, 1)

            def period(it, j):
                turn(it, j)
                if before(it, j, 1):
                    multiply(*before(it, j, 1))
            pe.wait_ge(weights, 32)
            walk(period)(pe)
            multiply(UNITS // RU, 0)
            R.tensor(pe)
            pe.wait_ge(made, 1)
            pe.matmul(p_slot[:, :], R.zero[:, :], in_slot[:, 0, :], start=True, stop=False)
            with pe.Fori(0, PAIRED // B) as it:
                for j in range(B):
                    pe.wait_ge(made, it * B + j + 1)
                    pe.matmul(p_slot[:, :], in_lane[:, j, :], in_slot[:, j, :], start=False, stop=False).then_inc(used, 1)
            pe.matmul(p_slot[:, :], R.zero[:, :], in_slot[:, B - 1, :], start=False, stop=True).then_inc(put, 1)

        @block.vector
        def _(dve):
            st = Steps(dve, vec)
            st.then(dve.tensor_scalar(inv[:, :], acc[:, 0:NT, F], 1e-30, None, ALU.max))
            dve.reciprocal(inv[:, :], inv[:, :]).then_inc(inverted, 1)
            dve.memset(R.zero[:, :], 0.0)
            dve.wait_ge(numbered, 2)
            dve.tensor_copy(pair[:, :], pair32[:, :])
            st.then(dve.tensor_copy(spare[:, :], spare32[:, :]))
            for k in range(CHUNKS):
                dve.wait_ge(clipped, k + 1)
                dve.wait_ge(xload[k % XR], 16 * (k // XR + 1))
                if k == CHUNKS - 1:
                    dve.wait_ge(last_loaded, 16)
                for b in range(k * U, (k + 1) * U):
                    xb = xr[:, k % XR, b % U, :] if b < NT - 1 else xlast[:, :]
                    st.done(dve.tensor_tensor(acc[:, b, 0:F], acc[:, b, 0:F], xb, ALU.add))
                st.settle()
                dve.sem_inc(resident, 1)
                for b in range(k * U, (k + 1) * U):
                    st.done(dve.bn_stats(stats[:, b, :], acc[:, b, 0:F]))
            st.settle()
            st.then(dve.tensor_tensor(mean[:, :], stats[:, :, 1], stats[:, :, 4], ALU.add))
            st.then(dve.tensor_tensor(rstd[:, :], stats[:, :, 1], stats[:, :, 4], ALU.subtract))
            st.then(dve.tensor_tensor(var[:, :], stats[:, :, 2], stats[:, :, 5], ALU.add))
            st.then(dve.tensor_scalar(mean[:, :], mean[:, :], 0.5, None, ALU.mult))
            st.then(dve.tensor_tensor(rstd[:, :], rstd[:, :], rstd[:, :], ALU.mult))
            st.then(dve.tensor_scalar(rstd[:, :], rstd[:, :], 0.25, None, ALU.mult))
            st.then(dve.scalar_tensor_tensor(var[:, :], var[:, :], 1.0 / F, rstd[:, :], ALU.mult, ALU.add))
            dve.sem_inc(spread, 1)
            dve.wait_ge(rooted, 1)
            st.then(dve.reciprocal(rstd[:, :], rstd[:, :]))
            dve.wait_ge(weights, 32)

            def norm(it, j):
                u = it * RU + j
                wait(dve, turned, u - RU + 1)
                wait(dve, saved[j], it * 16)
                for a in range(width(it)):
                    b = u * 2 + a
                    ins = dve.tensor_scalar(xn[:, j, a, :], row(acc, b)[:, 0:F], mean[:, bass.ds(b, 1)], rstd[:, bass.ds(b, 1)],
                                            ALU.subtract, ALU.mult)
                ins.then_inc(ready, 1)

            def add_bias(it, j):
                u, n = it * RU + j, width(it)
                dve.wait_ge(multiplied, u + 1)
                dve.tensor_tensor(logits[:, bass.ds(u * 2, n), :], pG[j % 2][:, 0:n, :], over_middle(bgb[:, :], n), ALU.add).then_inc(added, 1)

            def period(it, j):
                norm(it, j)
                if before(it, j, 2):
                    add_bias(*before(it, j, 2))
            walk(period)(dve)
            add_bias(UNITS // RU - 1, RU - 1)
            add_bias(UNITS // RU, 0)
            dve.wait_ge(added, UNITS)
            st.then(dve.tensor_copy(iotaE[:, :], c["iota"][:, 0:NE]))
            experts_of = over_middle(iotaE[:, :], NT)
            for k in range(TOPK):
                st.then(dve.tensor_reduce(top[k][:, :], logits[:, :, :], X, ALU.max))
                st.then(dve.tensor_tensor(same[:, :, :], logits[:, :, :], over_last(top[k][:, :], NE), ALU.is_equal))
                st.then(dve.tensor_scalar(same[:, :, :], same[:, :, :], -float(NE), float(NE), ALU.mult, ALU.add))
                st.then(dve.tensor_tensor(same[:, :, :], same[:, :, :], experts_of, ALU.add))
                st.then(dve.tensor_reduce(which[:, :], same[:, :, :], X, ALU.min))
                st.then(dve.tensor_tensor(hot[k][:, :, :], over_last(which[:, :], NE), experts_of, ALU.is_equal))
                if k == 0:
                    st.then(dve.scalar_tensor_tensor(flat(logits[:, :, :]), flat(hot[k][:, :, :]), FAR, flat(logits[:, :, :]), ALU.mult, ALU.add))
                st.then(dve.tensor_scalar(hot[k][:, NT - 1, :], hot[k][:, NT - 1, :], c["valid"][:, :], None, ALU.mult))
            st.then(dve.tensor_tensor(ratio[:, :], top[1][:, :], top[0][:, :], ALU.subtract))
            dve.sem_inc(differ, 1)
            st.then(dve.tensor_tensor(R.onehot[:, :, :], hot[0][:, :, :].rearrange("p b e -> p e b"), hot[1][:, :, :].rearrange("p b e -> p e b"), ALU.add))
            R.vector(dve, st)
            for k in range(TOPK):
                ep = place[:, :, :].rearrange("p b e -> p e b")
                hotk = hot[k][:, :, :].rearrange("p b e -> p e b")
                st.then(dve.tensor_tensor(ep, R.rank[:, :, :], over_last(R.base[:, :], NT), ALU.add))
                st.then(dve.tensor_tensor(ep, ep, hotk, ALU.mult))
                st.then(dve.tensor_reduce(posf[:, :], place[:, :, :], X, ALU.add))
                st.then(dve.tensor_copy(pos32[:, k, :], posf[:, :]))
            st.then(dve.tensor_scalar(part32[:, :], flat(pos32[:, :, :]), P - 1, None, ALU.bitwise_and))
            st.then(dve.tensor_copy(flat(lane[:, :, :]), part32[:, :]))
            st.then(dve.tensor_scalar(part32[:, :], flat(pos32[:, :, :]), P.bit_length() - 1, None, ALU.logical_shift_right))
            st.then(dve.tensor_copy(slot[:, :], part32[:, :]))
            st.then(dve.tensor_scalar(lane[:, :, NT - 1], lane[:, :, NT - 1], -1000.0, c["valid"][:, :], ALU.add, ALU.mult))
            st.then(dve.tensor_scalar(lane[:, :, NT - 1], lane[:, :, NT - 1], 1000.0, None, ALU.add))
            lanes = flat(lane[:, :, :])

            def masks(n, j):
                at = bass.ds(n, 1)
                dve.tensor_scalar(in_lane[:, j, :], c["iota16"][:, 0:P], lanes[:, at], pair[:, at], ALU.is_equal, ALU.mult)
                dve.tensor_scalar(in_slot[:, j, :], c["iota16"][:, 0:XSLOTS], slot[:, at], None, ALU.is_equal).then_inc(made, 1)
            for j in range(B):
                masks(j, j)
            with dve.Fori(1, PAIRED // B) as it:
                for j in range(B):
                    dve.wait_ge(used, (it - 1) * B + j + 1)
                    masks(it * B + j, j)
            st.then(dve.tensor_scalar(g["expert32"][:, :], R.kind[:, :], float(NE - 1), None, ALU.min))
            dve.wait_ge(expd, 1)
            st.then(dve.tensor_scalar(posf[:, :], ratio[:, :], 1.0, None, ALU.add))
            st.then(dve.reciprocal(g["weight"][:, 0, :], posf[:, :]))
            st.then(dve.tensor_tensor(g["weight"][:, 1, :], g["weight"][:, 0, :], ratio[:, :], ALU.mult))
            dve.wait_ge(put, 1)
            st.done(dve.tensor_scalar(empty[:, :], p_slot[:, :], 0.0, None, ALU.is_equal))
            st.done(dve.tensor_scalar(holds[:, :], p_slot[:, :], -1.0, None, ALU.add))
            st.then(dve.tensor_scalar(token[:, :], p_slot[:, :], float(NT * P), -float(NT * P), ALU.is_gt, ALU.mult))
            st.done(dve.tensor_tensor(token[:, :], token[:, :], holds[:, :], ALU.add))
            st.then(dve.tensor_tensor(empty[:, :], empty[:, :], spare[:, :], ALU.mult))
            st.done(dve.tensor_scalar(g["take"][:, :], token[:, :], 0.0, None, ALU.max))
            st.then(dve.tensor_tensor(g["give"][:, :], empty[:, :], holds[:, :], ALU.add))


def experts(nc, c, g, xn_rows, ys, W1, b1, W2, b2):
    ctx = ExitStack()
    with ctx:
        sb = lambda n, s, d=FP32: ctx.enter_context(nc.sbuf_tensor(f"e_{n}", s, d))
        ps = lambda n, s, d=FP32: ctx.enter_context(nc.psum_tensor(f"e_{n}", s, d))
        sem = lambda n: ctx.enter_context(nc.semaphore(f"e_{n}"))
        T = XG * P
        w1h, w1l = sb("w1h", [P, NE * KT, H], BF16), sb("w1l", [P, NE * KT, H], BF16)
        w2h, w2l = sb("w2h", [P, NE * HC, F], BF16), sb("w2l", [P, NE * HC, F], BF16)
        b1c = sb("b1c", [P, NE, HC])
        b2b = sb("b2b", [P, NE, F])
        b1r = sb("b1r", [NE * HC, P])
        xt = sb("xt", [P, 2, XG, F])
        xh, xl = sb("xh", [P, 2, KT, T], BF16), sb("xl", [P, 2, KT, T], BF16)
        hf = sb("hf", [P, 2, HC, T])
        hh, hl = sb("hh", [P, 2, HC, T], BF16), sb("hl", [P, 2, HC, T], BF16)
        yt = sb("yt", [P, 2, XG, F])
        BANKS = 4
        HPB = HC // BANKS
        pT = ps("pT", [P, KT, T])
        pH = [ps(f"pH{j}", [P, HPB, T]) for j in range(BANKS)]
        pY = [ps(f"pY{i}", [P, XG, F]) for i in range(2)]
        stage = hf
        wload = [sem(f"wload{i}") for i in range(2)]
        high, rest, biases, b1turned, b1kept = (sem(n) for n in ("high", "rest", "biases", "b1turned", "b1kept"))
        take, give = sb("take", [P, 2, XG], I32), sb("give", [P, 2, XG], I32)
        xload = [sem(f"xload{i}") for i in range(2)]
        staged, issued = sem("staged"), sem("issued")
        turned, xhigh, xrest, hidden, gelued, hhigh, hrest, out_s, biased = (sem(n) for n in (
            "turned", "xhigh", "xrest", "hidden", "gelued", "hhigh", "hrest", "out", "biased"))
        stored = [sem(f"stored{i}") for i in range(2)]
        assert KT * H == HC * T and HC * F == HC * T
        chunks = 2 * NE
        w1v = W1.rearrange("e (k p) h -> e p k h", p=P)
        w2v = W2.rearrange("e (k p) f -> e p k f", p=P)
        block = ctx.enter_context(nc.Block())

        def chunk(n):
            e = n // 2
            if n % 2 == 0:
                return w1v[e], w1h[:, e * KT:(e + 1) * KT, :], w1l[:, e * KT:(e + 1) * KT, :], H
            return w2v[e], w2h[:, e * HC:(e + 1) * HC, :], w2l[:, e * HC:(e + 1) * HC, :], F

        @block.sync
        def _(sp):
            for n in range(chunks):
                if n >= 2:
                    sp.wait_ge(rest, n - 1)
                d, _, _, width = chunk(n)
                sp.dma_start(flat(stage[:, n % 2, :, :]).rearrange("p (k f) -> p k f", f=width), d).then_inc(wload[n % 2], 16)

        @block.gpsimd
        def _(pool):
            def stage(to, table, t):
                nonlocal copies
                pool.tensor_copy(to, g[table][:, bass.ds(t * XG, XG)]).then_inc(staged, 1)
                copies = copies + 1
                pool.wait_ge(staged, copies)
                pool.sem_inc(issued, 1)

            def gather(it, i):
                t = it * 2 + i
                wait(pool, xload[i], it * 16 * XG)
                wait(pool, turned, t - 1)
                pool.nop()
                stage(take[:, i, :], "take", t)
                for a in range(XG):
                    pool.indirect_dma_start(xt[:, i, a, :], None, xn_rows, bass.IndirectOffsetOnAxis(ap=take[:, i, a:a + 1], axis=0)
                                            ).then_inc(xload[i], 16)

            def scatter(it, i):
                t = it * 2 + i
                wait(pool, stored[i], it * 16 * XG)
                pool.wait_ge(biased, t + 1)
                pool.nop()
                stage(give[:, i, :], "give", t)
                for a in range(XG):
                    pool.indirect_dma_start(ys, bass.IndirectOffsetOnAxis(ap=give[:, i, a:a + 1], axis=0), yt[:, i, a, :], None
                                            ).then_inc(stored[i], 16)
            copies = 0
            for t in range(4):
                gather(t // 2, t % 2)
            with pool.Fori(2, XT // 2) as it:
                copies = it * 4 - 4
                for i in range(2):
                    gather(it, i)
                    scatter(it - 2, i)
            copies = XT * 2 - 4
            for t in range(XT - 4, XT):
                scatter(t // 2, t % 2)
            for i in range(2):
                pool.wait_ge(stored[i], 16 * XG * (XT // 2))

        @block.scalar
        def _(act):
            act.dma_start(b1r[:, :], b1.rearrange("e (k p) -> (e k) p", p=P)).then_inc(biases, 16)
            act.dma_start(b2b[:, :, :], b2.rearrange("(a e) f -> a e f", a=1).partition_broadcast(P).rearrange("p a e f -> p (a e) f")).then_inc(biases, 16)
            for n in range(chunks):
                act.wait_ge(wload[n % 2], 16 * (n // 2 + 1))
                _, h, _, _ = chunk(n)
                act.activation(flat(h), flat(stage[:, n % 2, :, :]), ACT.Copy).then_inc(high, 1)
            act.wait_ge(b1turned, 1)
            act.activation(flat(b1c[:, :, :]), pY[0][:, 0, 0:NE * HC], ACT.Copy).then_inc(b1kept, 1)

            def x_high(t, i, first):
                act.wait_ge(turned, t + 1)
                if not first:
                    act.wait_ge(hidden, (t - 1) * BANKS)
                act.activation(xh[:, i, :, :], pT[:, :, :], ACT.Copy).then_inc(xhigh, 1)

            def gelu(t, i, first):
                e = act.value_load(g["expert32"][0:1, bass.ds(t, 1)], min_val=0, max_val=NE - 1)
                if not first:
                    act.wait_ge(hrest, (t - 1) * BANKS)
                for m in range(HC):
                    if m % HPB == 0:
                        act.wait_ge(hidden, t * BANKS + m // HPB + 1)
                        act.nop()
                    act.activation(hf[:, i, m, :], pH[m // HPB][:, m % HPB, :], ACT.Gelu,
                                   bias=b1c[:, bass.ds(e, 1), m]).then_inc(gelued, 1)
            act.wait_ge(b1kept, 1)
            act.wait_ge(rest, chunks)
            x_high(0, 0, True)
            x_high(1, 1, True)
            gelu(0, 0, True)
            x_high(2, 0, False)
            gelu(1, 1, True)
            with act.Fori(1, XT // 2 - 1) as it:
                for i in range(2):
                    x_high(it * 2 + i + 1, 1 - i, False)
                    gelu(it * 2 + i, i, False)
            x_high(XT - 1, 1, False)
            gelu(XT - 2, 0, False)
            gelu(XT - 1, 1, False)

        @block.vector
        def _(dve):
            for n in range(chunks):
                dve.wait_ge(high, n + 1)
                _, h, low, _ = chunk(n)
                dve.tensor_tensor(flat(low), flat(stage[:, n % 2, :, :]), flat(h), ALU.subtract).then_inc(rest, 1)
            dve.wait_ge(biases, 32)

            def x_rest(t, i, first):
                dve.wait_ge(xhigh, t + 1)
                if not first:
                    dve.wait_ge(hidden, (t - 1) * BANKS)
                dve.tensor_tensor(xl[:, i, :, :], pT[:, :, :], xh[:, i, :, :], ALU.subtract).then_inc(xrest, 1)

            def split(t, i, first):
                if not first:
                    dve.wait_ge(out_s, t - 1)
                for j in range(BANKS):
                    ms = slice(j * HPB, (j + 1) * HPB)
                    dve.wait_ge(gelued, t * HC + (j + 1) * HPB)
                    dve.tensor_copy(hh[:, i, ms, :], hf[:, i, ms, :]).then_inc(hhigh, 1)
                    dve.wait_ge(hhigh, t * BANKS + j + 1)
                    dve.tensor_tensor(hl[:, i, ms, :], hf[:, i, ms, :], hh[:, i, ms, :], ALU.subtract).then_inc(hrest, 1)

            def add_bias(t, it, i, first):
                e = dve.value_load(g["expert32"][0:1, bass.ds(t, 1)], min_val=0, max_val=NE - 1)
                dve.wait_ge(out_s, t + 1)
                if not first:
                    dve.wait_ge(stored[i], it * 16 * XG)
                bias = b2b[:, bass.ds(e, 1), :].rearrange("p a f -> p (a f)")
                dve.tensor_tensor(yt[:, i, :, :], pY[i][:, :, :], over_middle(bias, XG), ALU.add).then_inc(biased, 1)
            x_rest(0, 0, True)
            x_rest(1, 1, True)
            split(0, 0, True)
            x_rest(2, 0, False)
            split(1, 1, True)
            add_bias(0, 0, 0, True)
            x_rest(3, 1, False)
            split(2, 0, False)
            add_bias(1, 0, 1, True)
            with dve.Fori(1, XT // 2 - 1) as it:
                for i in range(2):
                    if i == 0:
                        x_rest(it * 2 + 2, 0, False)
                        split(it * 2 + 1, 1, False)
                    else:
                        x_rest(it * 2 + 3, 1, False)
                        split(it * 2 + 2, 0, False)
                    add_bias(it * 2 + i, it, i, False)
            split(XT - 1, 1, False)
            add_bias(XT - 2, XT // 2 - 1, 0, False)
            add_bias(XT - 1, XT // 2 - 1, 1, False)

        @block.tensor
        def _(pe):
            pe.wait_ge(biases, 32)
            pe.transpose(pY[0][:, 0, 0:NE * HC], b1r[:, :], c["ident"][0:NE * HC, 0:NE * HC]).then_inc(b1turned, 1)
            pe.wait_ge(rest, chunks)
            pe.wait_ge(b1kept, 1)

            def turn(t, it, i, first):
                pe.wait_ge(xload[i], (it + 1) * 16 * XG)
                if not first:
                    pe.wait_ge(xrest, t)
                for a in range(XG):
                    for k in range(KT):
                        ins = pe.transpose(pT[:, k, a * P:(a + 1) * P], xt[:, i, a, k * P:(k + 1) * P], c["ident"][:, :])
                ins.then_inc(turned, 1)

            def layer1(t, i, first):
                e = pe.value_load(g["expert32"][0:1, bass.ds(t, 1)], min_val=0, max_val=NE - 1)
                pe.wait_ge(xrest, t + 1)
                for m in range(HC):
                    cols = slice(m * P, (m + 1) * P)
                    if m % HPB == 0 and not first:
                        pe.wait_ge(gelued, (t - 1) * HC + m + HPB)
                    for k in range(KT):
                        wh = w1h[:, bass.ds(e * KT + k, 1), cols].rearrange("p a f -> p (a f)")
                        wl = w1l[:, bass.ds(e * KT + k, 1), cols].rearrange("p a f -> p (a f)")
                        to = pH[m // HPB][:, m % HPB, :]
                        pe.matmul(to, wh, xh[:, i, k, :], start=k == 0, stop=False)
                        pe.matmul(to, wh, xl[:, i, k, :], start=False, stop=False)
                        ins = pe.matmul(to, wl, xh[:, i, k, :], start=False, stop=k == KT - 1)
                    if m % HPB == HPB - 1:
                        ins.then_inc(hidden, 1)

            def layer2(t, i, first):
                e = pe.value_load(g["expert32"][0:1, bass.ds(t, 1)], min_val=0, max_val=NE - 1)
                if not first:
                    pe.wait_ge(biased, t - 1)
                for m in range(HC):
                    if m % HPB == 0:
                        pe.wait_ge(hrest, t * BANKS + m // HPB + 1)
                    wh = w2h[:, bass.ds(e * HC + m, 1), :].rearrange("p a f -> p (a f)")
                    wl = w2l[:, bass.ds(e * HC + m, 1), :].rearrange("p a f -> p (a f)")
                    for a in range(XG):
                        rows = slice(a * P, (a + 1) * P)
                        pe.matmul(pY[i][:, a, :], hh[:, i, m, rows], wh, start=m == 0 and a == 0, stop=False, skip_group_check=True)
                        pe.matmul(pY[i][:, a, :], hh[:, i, m, rows], wl, start=False, stop=False, skip_group_check=True)
                        ins = pe.matmul(pY[i][:, a, :], hl[:, i, m, rows], wh, start=False, stop=m == HC - 1, skip_group_check=True)
                ins.then_inc(out_s, 1)
            turn(0, 0, 0, True)
            turn(1, 0, 1, False)
            layer1(0, 0, True)
            turn(2, 1, 0, False)
            layer1(1, 1, False)
            layer2(0, 0, True)
            turn(3, 1, 1, False)
            layer1(2, 0, False)
            layer2(1, 1, True)
            with pe.Fori(2, XT // 2) as it:
                for i in range(2):
                    turn(it * 2 + i, it, i, False)
                    layer1(it * 2 + i - 1, 1 - i, False)
                    layer2(it * 2 + i - 2, i, False)
            layer1(XT - 1, 1, False)
            layer2(XT - 2, 0, False)
            layer2(XT - 1, 1, False)


def combine(nc, g, x1, ys, out):
    ctx = ExitStack()
    with ctx:
        sb = lambda n, s, d=FP32: ctx.enter_context(nc.sbuf_tensor(f"c_{n}", s, d))
        sem = lambda n: ctx.enter_context(nc.semaphore(f"c_{n}"))
        CHUNKS = NT // U
        xr = sb("x", [P, NT, F])
        y = [sb(f"y{k}", [P, NT, F]) for k in range(TOPK)]
        xload = [sem(f"xload{k}") for k in range(CHUNKS)]
        vec, mixed, stored = sem("vec"), sem("mixed"), sem("stored")
        block = ctx.enter_context(nc.Block())

        def parts(k):
            whole = [(k * U, min((k + 1) * U, NT - 1), P)]
            return whole + ([(NT - 1, NT, LAST)] if k == CHUNKS - 1 else [])

        def rows_of(dram, first, b0, b1, n):
            return dram[first + b0 * P:first + (b1 - 1) * P + n, :].rearrange("(b p) f -> p b f", p=n)

        def load(eng, to, dram, first, k):
            for b0, b1, n in parts(k):
                eng.dma_start(to[0:n, b0:b1, :], rows_of(dram, first, b0, b1, n)).then_inc(xload[k], 16)

        @block.sync
        def _(sp):
            for k in range(CHUNKS):
                load(sp, y[0], ys, 0, k)
                load(sp, xr, x1, 0, k)

        @block.scalar
        def _(act):
            for k in range(CHUNKS):
                load(act, y[1], ys, NT * P, k)
            for k in range(CHUNKS):
                act.wait_ge(mixed, k + 1)
                for b0, b1, n in parts(k):
                    act.dma_start(rows_of(out, 0, b0, b1, n), xr[0:n, b0:b1, :]).then_inc(stored, 16)
            act.wait_ge(stored, 16 * (CHUNKS + 1))

        @block.vector
        def _(dve):
            st = Steps(dve, vec)
            for k in range(CHUNKS):
                dve.wait_ge(xload[k], 16 * 3 * len(parts(k)))
                for i in range(TOPK):
                    for b0, b1, n in parts(k):
                        for b in range(b0, b1):
                            here = xr[0:n, b, :]
                            st.done(dve.scalar_tensor_tensor(here, y[i][0:n, b, :], g["weight"][0:n, i, b:b + 1], here, ALU.mult, ALU.add))
                    st.settle()
                dve.sem_inc(mixed, 1)


_INS = ["x", "src", "dst", "L0_gnn_W_w", "L0_gnn_W_b", "L0_gnn_a_w", "L0_gnn_a_b", "L0_ffn_Wg", "L0_ffn_bg",
        "L0_ffn_W1", "L0_ffn_b1", "L0_ffn_W2", "L0_ffn_b2"]


def kernel(**inputs):
    import concourse.bacc as _bacc
    from concourse.bass_utils import run_bass_kernel_spmd as _run

    nc = _bacc.Bacc("TRN2", target_bir_lowering=False, num_devices=1)
    arrays, args = {}, []
    for name in _INS:
        a = np.ascontiguousarray(inputs[name])
        arrays[f"in_{name}_dram"] = a
        args.append(nc.dram_tensor(f"in_{name}_dram", a.shape, mybir.dt.from_np(a.dtype), kind="ExternalInput").ap())
    args.append(nc.dram_tensor("out_0_dram", (N, F), FP32, kind="ExternalOutput").ap())
    gnn_moe_kernel(nc, *args)
    return _run(nc, [arrays], core_ids=[0]).results[0]["out_0_dram"]
```

```python
from contextlib import ExitStack

import numpy as np
import concourse.bass as bass
import concourse.mybir as mybir
from concourse.alu_op_type import AluOpType as ALU

FP32, BF16, FP16 = mybir.dt.float32, mybir.dt.bfloat16, mybir.dt.float16
I32 = mybir.dt.int32
ACT = mybir.ActivationFunctionType
X = mybir.AxisListType.X

P = 128
N, F, E = 6250, 256, 100000
NT = -(-N // P)
LAST = N - (NT - 1) * P
U = 7
assert NT % U == 0 and NT % 8 == 1
KT = F // P
EPS = 1e-5
SLOPE = 0.2
FAR = -1e30

EP = 125
ET = E // EP
BY_DMA = 352
G = 3
GROUPS = (E + NT * (G * P - 1)) // (G * P)
GROUPS += GROUPS % 2
PAIRS = GROUPS // 2
RING = 6
SLOTS = G * GROUPS
TW = F + 2
COUNT, SCORE = F, F + 1
AW = F + 1

NE, H = 8, 1024
HC = H // P
TOPK = 2
XG = 2
XT = (N * TOPK + NE * (XG * P - 1)) // (XG * P)
XT += XT % 2
XSLOTS = XT * XG
REGION = max(NT * ET, 2 * NE * (F // P) * H, 2 * NT * F, 2 * RING * 2 * G * TW)
CH = 8
XR = 3


class Steps:

    def __init__(self, eng, sem):
        self.eng, self.sem, self.base, self.n = eng, sem, 0, 0

    def done(self, ins):
        ins.then_inc(self.sem, 1)
        self.n += 1

    def settle(self):
        self.eng.wait_ge(self.sem, self.base + self.n)

    def then(self, ins):
        self.done(ins)
        self.settle()


def repeat(eng, steps, count, per, body):
    start = steps.base + steps.n
    with eng.Fori(0, count) as it:
        steps.base, steps.n = it * per + start, 0
        body(it)
        assert steps.n == per, (steps.n, per)
    steps.base, steps.n = start + count * per, 0


def flat(ap):
    return ap.rearrange("p a b -> p (a b)")


def wait(eng, on, value):
    if not isinstance(value, int) or value > 0:
        eng.wait_ge(on, value)


def load_x(eng, x, xr, xload, k):
    eng.dma_start(xr[:, k % XR, :, :], x[k * CH * P:(k + 1) * CH * P, :].rearrange("(b p) f -> p b f", p=P)).then_inc(xload[k % XR], 16)


def row(ap, b):
    return ap[:, bass.ds(b, 1), :].rearrange("p b a -> p (b a)")


def over_middle(ap, n):
    return ap.unsqueeze(1).broadcast_to([ap.shape[0], n, ap.shape[1]])


def over_last(ap, n):
    return ap.unsqueeze(2).broadcast_to([ap.shape[0], ap.shape[1], n])


def carve(big, first, shape, dt=BF16):
    size = shape[0] * shape[1] * (2 if dt in (FP32, I32) else 1)
    assert first % 2 == 0 and first + size <= big.shape[1]
    return big[:, first:first + size].bitcast(dt).rearrange("p (a b) -> p a b", a=shape[0])


def gnn_moe_kernel(nc, x, src, dst, W_w, W_b, a_w, a_b, Wg, bg, W1, b1, W2, b2, out):
    with ExitStack() as ctx:
        def sb(name, shape, dt=FP32, stack=ctx):
            return stack.enter_context(nc.sbuf_tensor(name, shape, dt))

        table = nc.dram_tensor("table", (NT * P, TW), FP32, kind="Internal").ap()
        xn_rows = nc.dram_tensor("expert_in", (NT * P, F), FP32, kind="Internal").ap()
        ys = nc.dram_tensor("expert_out", (TOPK * NT * P + XSLOTS * P, F), FP32, kind="Internal").ap()
        spots = nc.dram_tensor("spots", (P * SLOTS, 1), I32, kind="Internal").ap()
        x1 = nc.dram_tensor("residual", (NT * P, F), FP32, kind="Internal").ap()

        c = {}
        c["ident"] = sb("ident", [P, P])
        c["before"] = sb("before", [P, P])
        c["ones"] = sb("ones", [P, P])
        c["iota"] = sb("iota", [P, GROUPS])
        c["iota16"] = sb("iota16", [P, SLOTS], FP16)
        c["eps"] = sb("eps", [P, 1])
        c["valid"] = sb("valid", [P, 1])
        row_score = sb("row_score", [P, NT])
        row_scoreT = sb("row_scoreT", [NT, P])
        lift = sb("lift", [P, 1])
        constants(nc, c)
        g = {}
        g["take"] = sb("take", [P, XSLOTS], I32)
        g["give"] = sb("give", [P, XSLOTS], I32)
        g["weight"] = sb("weight", [P, TOPK, NT])
        g["expert32"] = sb("expert32", [P, XT], I32)
        with ExitStack() as region:
            big = sb("region", [P, REGION], BF16, region)
            s = {}
            for name, shape, dt in [
                ("cols", [P, SLOTS], I32),
                ("rows", [P, SLOTS], FP32),
                ("tile32", [P, GROUPS], I32),
                ("fresh", [P, GROUPS], FP32),
                ("rscore", [P, GROUPS], FP32),
            ]:
                s[name] = sb(name, shape, dt, region)
            with ExitStack() as edges:
                e = {name: sb(name, [EP, ET], I32, edges) for name in ("row", "col")}
                projection(nc, c, big, x, W_w, W_b, a_w, a_b, src, dst, e, table, spots, row_score, row_scoreT, lift)
                route_edges(nc, c, big, s, e, spots, row_scoreT)
            big2 = sb("region2", [P, max(2 * (NT + 1) * AW, 2 * NE * HC * F)], BF16, region)
            acc = carve(big2, 0, (NT + 1, AW), FP32)
            w1h, w1l = (carve(big, k * NE * KT * H, (NE * KT, H)) for k in range(2))
            w2h, w2l = (carve(big2, k * NE * HC * F, (NE * HC, F)) for k in range(2))
            spare = 2 * NE * KT * H
            with ExitStack() as ahead:
                xr = sb("x_ahead", [P, XR, CH, F], FP32, ahead)
                xload = [ahead.enter_context(nc.semaphore(f"x_ahead{k}")) for k in range(XR)]
                attention(nc, c, big, s, table, acc, lift, x, xr, xload)
                gate(nc, c, g, s, big, spare, x, xr, xload, acc, Wg, bg, W1, w1h, w1l, W2, w2h, w2l, xn_rows, x1)
            experts(nc, c, g, big, spare, xn_rows, ys, w1h, w1l, w2h, w2l, b1, b2)
        combine(nc, g, x1, ys, out)


def constants(nc, c):
    with nc.sbuf_tensor("iota32", [P, SLOTS], I32) as iota32, nc.semaphore("filled") as filled, nc.Block() as block:
        @block.gpsimd
        def _(pool):
            pool.iota(iota32[:, :], [[1, SLOTS]], base=0, channel_multiplier=0).then_inc(filled, 1)
            pool.memset(c["ones"][:, :], 1.0).then_inc(filled, 1)
            pool.memset(c["ident"][:, :], 0.0).then_inc(filled, 1)
            pool.memset(c["eps"][:, :], EPS)
            pool.wait_ge(filled, 3)
            pool.affine_select(out=c["ident"][:, :], in_=c["ident"][:, :], compare_op=ALU.not_equal, fill=1.0,
                               base=0, pattern=[[-1, P]], channel_multiplier=1).then_inc(filled, 1)
            pool.affine_select(out=c["before"][:, :], in_=c["ones"][:, :], compare_op=ALU.is_gt, fill=0.0,
                               base=0, pattern=[[1, P]], channel_multiplier=-1)
            pool.affine_select(out=c["valid"][:, :], in_=c["ones"][:, 0:1], compare_op=ALU.is_gt, fill=0.0,
                               base=LAST, pattern=[[1, 1]], channel_multiplier=-1)

        @block.vector
        def _(dve):
            dve.wait_ge(filled, 4)
            dve.tensor_copy(c["iota"][:, :], iota32[:, 0:GROUPS])
            dve.tensor_copy(c["iota16"][:, :], iota32[:, :])


def projection(nc, c, big, x, W_w, W_b, a_w, a_b, src, dst, e, table, spots, row_score, row_scoreT, lift):
    ctx = ExitStack()
    with ctx:
        sb = lambda n, s, d=FP32: ctx.enter_context(nc.sbuf_tensor(n, s, d))
        ps = lambda n, s, d=FP32: ctx.enter_context(nc.psum_tensor(n, s, d))
        sem = lambda n: ctx.enter_context(nc.semaphore(n))
        xa = carve(big, 0, (NT, F), FP32)
        wh = sb("p_wh", [P, NT, TW])
        whf = sb("p_whf", [P, 2, F])
        score = sb("p_score", [P, NT])
        halves = wh[:, :, 0:SCORE].bitcast(BF16)
        stats = sb("p_stats", [P, NT, 6])
        mv = sb("p_mv", [P, NT, 2])
        rstd = sb("p_rstd", [P, NT])
        xn = sb("p_xn", [P, 2, F])
        xT = sb("p_xT", [P, 2, KT, P])
        wx = sb("p_wx", [P, KT, TW])
        bx = sb("p_bx", [P, TW])
        av = sb("p_av", [P, 2, F])
        ab = sb("p_ab", [P, 1])
        junk = sb("p_junk", [P, F])
        ZQ = 3
        assert SLOTS % ZQ == 0
        zeros = sb("p_zeros", [P, SLOTS // ZQ], I32)
        low = sb("p_low", [P, 1])
        lowT = sb("p_lowT", [1, 1])
        pT = [ps(f"p_pT{i}", [P, KT, P]) for i in range(2)]
        pW = [ps(f"p_pW{i}", [P, TW]) for i in range(2)]
        pL = ps("p_pL", [P, 512])
        loaded = [sem(f"x_loaded{k}") for k in range(NT // U)]
        weights, vec, cleared = sem("w_loaded"), sem("p_vec"), sem("p_cleared")
        spread, rooted, ready = sem("var_ready"), sem("std_ready"), sem("xn_ready")
        turned, kept, multiplied, added = sem("xT_psum"), sem("xT_sbuf"), sem("wh_psum"), sem("wh_sbuf")
        low_ready, low_turned, low_one, low_all = sem("low_ready"), sem("low_turned"), sem("low_one"), sem("low_all")
        highs, lows, edges = sem("p_highs"), sem("p_lows"), sem("edges")
        shifted, rowT, stored, zeroed = sem("shifted"), sem("rowT"), sem("stored"), sem("zeroed")
        block = ctx.enter_context(nc.Block())

        @block.sync
        def _(sp):
            for k in range(NT // U):
                b0, b1 = k * U, min((k + 1) * U, NT - 1)
                sp.dma_start(xa[:, b0:b1, :], x[b0 * P:b1 * P, :].rearrange("(b p) f -> p b f", p=P)).then_inc(loaded[k], 16)
            sp.wait_ge(cleared, 1)
            sp.dma_start(xa[0:LAST, NT - 1, :], x[(NT - 1) * P:N, :]).then_inc(loaded[-1], 16)
            sp.dma_start(e["row"][:, :], src.rearrange("(p t) -> p t", p=EP)).then_inc(edges, 16)
            sp.dma_start(e["col"][:, :], dst.rearrange("(p t) -> p t", p=EP)).then_inc(edges, 16)
            sp.wait_ge(edges, 32)
            sp.wait_ge(cleared, 3)

            def store(b, n):
                sp.wait_ge(highs, b + n)
                sp.wait_ge(lows, b + n)
                sp.nop()
                sp.dma_start(table[bass.ds(b * P, n * P), :].rearrange("(b p) f -> p b f", p=P), wh[:, bass.ds(b, n), :]).then_inc(stored, 16)
            with sp.Fori(0, NT // 2) as it:
                store(it * 2, 2)
            store(NT - 1, 1)
            sp.wait_ge(stored, 16 * (NT // 2 + 1))

        @block.gpsimd
        def _(pool):
            pool.memset(xa[:, NT - 1, :], 0.0).then_inc(cleared, 1)
            pool.memset(zeros[:, :], 0).then_inc(cleared, 1)
            pool.memset(halves[:, :, 2 * COUNT:2 * COUNT + 1], 1.0)
            pool.memset(halves[:, :, 2 * COUNT + 1:2 * COUNT + 2], 0.0).then_inc(cleared, 1)

            def low_half(b, i):
                pool.wait_ge(highs, b + 1)
                pool.nop()
                pool.tensor_tensor(row(halves, b)[:, 0:F], whf[:, i, :], row(halves, b)[:, F:2 * F], ALU.subtract).then_inc(lows, 1)
            with pool.Fori(0, NT // 2) as it:
                for i in range(2):
                    low_half(it * 2 + i, i)
            low_half(NT - 1, 0)

        @block.scalar
        def _(act):
            act.dma_start(wx[:, :, 0:F], W_w.rearrange("(k p) f -> p k f", p=P)).then_inc(weights, 16)
            act.dma_start(bx[:, 0:F], W_b.rearrange("(a f) -> a f", a=1).partition_broadcast(P).rearrange("p a f -> p (a f)")).then_inc(weights, 16)
            act.dma_start(av[:, 0, :], a_w[F:2 * F].rearrange("(a f) -> a f", a=1).partition_broadcast(P).rearrange("p a f -> p (a f)")).then_inc(weights, 16)
            act.dma_start(av[:, 1, :], a_w[0:F].rearrange("(a f) -> a f", a=1).partition_broadcast(P).rearrange("p a f -> p (a f)")).then_inc(weights, 16)
            act.dma_start(ab[:, :], a_b.rearrange("(a f) -> a f", a=1).partition_broadcast(P).rearrange("p a f -> p (a f)")).then_inc(weights, 16)
            act.wait_ge(spread, 1)
            act.activation(rstd[:, :], mv[:, :, 1], ACT.Sqrt, bias=c["eps"][:, :]).then_inc(rooted, 1)
            act.wait_ge(cleared, 2)
            act.dma_start(spots.rearrange("(p q t) a -> p q (t a)", p=P, q=ZQ), over_middle(zeros[:, :], ZQ)).then_inc(zeroed, 16)

            def keep(b, i, first):
                act.wait_ge(turned, b + 1)
                if not first:
                    act.wait_ge(multiplied, b - 1)
                act.activation(xT[:, i, :, :], pT[i][:, :, :], ACT.Copy).then_inc(kept, 1)

            def high(b, i):
                act.wait_ge(added, b + 1)
                act.nop()
                act.activation(row(halves, b)[:, F:2 * F], whf[:, i, :], ACT.Copy).then_inc(highs, 1)
            keep(0, 0, True)
            keep(1, 1, True)
            with act.Fori(0, NT // 2 - 1) as it:
                for i in range(2):
                    keep(it * 2 + i + 2, i, False)
                    high(it * 2 + i, i)
            keep(NT - 1, 0, False)
            for b in range(NT - 3, NT):
                high(b, b % 2)
            act.wait_ge(zeroed, 16)

        @block.vector
        def _(dve):
            st = Steps(dve, vec)
            dve.wait_ge(weights, 80)
            for i in range(2):
                for k in range(KT):
                    st.then(dve.tensor_tensor_reduce(out=junk[:, :], in0=wx[:, k, 0:F], in1=av[:, i, :], scale=1.0, scalar=0.0,
                                                     op0=ALU.mult, op1=ALU.add, accum_out=wx[:, k, COUNT + i:COUNT + i + 1]))
                st.then(dve.tensor_tensor_reduce(out=junk[:, :], in0=bx[:, 0:F], in1=av[:, i, :], scale=1.0, scalar=0.0,
                                                 op0=ALU.mult, op1=ALU.add, accum_out=bx[:, COUNT + i:COUNT + i + 1]))
            st.then(dve.tensor_tensor(bx[:, COUNT:COUNT + 1], bx[:, COUNT:COUNT + 1], ab[:, :], ALU.add))
            for b in range(NT):
                if b % U == 0:
                    dve.wait_ge(loaded[b // U], 16 if b < NT - U else 32)
                st.done(dve.bn_stats(stats[:, b, :], xa[:, b, :]))
            st.settle()
            st.then(dve.tensor_tensor(mv[:, :, 0], stats[:, :, 1], stats[:, :, 4], ALU.add))
            st.then(dve.tensor_tensor(rstd[:, :], stats[:, :, 1], stats[:, :, 4], ALU.subtract))
            st.then(dve.tensor_tensor(mv[:, :, 1], stats[:, :, 2], stats[:, :, 5], ALU.add))
            st.then(dve.tensor_scalar(mv[:, :, 0], mv[:, :, 0], 0.5, None, ALU.mult))
            st.then(dve.tensor_tensor(rstd[:, :], rstd[:, :], rstd[:, :], ALU.mult))
            st.then(dve.tensor_scalar(rstd[:, :], rstd[:, :], 0.25, None, ALU.mult))
            st.then(dve.scalar_tensor_tensor(mv[:, :, 1], mv[:, :, 1], 1.0 / F, rstd[:, :], ALU.mult, ALU.add))
            dve.sem_inc(spread, 1)
            dve.wait_ge(rooted, 1)
            st.then(dve.reciprocal(rstd[:, :], rstd[:, :]))

            def norm(b, i, first):
                if not first:
                    dve.wait_ge(turned, b - 1)
                dve.tensor_scalar(xn[:, i, :], xa[:, bass.ds(b, 1), :].rearrange("p a f -> p (a f)"), mv[:, bass.ds(b, 1), 0], rstd[:, bass.ds(b, 1)],
                                  ALU.subtract, ALU.mult).then_inc(ready, 1)

            def add_bias(b, i, first=False):
                dve.wait_ge(multiplied, b + 1)
                if not first:
                    dve.wait_ge(lows, b - 1)
                dve.tensor_tensor(score[:, bass.ds(b, 1)], pW[i][:, COUNT:SCORE], bx[:, COUNT:SCORE], ALU.add)
                dve.tensor_tensor(row(wh, b)[:, SCORE:TW], pW[i][:, SCORE:TW], bx[:, SCORE:TW], ALU.add)
                dve.tensor_tensor(whf[:, i, :], pW[i][:, 0:F], bx[:, 0:F], ALU.add).then_inc(added, 1)
            norm(0, 0, True)
            norm(1, 1, True)
            for b in range(2):
                norm(b + 2, b, False)
                add_bias(b, b, True)
            with dve.Fori(1, NT // 2 - 1) as it:
                for i in range(2):
                    norm(it * 2 + i + 2, i, False)
                    add_bias(it * 2 + i, i)
            norm(NT - 1, 0, False)
            add_bias(NT - 3, 0)
            add_bias(NT - 2, 1)
            add_bias(NT - 1, 0)
            dve.wait_ge(added, NT)
            dve.tensor_reduce(low[:, :], wh[:, :, SCORE], X, ALU.min).then_inc(low_ready, 1)
            dve.wait_ge(low_turned, 1)
            dve.tensor_reduce(lowT[:, :], pL[0:1, 0:P], X, ALU.min).then_inc(low_one, 1)
            dve.wait_ge(low_all, 1)
            st.then(dve.tensor_scalar(lift[:, :], pL[:, P:P + 1], -1.0, 1.0, ALU.mult, ALU.add))
            st.then(dve.tensor_scalar(row_score[:, :], score[:, :], lift[:, :], None, ALU.subtract))
            dve.sem_inc(shifted, 1)
            dve.wait_ge(rowT, 1)
            dve.tensor_copy(row_scoreT[:, :], pL[0:NT, 2 * P:3 * P])

        @block.tensor
        def _(pe):
            def turn(b, i, first):
                pe.wait_ge(ready, b + 1)
                if not first:
                    pe.wait_ge(kept, b - 1)
                for k in range(KT):
                    ins = pe.transpose(pT[i][:, k, :], xn[:, i, k * P:(k + 1) * P], c["ident"][:, :])
                ins.then_inc(turned, 1)

            def multiply(b, i, first):
                pe.wait_ge(kept, b + 1)
                if not first:
                    pe.wait_ge(added, b - 1)
                for k in range(KT):
                    ins = pe.matmul(pW[i][:, :], xT[:, i, k, :], wx[:, k, :], start=k == 0, stop=k == KT - 1)
                ins.then_inc(multiplied, 1)
            turn(0, 0, True)
            turn(1, 1, True)
            multiply(0, 0, True)
            turn(2, 0, False)
            multiply(1, 1, True)
            with pe.Fori(1, NT // 2) as it:
                for i in range(2):
                    turn(it * 2 + i + 1, (i + 1) % 2, False)
                    multiply(it * 2 + i, i, False)
            multiply(NT - 1, 0, False)
            pe.wait_ge(low_ready, 1)
            pe.transpose(pL[0:1, 0:P], low[:, :], c["ident"][:, :]).then_inc(low_turned, 1)
            pe.wait_ge(low_one, 1)
            pe.matmul(pL[:, P:P + 1], c["ones"][0:1, :], lowT[:, :], start=True, stop=True).then_inc(low_all, 1)
            pe.wait_ge(shifted, 1)
            pe.transpose(pL[0:NT, 2 * P:3 * P], row_score[:, :], c["ident"][:, :]).then_inc(rowT, 1)


class Route:

    def __init__(self, ctx, nc, c, tag, parts, nb, nt, size, tiles, onehot=None):
        self.c, self.parts, self.nb, self.nt, self.size, self.tiles = c, parts, nb, nt, size, tiles
        self.per, self.shift = size // P, 11
        self.up = (1 << self.shift) // self.per + 1
        most = -(-parts * nt // P) + self.per
        assert all(n * self.up >> self.shift == n // self.per for n in range(most + 1)) and most * self.up < 1 << 24
        sb = lambda n, s, d=FP32: ctx.enter_context(nc.sbuf_tensor(f"{tag}_{n}", s, d))
        ps = lambda n, s: ctx.enter_context(nc.psum_tensor(f"{tag}_{n}", s, FP32))
        self.onehot = sb("onehot", [parts, nb, nt], FP16) if onehot is None else onehot
        self.rank = sb("rank", [parts, nb, nt], FP16)
        self.upto = sb("upto", [parts, nb])
        self.own = sb("own", [parts, nb])
        self.base = sb("base", [parts, nb])
        self.t32 = sb("t32", [P, nb], I32)
        self.need = sb("need", [P, nb])
        self.end = sb("end", [P, nb])
        self.begin = sb("begin", [P, nb])
        self.endc = sb("endc", [nb, 1])
        self.beginc = sb("beginc", [nb, 1])
        self.past = sb("past", [nb, tiles])
        self.member = sb("member", [nb, tiles])
        self.kind = sb("kind", [P, tiles])
        self.zero = sb("zero", [P, P]) if nb == NE else None
        self.p_n = ps("p_n", [P, 512])
        self.p_kind = ps("p_kind", [P, tiles])
        self.to_t = ctx.enter_context(nc.semaphore(f"{tag}_to_tensor"))
        self.to_v = ctx.enter_context(nc.semaphore(f"{tag}_to_vector"))

    def vector(self, dve, st):
        nb, nt, parts = self.nb, self.nt, self.parts
        st.then(dve.tensor_tensor_scan(flat(self.rank[:, :, :]), flat(self.onehot[:, :, :]), flat(self.onehot[:, :, :]), 0.0, ALU.add, ALU.max))
        st.then(dve.tensor_copy(self.upto[:, :], self.rank[:, :, nt - 1]))
        st.then(dve.tensor_copy(self.own[:, :], self.upto[:, :]))
        st.then(dve.tensor_tensor(self.own[:, 1:nb], self.upto[:, 1:nb], self.upto[:, 0:nb - 1], ALU.subtract))
        dve.sem_inc(self.to_t, 1)
        dve.wait_ge(self.to_v, 1)
        st.then(dve.tensor_scalar(self.t32[:, :], self.p_n[:, 0:nb], float(P - 1), None, ALU.add))
        st.then(dve.tensor_scalar(self.t32[:, :], self.t32[:, :], P.bit_length() - 1, None, ALU.logical_shift_right))
        st.then(dve.tensor_scalar(self.t32[:, :], self.t32[:, :], float(self.per - 1), float(self.up), ALU.add, ALU.mult))
        st.then(dve.tensor_scalar(self.t32[:, :], self.t32[:, :], self.shift, None, ALU.logical_shift_right))
        st.then(dve.tensor_copy(self.need[:, :], self.t32[:, :]))
        st.then(dve.tensor_tensor_scan(self.end[:, :], self.need[:, :], self.need[:, :], 0.0, ALU.add, ALU.max))
        st.then(dve.tensor_tensor(self.begin[:, :], self.end[:, :], self.need[:, :], ALU.subtract))
        st.then(dve.tensor_tensor(self.base[:, :], self.own[:, :], self.upto[:, :], ALU.subtract))
        st.then(dve.scalar_tensor_tensor(self.base[:, :], self.base[:, :], -1.0, self.p_n[0:parts, P:P + nb], ALU.add, ALU.add))
        st.then(dve.scalar_tensor_tensor(self.base[:, :], self.begin[0:parts, :], float(self.size), self.base[:, :], ALU.mult, ALU.add))
        dve.sem_inc(self.to_t, 1)
        dve.wait_ge(self.to_v, 2)
        st.then(dve.tensor_copy(self.endc[:, :], self.p_n[0:nb, 2 * P:2 * P + 1]))
        st.then(dve.tensor_copy(self.beginc[:, :], self.p_n[0:nb, 3 * P:3 * P + 1]))
        st.then(dve.tensor_scalar(self.past[:, :], self.c["iota"][0:nb, 0:self.tiles], self.endc[:, :], None, ALU.is_ge))
        st.then(dve.scalar_tensor_tensor(self.member[:, :], self.c["iota"][0:nb, 0:self.tiles], self.beginc[:, :], self.past[:, :], ALU.is_ge, ALU.subtract))
        dve.sem_inc(self.to_t, 1)
        dve.wait_ge(self.to_v, 3)
        st.then(dve.tensor_copy(self.kind[:, :], self.p_kind[:, :]))

    def tensor(self, pe):
        nb, parts = self.nb, self.parts
        pe.wait_ge(self.to_t, 1)
        pe.matmul(self.p_n[:, 0:nb], self.c["ones"][0:parts, :], self.own[:, :], start=True, stop=True)
        pe.matmul(self.p_n[0:parts, P:P + nb], self.c["before"][0:parts, 0:parts], self.own[:, :], start=True, stop=True).then_inc(self.to_v, 1)
        pe.wait_ge(self.to_t, 2)
        pe.transpose(self.p_n[0:nb, 2 * P:3 * P], self.end[:, :], self.c["ident"][:, :])
        pe.transpose(self.p_n[0:nb, 3 * P:4 * P], self.begin[:, :], self.c["ident"][:, :]).then_inc(self.to_v, 1)
        pe.wait_ge(self.to_t, 3)
        pe.matmul(self.p_kind[:, :], self.c["ones"][0:nb, :], self.past[:, :], start=True, stop=True).then_inc(self.to_v, 1)


def route_edges(nc, c, big, s, e, spots, row_scoreT):
    ctx = ExitStack()
    with ctx:
        sb = lambda n, s, d=FP32: ctx.enter_context(nc.sbuf_tensor(f"r_{n}", s, d))
        ps = lambda n, s, d=FP32: ctx.enter_context(nc.psum_tensor(f"r_{n}", s, d))
        sem = lambda n: ctx.enter_context(nc.semaphore(f"r_{n}"))
        row32, col32 = e["row"], e["col"]
        part32, part = sb("part32", [P, SLOTS], I32), sb("part", [P, SLOTS])
        low32, pos = part32[0:EP, 0:ET], part[0:EP, 0:ET]
        tmp32 = sb("tmp32", [EP, ET], I32)
        tile16 = sb("tile16", [EP, ET], FP16)
        high, low = sb("high", [EP, ET], FP16), sb("low", [EP, ET], FP16)
        value, address = row32, col32
        HALF = 16
        assert BY_DMA % (2 * HALF) == 0 and (ET - BY_DMA) % 4 == 0
        staged_value, staged_address = sb("staged_value", [EP, 2, HALF], I32), sb("staged_address", [EP, 2, HALF], I32)
        slot, lane = sb("slot", [EP, ET], FP16), sb("lane", [EP, ET], FP16)
        R = Route(ctx, nc, c, "r_e", EP, NT, ET, G * P, GROUPS, carve(big, 0, (NT, ET), FP16)[0:EP])
        B = 4
        lane_high, lane_low = sb("lane_high", [EP, B, P], FP16), sb("lane_low", [EP, B, P], FP16)
        in_slot = flat(R.rank[:, :, :])[:, 0:B * SLOTS].rearrange("p (j s) -> p j s", j=B)
        none = sb("none", [EP, P], FP16)
        HE = ET // 2
        PB = 4
        chosen = [v[0:EP, 0:ET].bitcast(FP16)[:, k * ET:(k + 1) * ET] for v in (s["rows"], s["cols"]) for k in range(2)]
        base_low, base_high = R.upto[:, :], R.own[:, :]
        ident16 = lane_low[:, 0, 0:EP]
        by_base = [lane_high[:, j, 0:EP] for j in range(PB)]
        based, scaled = sem("based"), sem("scaled")
        picked, summed = sem("picked"), sem("summed")
        addressed, staged, issued, fetched = sem("addressed"), sem("staged"), sem("issued"), sem("fetched")
        written = [sem(f"written{i}") for i in range(2)]
        C0 = SLOTS // 2
        p_high = [ps(f"p_high{k}", [P, C0]) for k in range(2)]
        p_low = [ps(f"p_low{k}", [P, C0]) for k in range(2)]
        p_score = ps("p_score", [P, GROUPS])
        loaded, vec, made, placed, scores, zeroed, put = (sem(n) for n in (
            "loaded", "vec", "made", "placed", "scores", "zeroed", "put"))
        block = ctx.enter_context(nc.Block())

        @block.sync
        def _(sp):
            for i in range(2):
                sp.wait_ge(written[i], BY_DMA // 2 * 16)
            sp.wait_ge(addressed, 2)
            sp.dma_start(part32[:, :], spots.rearrange("(p t) a -> p (t a)", p=P)).then_inc(fetched, 16)
            sp.wait_ge(fetched, 16)

        @block.gpsimd
        def _(pool):
            pool.wait_ge(addressed, 1)

            def scatter(it, i):
                first = ET - BY_DMA + (it * 2 + i) * HALF
                pool.tensor_copy(staged_value[:, i, :], value[:, bass.ds(first, HALF)]).then_inc(staged, 1)
                pool.tensor_copy(staged_address[:, i, :], address[:, bass.ds(first, HALF)]).then_inc(staged, 1)
                pool.wait_ge(staged, (it * 2 + i + 1) * 2)
                pool.sem_inc(issued, 1)
                for j in range(HALF):
                    pool.indirect_dma_start(spots, bass.IndirectOffsetOnAxis(ap=staged_address[:, i, j:j + 1], axis=0),
                                            staged_value[:, i, j:j + 1], None).then_inc(written[i], 16)
            for i in range(2):
                scatter(0, i)
            with pool.Fori(1, BY_DMA // (2 * HALF)) as it:
                for i in range(2):
                    pool.wait_ge(written[i], it * HALF * 16)
                    pool.nop()
                    scatter(it, i)

        @block.scalar
        def _(act):
            act.wait_ge(based, 1)
            for b in range(NT):
                if b >= PB:
                    act.wait_ge(summed, b - PB + 1)
                act.activation(by_base[b % PB], ident16, ACT.Copy, scale=base_high[:, b:b + 1]).then_inc(scaled, 1)

        @block.vector
        def _(dve):
            st = Steps(dve, vec)
            dve.memset(none[:, :], 0.0).then_inc(zeroed, 1)
            st.done(dve.tensor_scalar(low32, row32[:, :], P - 1, None, ALU.bitwise_and))
            st.done(dve.tensor_scalar(tmp32[:, :], col32[:, :], 7, 7, ALU.bitwise_and, ALU.logical_shift_left))
            st.then(dve.tensor_scalar(row32[:, :], row32[:, :], 7, None, ALU.logical_shift_right))
            st.then(dve.tensor_copy(tile16[:, :], row32[:, :]))
            st.then(dve.tensor_scalar(value[:, :], col32[:, :], 7, None, ALU.logical_shift_left))
            st.done(dve.scalar_tensor_tensor(low[:, :], tmp32[:, :], 1.0, low32, ALU.add, ALU.add))
            st.then(dve.tensor_scalar(col32[:, :], col32[:, :], 3, None, ALU.logical_shift_right))
            st.done(dve.scalar_tensor_tensor(value[:, :], value[:, :], 1.0, low32, ALU.add, ALU.add))
            st.done(dve.tensor_copy(high[:, :], col32[:, :]))
            for b in range(NT):
                st.done(dve.tensor_scalar(R.onehot[:, b, :], tile16[:, :], float(b), None, ALU.is_equal))
            st.settle()
            R.vector(dve, st)
            base32, low_part = R.t32[0:EP, :], R.need[0:EP, :].bitcast(I32)
            st.done(dve.tensor_copy(ident16, c["ident"][0:EP, 0:EP]))
            st.then(dve.tensor_copy(base32, R.base[:, :]))
            st.then(dve.tensor_scalar(low_part, base32, P - 1, None, ALU.bitwise_and))
            st.done(dve.tensor_copy(base_low, low_part))
            st.then(dve.tensor_scalar(base32, base32, 7, None, ALU.arith_shift_right))
            st.then(dve.tensor_copy(base_high, base32))
            dve.sem_inc(based, 1)
            for b in range(NT):
                if b >= PB:
                    dve.wait_ge(summed, b - PB + 1)
                dve.scalar_tensor_tensor(chosen[b % PB], R.rank[:, b, :], base_low[:, b:b + 1], R.onehot[:, b, :], ALU.add, ALU.mult).then_inc(picked, 1)
            dve.wait_ge(summed, NT)
            for k in range(2):
                w = slice(k * HE, (k + 1) * HE)
                st.then(dve.tensor_copy(pos[:, w], p_low[k][0:EP, 0:HE]))
                st.then(dve.scalar_tensor_tensor(pos[:, w], p_high[k][0:EP, 0:HE], float(P), pos[:, w], ALU.mult, ALU.add))
            st.then(dve.tensor_copy(tmp32[:, :], pos))
            st.then(dve.tensor_scalar(low32, tmp32[:, :], P - 1, None, ALU.bitwise_and))
            st.then(dve.tensor_scalar(tmp32[:, :], tmp32[:, :], 7, None, ALU.logical_shift_right))
            dve.scalar_tensor_tensor(address[:, :], low32, float(SLOTS), tmp32[:, :], ALU.mult, ALU.add).then_inc(addressed, 1)
            st.done(dve.tensor_copy(lane[:, :], low32))
            st.then(dve.tensor_copy(slot[:, :], tmp32[:, :]))
            dve.sem_inc(addressed, 1)

            def masks(t, j):
                dve.tensor_scalar(lane_high[:, j, :], c["iota16"][0:EP, 0:P], lane[:, bass.ds(t, 1)], high[:, bass.ds(t, 1)], ALU.is_equal, ALU.mult)
                dve.tensor_scalar(lane_low[:, j, :], c["iota16"][0:EP, 0:P], lane[:, bass.ds(t, 1)], low[:, bass.ds(t, 1)], ALU.is_equal, ALU.mult)
                dve.tensor_scalar(in_slot[:, j, :], c["iota16"][0:EP, :], slot[:, bass.ds(t, 1)], None, ALU.is_equal).then_inc(made, 1)
            for j in range(B):
                masks(j, j)
            with dve.Fori(1, (ET - BY_DMA) // B) as it:
                for j in range(B):
                    dve.wait_ge(placed, (it - 1) * B + j + 1)
                    masks(it * B + j, j)
            kind = R.kind
            st.done(dve.tensor_copy(s["tile32"][:, :], kind[:, :]))
            st.done(dve.memset(s["fresh"][:, 0:1], FAR))
            st.then(dve.tensor_tensor(s["fresh"][:, 1:GROUPS], kind[:, 1:GROUPS], kind[:, 0:GROUPS - 1], ALU.not_equal))
            st.then(dve.tensor_scalar(s["fresh"][:, 1:GROUPS], s["fresh"][:, 1:GROUPS], FAR, None, ALU.mult))
            dve.wait_ge(scores, 1)
            st.then(dve.tensor_copy(s["rscore"][:, :], p_score[:, :]))
            dve.wait_ge(put, 1)
            dve.wait_ge(fetched, 16)
            for k in range(2):
                w = slice(k * C0, (k + 1) * C0)
                st.then(dve.tensor_tensor(part[:, w], part32[:, w], p_low[k][:, :], ALU.add))
                st.then(dve.scalar_tensor_tensor(part[:, w], p_high[k][:, :], 8.0 * P, part[:, w], ALU.mult, ALU.add))
                st.then(dve.tensor_scalar(part32[:, w], part[:, w], -1.0, None, ALU.add))
                st.done(dve.tensor_scalar(s["cols"][:, w], part32[:, w], 7, None, ALU.arith_shift_right))
                st.then(dve.tensor_scalar(part32[:, w], part32[:, w], P - 1, None, ALU.bitwise_and))
                st.done(dve.tensor_scalar(s["rows"][:, w], part[:, w], 0.0, 1000.0, ALU.is_equal, ALU.mult))
                st.then(dve.tensor_scalar(s["cols"][:, w], s["cols"][:, w], 0, None, ALU.max))
                st.then(dve.tensor_tensor(s["rows"][:, w], s["rows"][:, w], part32[:, w], ALU.add))

        @block.tensor
        def _(pe):
            R.tensor(pe)
            pe.wait_ge(based, 1)
            for b in range(NT):
                pe.wait_ge(picked, b + 1)
                pe.wait_ge(scaled, b + 1)
                for k in range(2):
                    w = slice(k * HE, (k + 1) * HE)
                    pe.matmul(p_low[k][0:EP, 0:HE], ident16, chosen[b % PB][:, w], start=b == 0, stop=b == NT - 1)
                    ins = pe.matmul(p_high[k][0:EP, 0:HE], by_base[b % PB], R.onehot[:, b, w], start=b == 0, stop=b == NT - 1)
                ins.then_inc(summed, 1)
            pe.matmul(p_score[:, :], row_scoreT[:, :], R.member[:, :], start=True, stop=True).then_inc(scores, 1)
            pe.wait_ge(zeroed, 1)
            pe.wait_ge(made, 1)
            for p in (p_high, p_low):
                for k in range(2):
                    pe.matmul(p[k][:, :], none[:, :], in_slot[:, 0, k * C0:(k + 1) * C0], start=True, stop=False)

            def place(t, j):
                pe.wait_ge(made, t + 1)
                for p, value in ((p_high, lane_high), (p_low, lane_low)):
                    for k in range(2):
                        ins = pe.matmul(p[k][:, :], value[:, j, :], in_slot[:, j, k * C0:(k + 1) * C0], start=False, stop=False)
                ins.then_inc(placed, 1)
            with pe.Fori(0, (ET - BY_DMA) // B) as it:
                for j in range(B):
                    place(it * B + j, j)
            for p in (p_high, p_low):
                for k in range(2):
                    ins = pe.matmul(p[k][:, :], none[:, :], in_slot[:, B - 1, k * C0:(k + 1) * C0], start=False, stop=True)
            ins.then_inc(put, 1)


def attention(nc, c, big, s, table, acc, lift, x, xr, xload):
    ctx = ExitStack()
    with ctx:
        sb = lambda n, s, d=FP32: ctx.enter_context(nc.sbuf_tensor(f"a_{n}", s, d))
        ps = lambda n, s, d=FP32: ctx.enter_context(nc.psum_tensor(f"a_{n}", s, d))
        sem = lambda n: ctx.enter_context(nc.semaphore(f"a_{n}"))
        T = 2 * G
        index = sb("index", [P, RING * T], I32)
        run = sb("run", [P, 3, 2, AW])
        rows = carve(big, 0, (RING * T, TW), FP32)
        lane = sb("lane", [P, RING * T])
        fresh, rscore = sb("fresh", [P, RING, 2]), sb("rscore", [P, RING, 2])
        lifted = sb("lifted", [P, 3, T])
        onehot = sb("onehot", [P, 3, T, P], BF16)
        raised, member = (carve(big, 2 * RING * T * TW + k * 4 * T * P, (2 * T, P), FP32).rearrange("p (i j) m -> p i j m", i=2)
                          for k in range(2))
        high, low = sb("high", [P, 2, T, P], BF16), sb("low", [P, 2, T, P], BF16)
        tile_mx, sum_e, row_e = sb("tile_mx", [P, 2]), sb("sum_e", [P, 2]), sb("row_e", [P, 2])
        drop, factor = sb("drop", [P, 2, 2]), sb("factor", [P, RING, 2])
        row_info = sb("row_info", [P, 2, 2, 2])
        e1, e2, e3 = sb("e1", [P, T]), sb("e2", [P, T]), sb("e3", [P, T])
        expo, w, w_low = sb("expo", [P, 2, T]), sb("w", [P, 2, T]), sb("w_low", [P, T])
        w_high = sb("w_high", [P, 2, T], BF16)
        p_turn = ps("p_turn", [P, 2, 512])
        p_slot = [ps(f"p_slot{i}", [P, T, 2]) for i in range(2)]
        p_sum = [[ps(f"p_sum{i}{h}", [P, AW]) for h in range(2)] for i in range(2)]
        staged, issued = sem("staged"), sem("issued")
        gathered = [sem(f"gathered{d}") for d in range(RING)]
        masked, lifted_s, raised_s, turned, reduced, informed, dropped, cleared = (sem(n) for n in (
            "masked", "lifted_s", "raised_s", "turned", "reduced", "informed", "dropped", "cleared"))
        membered, spread, exponents, exps, halved, highs, lows, factored, summed, added, vec, kept = (sem(n) for n in (
            "membered", "spread", "exponents", "exps", "halved", "highs", "lows", "factored", "summed", "added", "vec", "kept"))
        block = ctx.enter_context(nc.Block())
        HALF = RING // 2
        RINGS, REST = PAIRS // RING, PAIRS % RING
        assert RING % 6 == 0 and REST >= 2 and RINGS >= 3

        def shift(it, d, n):
            it, d = (it + (d + n) // RING if (d + n) // RING else it), (d + n) % RING
            return (it, d) if not isinstance(it, int) or 0 <= it * RING + d < PAIRS else None

        def size(it, half):
            return min(HALF, PAIRS - it * RING - half * HALF) if isinstance(it, int) else HALF

        def walk(eng, period, steps=None):
            for d in range(RING):
                period(0, d)
            def ring(it):
                for d in range(RING):
                    period(it + 1, d)
            if steps is None:
                with eng.Fori(0, RINGS - 2) as it:
                    ring(it)
            else:
                repeat(eng, steps, RINGS - 2, 9 * RING + 6, ring)
            for d in range(RING):
                period(RINGS - 1, d)
            for d in range(REST):
                period(RINGS, d)

        @block.sync
        def _(sp):
            for k in range(XR):
                load_x(sp, x, xr, xload, k)

        @block.gpsimd
        def _(pool):
            def period(it, d):
                q = it * RING + d
                if d % HALF == 0:
                    n = size(it, d // HALF)
                    for e in range(d, d + n):
                        wait(pool, gathered[e], it * 16 * T)
                    pool.nop()
                    pool.tensor_copy(index[:, d * T:(d + n) * T], s["cols"][:, bass.ds(q * T, n * T)]).then_inc(staged, 1)
                    pool.wait_ge(staged, it * 2 + d // HALF + 1)
                wait(pool, summed, (q - RING + 1) * 2)
                pool.sem_inc(issued, 1)
                for j in range(d * T, (d + 1) * T):
                    pool.indirect_dma_start(rows[:, j, :], None, table, bass.IndirectOffsetOnAxis(ap=index[:, j:j + 1], axis=0)
                                            ).then_inc(gathered[d], 16)
            walk(pool, period)

        @block.scalar
        def _(act):
            def lift_scores(it, d):
                act.wait_ge(gathered[d], (it + 1) * 16 * T)
                act.activation(lifted[:, d % 3, :], rows[:, d * T:(d + 1) * T, SCORE], ACT.Identity, bias=lift[:, :]).then_inc(lifted_s, 1)

            def raise_scores(it, d):
                q = it * RING + d
                act.wait_ge(masked, q + 1)
                wait(act, turned, q - 1)
                act.wait_ge(lifted_s, q + 1)
                for j in range(T):
                    ins = act.activation(raised[:, d % 2, j, :], onehot[:, d % 3, j, :], ACT.Copy, scale=lifted[:, d % 3, j:j + 1])
                ins.then_inc(raised_s, 1)

            def members(it, d):
                q = it * RING + d
                act.wait_ge(reduced, q + 1)
                wait(act, spread, q - 1)
                act.activation(member[:, d % 2, :, :].rearrange("p (h j) m -> p h (j m)", h=2), p_turn[:, :, 0:G * P], ACT.Sign).then_inc(membered, 1)
                act.wait_ge(dropped, q + 1)
                act.activation(factor[:, d, :], drop[:, d % 2, :], ACT.Exp).then_inc(factored, 1)

            def weigh_high(it, d):
                q, i = it * RING + d, d % 2
                act.wait_ge(exponents, q + 1)
                act.activation(w[:, i, :], expo[:, i, :], ACT.Exp).then_inc(exps, 1)
                act.wait_ge(exps, q + 1)
                act.activation(w_high[:, i, :], w[:, i, :], ACT.Copy).then_inc(halved, 1)
                wait(act, summed, (q - 1) * 2)
                for j in range(T):
                    ins = act.activation(high[:, i, j, :], onehot[:, d % 3, j, :], ACT.Copy, scale=w[:, i, j:j + 1])
                ins.then_inc(highs, 1)

            def keep(it, d, h):
                g = (it * RING + d) * 2 + h
                tile = act.value_load(s["tile32"][0:1, bass.ds(g, 1)], min_val=0, max_val=NT)
                act.wait_ge(added, g + 1)
                wait(act, kept, g)
                act.nop()
                act.activation(row(acc, tile), run[:, d % 3, h, :], ACT.Copy).then_inc(kept, 1)

            def period(it, d):
                if shift(it, d, -3):
                    keep(*shift(it, d, -3), 0)
                weigh_high(it, d)
                if shift(it, d, -3):
                    keep(*shift(it, d, -3), 1)
                if shift(it, d, 2):
                    lift_scores(*shift(it, d, 2))
                if shift(it, d, 1):
                    members(*shift(it, d, 1))
                if shift(it, d, 2):
                    raise_scores(*shift(it, d, 2))
            lift_scores(0, 0)
            raise_scores(0, 0)
            lift_scores(0, 1)
            members(0, 0)
            raise_scores(0, 1)
            act.wait_ge(cleared, 3)
            walk(act, period)
            for n in (-3, -2, -1):
                for h in range(2):
                    keep(*shift(RINGS, REST, n), h)

        @block.tensor
        def _(pe):
            def turn(it, d):
                q = it * RING + d
                pe.wait_ge(raised_s, q + 1)
                wait(pe, membered, q)
                for j in range(T):
                    ins = pe.transpose(p_turn[:, j // G, j % G * P:(j % G + 1) * P], raised[:, d % 2, j, :], c["ident"][:, :])
                ins.then_inc(turned, 1)

            def spread_info(it, d):
                q, i = it * RING + d, d % 2
                pe.wait_ge(informed, q + 1)
                pe.wait_ge(membered, q + 1)
                wait(pe, exponents, q - 1)
                for j in range(T):
                    ins = pe.matmul(p_slot[i][:, j, :], member[:, i, j, :], row_info[:, i, j // G, :], start=True, stop=True)
                ins.then_inc(spread, 1)

            def sums(it, d):
                q, i = it * RING + d, d % 2
                pe.wait_ge(highs, q + 1)
                pe.wait_ge(lows, q + 1)
                wait(pe, added, (q - 1) * 2)
                for h in range(2):
                    for j in range(h * G, (h + 1) * G):
                        first, last = j == h * G, j == (h + 1) * G - 1
                        halves = rows[:, d * T + j, 0:SCORE].bitcast(BF16)
                        row_low, row_high = halves[:, 0:F], halves[:, F:F + AW]
                        pe.matmul(p_sum[i][h][:, :], high[:, i, j, :], row_high, start=first, stop=False)
                        pe.matmul(p_sum[i][h][:, 0:F], high[:, i, j, :], row_low, start=False, stop=False)
                        ins = pe.matmul(p_sum[i][h][:, :], low[:, i, j, :], row_high, start=False, stop=last)
                    ins.then_inc(summed, 1)

            def period(it, d):
                spread_info(it, d)
                if shift(it, d, 1):
                    turn(*shift(it, d, 1))
                if shift(it, d, -1):
                    sums(*shift(it, d, -1))
            turn(0, 0)
            walk(pe, period)
            sums(*shift(RINGS, REST, -1))

        @block.vector
        def _(dve):
            st = Steps(dve, vec)

            def stage(it, half):
                n, d0 = size(it, half), half * HALF
                q = it * RING + d0
                st.done(dve.tensor_copy(lane[:, d0 * T:(d0 + n) * T], s["rows"][:, bass.ds(q * T, n * T)]))
                st.done(dve.tensor_copy(flat(fresh[:, d0:d0 + n, :]), s["fresh"][:, bass.ds(q * 2, n * 2)]))
                st.then(dve.tensor_copy(flat(rscore[:, d0:d0 + n, :]), s["rscore"][:, bass.ds(q * 2, n * 2)]))

            def mask(d, j):
                return dve.tensor_scalar(onehot[:, d % 3, j, :], c["iota16"][:, 0:P], lane[:, d * T + j:d * T + j + 1], None, ALU.is_equal)

            def maxima(it, d, masks_too):
                q, i = it * RING + d, d % 2
                after = shift(it, d, 1) if masks_too else None
                if after:
                    wait(dve, highs, q - 1)
                    mask(after[1], 0)
                dve.wait_ge(turned, q + 1)
                st.done(dve.tensor_reduce(tile_mx[:, :], p_turn[:, :, 0:G * P], X, ALU.max))
                if after:
                    mask(after[1], 1)
                st.settle()
                dve.tensor_tensor(sum_e[:, :], tile_mx[:, :], rscore[:, d, :], ALU.add).then_inc(reduced, 1)
                if after:
                    mask(after[1], 2)
                dve.wait_ge(reduced, q + 1)
                st.done(dve.scalar_tensor_tensor(row_e[:, :], sum_e[:, :], SLOPE, sum_e[:, :], ALU.mult, ALU.max))
                wait(dve, spread, q - 1)
                st.done(dve.tensor_copy(row_info[:, i, :, 0], rscore[:, d, :]))
                if after:
                    mask(after[1], 3)
                st.settle()
                before, here = row_info[:, 1 - i, 1, 1:2], row_info[:, i, 0, 1:2]
                st.done(dve.scalar_tensor_tensor(here, before, fresh[:, d, 0:1], row_e[:, 0:1], ALU.add, ALU.max))
                if after:
                    mask(after[1], 4)
                st.settle()
                st.done(dve.scalar_tensor_tensor(drop[:, i, 0:1], before, fresh[:, d, 0:1], here, ALU.add, ALU.subtract))
                before, here = here, row_info[:, i, 1, 1:2]
                dve.scalar_tensor_tensor(here, before, fresh[:, d, 1:2], row_e[:, 1:2], ALU.add, ALU.max).then_inc(informed, 1)
                if after:
                    for j in range(5, T):
                        ins = mask(after[1], j)
                    ins.then_inc(masked, 1)
                dve.wait_ge(informed, q + 1)
                dve.scalar_tensor_tensor(drop[:, i, 1:2], before, fresh[:, d, 1:2], here, ALU.add, ALU.subtract).then_inc(dropped, 1)

            def exponent(it, d):
                q, i = it * RING + d, d % 2
                dve.wait_ge(spread, q + 1)
                st.then(dve.tensor_tensor(e1[:, :], lifted[:, d % 3, :], p_slot[i][:, :, 0], ALU.add))
                st.then(dve.scalar_tensor_tensor(e2[:, :], e1[:, :], SLOPE, e1[:, :], ALU.mult, ALU.max))
                st.then(dve.tensor_tensor(e3[:, :], e2[:, :], p_slot[i][:, :, 1], ALU.subtract))
                dve.tensor_scalar(expo[:, i, :], e3[:, :], 0.0, None, ALU.min).then_inc(exponents, 1)

            def weigh_low(it, d):
                q, i = it * RING + d, d % 2
                dve.wait_ge(halved, q + 1)
                st.then(dve.tensor_tensor(w_low[:, :], w[:, i, :], w_high[:, i, :], ALU.subtract))
                wait(dve, summed, (q - 1) * 2)
                for j in range(T):
                    ins = dve.tensor_scalar(low[:, i, j, :], onehot[:, d % 3, j, :], w_low[:, j:j + 1], None, ALU.mult)
                ins.then_inc(lows, 1)

            def add(it, d):
                q, i = it * RING + d, d % 2
                dve.wait_ge(factored, q + 1)
                wait(dve, kept, (q - 2) * 2)
                for h in range(2):
                    dve.wait_ge(summed, q * 2 + h + 1)
                    wait(dve, added, q * 2 + h)
                    before = run[:, d % 3, 0, :] if h else run[:, (d + 2) % 3, 1, :]
                    dve.scalar_tensor_tensor(run[:, d % 3, h, :], before, factor[:, d, h:h + 1], p_sum[i][h][:, :], ALU.mult, ALU.add).then_inc(added, 1)

            def period(it, d):
                if shift(it, d, -2):
                    add(*shift(it, d, -2))
                if d % HALF == 0:
                    ahead = shift(it, d, HALF)
                    if ahead and (d > 0 or not isinstance(it, int) or it > 0):
                        stage(ahead[0], ahead[1] // HALF)
                exponent(it, d)
                if shift(it, d, 1):
                    maxima(*shift(it, d, 1), True)
                weigh_low(it, d)
            dve.memset(row_info[:, :, :, :], 0.0).then_inc(cleared, 1)
            dve.memset(run[:, :, :, :], 0.0).then_inc(cleared, 1)
            dve.wait_ge(cleared, 2)
            dve.memset(acc[:, :, :], 0.0).then_inc(cleared, 1)
            stage(0, 0)
            stage(0, 1)
            for j in range(T):
                ins = mask(0, j)
            ins.then_inc(masked, 1)
            maxima(0, 0, True)
            walk(dve, period, st)
            add(*shift(RINGS, REST, -2))
            add(*shift(RINGS, REST, -1))
            dve.wait_ge(added, PAIRS * 2)


def gate(nc, c, g, s, big, spare_at, x, xr, xload, acc, Wg, bg, W1, w1h, w1l, W2, w2h, w2l, xn_rows, x1):
    ctx = ExitStack()
    with ctx:
        sb = lambda n, s, d=FP32: ctx.enter_context(nc.sbuf_tensor(f"g_{n}", s, d))
        ps = lambda n, s, d=FP32: ctx.enter_context(nc.psum_tensor(f"g_{n}", s, d))
        sem = lambda n: ctx.enter_context(nc.semaphore(f"g_{n}"))
        RU = 4
        UNITS = (NT + 1) // 2
        PAIRED = TOPK * NT
        B = 7
        CHUNKS = NT // CH + 1
        assert CH == 2 * RU
        xlast = sb("xlast", [P, F])
        xn = sb("xn", [P, RU, 2, F])
        inv = sb("inv", [P, NT])
        stats, mean, var, rstd = sb("stats", [P, NT, 6]), sb("mean", [P, NT]), sb("var", [P, NT]), sb("rstd", [P, NT])
        xT = carve(big, spare_at + 2 * B * (P + XSLOTS), (2 * 2 * KT, P), FP32).rearrange("p (i a k) m -> p i a k m", i=2, a=2)
        wg, bgb = sb("wg", [P, KT, NE]), sb("bgb", [P, NE])
        old = [v[:, :].bitcast(FP32)[:, 0:2 * NT * NE].rearrange("p (i b e) -> p i b e", i=2, e=NE) for v in (s["rows"], s["cols"])]
        logits, same, place = old[0][:, 0], old[0][:, 1], old[1][:, 0]
        top = [sb(f"top{k}", [P, NT]) for k in range(TOPK)]
        which = sb("which", [P, NT])
        hot = [old[1][:, 1], sb("hot", [P, NT, NE])]
        ratio = sb("ratio", [P, NT])
        iotaE = sb("iotaE", [P, NE])
        posf = sb("posf", [P, NT])
        pos32, part32 = sb("pos32", [P, TOPK, NT], I32), sb("part32", [P, PAIRED], I32)
        lane, slot = sb("lane", [P, TOPK, NT]), sb("slot", [P, PAIRED])
        pair32, pair = sb("pair32", [P, PAIRED], I32), sb("pair", [P, PAIRED])
        spare32, spare = sb("spare32", [P, XSLOTS], I32), sb("spare", [P, XSLOTS])
        assert PAIRED % B == 0
        in_lane = carve(big, spare_at, (B, P), FP32)
        in_slot = carve(big, spare_at + 2 * B * P, (B, XSLOTS), FP32)
        holds, empty, token = sb("holds", [P, XSLOTS]), sb("empty", [P, XSLOTS]), sb("token", [P, XSLOTS])
        R = Route(ctx, nc, c, "g_r", P, NE, NT, XG * P, XT)
        pT = [ps(f"pT{i}", [P, 2, KT, P]) for i in range(2)]
        pG = [ps(f"pG{i}", [P, 2, NE]) for i in range(2)]
        p_slot = ps("p_slot", [P, XSLOTS])
        weights, cleared, vec, spread, rooted, last_loaded = (sem(n) for n in ("weights", "cleared", "vec", "spread", "rooted", "last_loaded"))
        ready, turned, kept, multiplied, added, differ, expd = (sem(n) for n in (
            "ready", "turned", "kept", "multiplied", "added", "differ", "expd"))
        inverted, clipped, resident, x1_saved = sem("inverted"), sem("clipped"), sem("resident"), sem("x1_saved")
        numbered, made, used, put = sem("numbered"), sem("made"), sem("used"), sem("put")
        saved = [sem(f"saved{j}") for j in range(RU)]
        wload = [sem(f"wload{i}") for i in range(2)]
        w_high, w_low = sem("w_high"), sem("w_low")
        stage = [xr.rearrange("p a b f -> p (a b f)")[:, i * KT * H:(i + 1) * KT * H] for i in range(2)]
        w1v, w2v = W1.rearrange("e (k p) h -> e p k h", p=P), W2.rearrange("e (k p) f -> e p k f", p=P)
        halves = ([[flat(w[:, n * KT:(n + 1) * KT, :]) for w in (w1h, w1l)] for n in range(NE)]
                  + [[flat(w[:, n * HC:(n + 1) * HC, :]) for w in (w2h, w2l)] for n in range(NE)])
        block = ctx.enter_context(nc.Block())

        def walk(period):
            for it in range(UNITS // RU):
                for j in range(RU):
                    period(it, j)
            period(UNITS // RU, 0)

        def tiles(k):
            return slice(k * CH, min((k + 1) * CH, NT))

        def before(it, j, n):
            it, j = it + (j - n) // RU, (j - n) % RU
            return (it, j) if it >= 0 else None

        def width(it):
            return 1 if it == UNITS // RU else 2

        @block.sync
        def _(sp):
            sp.dma_start(wg[:, :, :], Wg.rearrange("(k p) f -> p k f", p=P)).then_inc(weights, 16)
            sp.dma_start(bgb[:, :], bg.rearrange("(a f) -> a f", a=1).partition_broadcast(P).rearrange("p a f -> p (a f)")).then_inc(weights, 16)
            sp.wait_ge(cleared, 1)
            sp.dma_start(xlast[0:LAST, :], x[(NT - 1) * P:N, :]).then_inc(last_loaded, 16)

            def chunk(k):
                b0, b1 = tiles(k).start, tiles(k).stop
                sp.wait_ge(resident, k + 1)
                sp.dma_start(x1[b0 * P:b1 * P, :].rearrange("(b p) f -> p b f", p=P), acc[:, b0:b1, 0:F]).then_inc(x1_saved, 16)
                if k + XR < CHUNKS - 1:
                    load_x(sp, x, xr, xload, k + XR)

            def period(it, j):
                u, n = it * RU + j, width(it)
                if j == 1:
                    chunk(it + 1)
                sp.wait_ge(ready, u + 1)
                sp.dma_start(xn_rows[u * 2 * P:(u * 2 + n) * P, :].rearrange("(b p) f -> p b f", p=P), xn[:, j, 0:n, :]).then_inc(saved[j], 16)
            chunk(0)
            walk(period)
            sp.wait_ge(weights, 32)
            sp.wait_ge(x1_saved, 16 * CHUNKS)
            for j in range(RU):
                sp.wait_ge(saved[j], 16 * (UNITS // RU + (1 if j == 0 else 0)))

        @block.gpsimd
        def _(pool):
            pool.memset(xlast[:, :], 0.0).then_inc(cleared, 1)
            pool.iota(pair32[:, :], [[P, PAIRED]], base=1, channel_multiplier=1).then_inc(numbered, 1)
            pool.iota(spare32[:, :], [[P, XSLOTS]], base=PAIRED * P + 1, channel_multiplier=1).then_inc(numbered, 1)
            for n in range(2 * NE):
                pool.wait_ge(w_high, n + 1)
                pool.tensor_tensor(halves[n][1], stage[n % 2], halves[n][0], ALU.subtract).then_inc(w_low, 1)

        @block.scalar
        def _(act):
            def load_weights(n):
                from_dram, width = (w1v[n], H) if n < NE else (w2v[n - NE], F)
                act.dma_start(stage[n % 2].rearrange("p (k h) -> p k h", h=width), from_dram).then_inc(wload[n % 2], 16)

            act.wait_ge(inverted, 1)

            def clip(k):
                for b in range(tiles(k).start, tiles(k).stop):
                    ins = act.activation(acc[:, b, 0:F], acc[:, b, 0:F], ACT.Relu, scale=inv[:, b:b + 1])
                ins.then_inc(clipped, 1)

            def root(k):
                act.wait_ge(spread, k + 1)
                act.activation(rstd[:, tiles(k)], var[:, tiles(k)], ACT.Sqrt, bias=c["eps"][:, :]).then_inc(rooted, 1)
            clip(0)
            clip(1)
            root(0)

            def period(it, j):
                u, n = it * RU + j, width(it)
                if j == RU - 1:
                    root(it + 1)
                act.wait_ge(turned, u + 1)
                wait(act, multiplied, u - 1)
                act.activation(xT[:, j % 2, 0:n, :, :], pT[j % 2][:, 0:n, :, :], ACT.Copy).then_inc(kept, 1)
                if j == 1 and it + 2 < CHUNKS:
                    clip(it + 2)
                if j == 1 and it == CHUNKS - 2:
                    act.wait_ge(resident, CHUNKS)
                    for n in range(2):
                        load_weights(n)
            walk(period)
            for n in range(2 * NE):
                act.wait_ge(wload[n % 2], 16 * (n // 2 + 1))
                if n == NE:
                    act.wait_ge(x1_saved, 16 * CHUNKS)
                    act.wait_ge(ready, UNITS)
                act.activation(halves[n][0], stage[n % 2], ACT.Copy).then_inc(w_high, 1)
                if n >= 1 and n + 1 < 2 * NE:
                    act.wait_ge(w_low, n)
                    load_weights(n + 1)
                if n == NE // 2:
                    act.wait_ge(differ, 1)
                    act.activation(ratio[:, :], ratio[:, :], ACT.Exp).then_inc(expd, 1)

        @block.tensor
        def _(pe):
            def turn(it, j):
                u = it * RU + j
                pe.wait_ge(ready, u + 1)
                wait(pe, kept, u - 1)
                for a in range(width(it)):
                    for k in range(KT):
                        ins = pe.transpose(pT[j % 2][:, a, k, :], xn[:, j, a, k * P:(k + 1) * P], c["ident"][:, :])
                ins.then_inc(turned, 1)

            def multiply(it, j):
                u = it * RU + j
                pe.wait_ge(kept, u + 1)
                wait(pe, added, u - 1)
                for a in range(width(it)):
                    for k in range(KT):
                        ins = pe.matmul(pG[j % 2][:, a, :], xT[:, j % 2, a, k, :], wg[:, k, :], start=k == 0, stop=k == KT - 1)
                ins.then_inc(multiplied, 1)

            def period(it, j):
                turn(it, j)
                if before(it, j, 1):
                    multiply(*before(it, j, 1))
            pe.wait_ge(weights, 32)
            walk(period)
            multiply(UNITS // RU, 0)
            R.tensor(pe)
            pe.wait_ge(made, 1)
            pe.matmul(p_slot[:, :], R.zero[:, :], in_slot[:, 0, :], start=True, stop=False)
            with pe.Fori(0, PAIRED // B) as it:
                for j in range(B):
                    pe.wait_ge(made, it * B + j + 1)
                    pe.matmul(p_slot[:, :], in_lane[:, j, :], in_slot[:, j, :], start=False, stop=False).then_inc(used, 1)
            pe.matmul(p_slot[:, :], R.zero[:, :], in_slot[:, B - 1, :], start=False, stop=True).then_inc(put, 1)

        @block.vector
        def _(dve):
            st = Steps(dve, vec)
            st.then(dve.tensor_scalar(inv[:, :], acc[:, 0:NT, F], 1e-30, None, ALU.max))
            dve.reciprocal(inv[:, :], inv[:, :]).then_inc(inverted, 1)
            dve.memset(R.zero[:, :], 0.0)
            dve.wait_ge(numbered, 2)
            dve.tensor_copy(pair[:, :], pair32[:, :])
            st.then(dve.tensor_copy(spare[:, :], spare32[:, :]))

            def residual(k):
                dve.wait_ge(clipped, k + 1)
                if k < CHUNKS - 1:
                    dve.wait_ge(xload[k % XR], 16 * (k // XR + 1))
                else:
                    dve.wait_ge(last_loaded, 16)
                for b in range(tiles(k).start, tiles(k).stop):
                    xb = xr[:, k % XR, b % CH, :] if b < NT - 1 else xlast[:, :]
                    st.done(dve.tensor_tensor(acc[:, b, 0:F], acc[:, b, 0:F], xb, ALU.add))
                st.settle()
                dve.sem_inc(resident, 1)

            def spread_of(k):
                for b in range(tiles(k).start, tiles(k).stop):
                    st.done(dve.bn_stats(stats[:, b, :], acc[:, b, 0:F]))
                st.settle()

            def variance(k):
                w = tiles(k)
                st.done(dve.tensor_tensor(mean[:, w], stats[:, w, 1], stats[:, w, 4], ALU.add))
                st.done(dve.tensor_tensor(rstd[:, w], stats[:, w, 1], stats[:, w, 4], ALU.subtract))
                st.then(dve.tensor_tensor(var[:, w], stats[:, w, 2], stats[:, w, 5], ALU.add))
                st.done(dve.tensor_scalar(mean[:, w], mean[:, w], 0.5, None, ALU.mult))
                st.then(dve.tensor_tensor(rstd[:, w], rstd[:, w], rstd[:, w], ALU.mult))
                st.then(dve.tensor_scalar(rstd[:, w], rstd[:, w], 0.25, None, ALU.mult))
                st.then(dve.scalar_tensor_tensor(var[:, w], var[:, w], 1.0 / F, rstd[:, w], ALU.mult, ALU.add))
                dve.sem_inc(spread, 1)

            def inverse(k):
                dve.wait_ge(rooted, k + 1)
                st.then(dve.reciprocal(rstd[:, tiles(k)], rstd[:, tiles(k)]))
            for step in (residual, spread_of, variance, inverse):
                step(0)
            dve.wait_ge(weights, 32)

            def norm(it, j):
                u = it * RU + j
                wait(dve, turned, u - RU + 1)
                wait(dve, saved[j], it * 16)
                for a in range(width(it)):
                    b = u * 2 + a
                    ins = dve.tensor_scalar(xn[:, j, a, :], row(acc, b)[:, 0:F], mean[:, bass.ds(b, 1)], rstd[:, bass.ds(b, 1)],
                                            ALU.subtract, ALU.mult)
                ins.then_inc(ready, 1)

            def add_bias(it, j):
                u, n = it * RU + j, width(it)
                dve.wait_ge(multiplied, u + 1)
                dve.tensor_tensor(logits[:, bass.ds(u * 2, n), :], pG[j % 2][:, 0:n, :], over_middle(bgb[:, :], n), ALU.add).then_inc(added, 1)

            def period(it, j):
                norm(it, j)
                if it + 1 < CHUNKS:
                    (residual, spread_of, variance, inverse)[j](it + 1)
                if before(it, j, 2):
                    add_bias(*before(it, j, 2))
            walk(period)
            add_bias(UNITS // RU - 1, RU - 1)
            add_bias(UNITS // RU, 0)
            dve.wait_ge(added, UNITS)
            st.then(dve.tensor_copy(iotaE[:, :], c["iota"][:, 0:NE]))
            experts_of = over_middle(iotaE[:, :], NT)
            for k in range(TOPK):
                st.then(dve.tensor_reduce(top[k][:, :], logits[:, :, :], X, ALU.max))
                st.then(dve.tensor_tensor(same[:, :, :], logits[:, :, :], over_last(top[k][:, :], NE), ALU.is_equal))
                st.then(dve.tensor_scalar(same[:, :, :], same[:, :, :], -float(NE), float(NE), ALU.mult, ALU.add))
                st.then(dve.tensor_tensor(same[:, :, :], same[:, :, :], experts_of, ALU.add))
                st.then(dve.tensor_reduce(which[:, :], same[:, :, :], X, ALU.min))
                st.then(dve.tensor_tensor(hot[k][:, :, :], over_last(which[:, :], NE), experts_of, ALU.is_equal))
                if k == 0:
                    st.then(dve.scalar_tensor_tensor(flat(logits[:, :, :]), flat(hot[k][:, :, :]), FAR, flat(logits[:, :, :]), ALU.mult, ALU.add))
                st.then(dve.tensor_scalar(hot[k][:, NT - 1, :], hot[k][:, NT - 1, :], c["valid"][:, :], None, ALU.mult))
            st.then(dve.tensor_tensor(ratio[:, :], top[1][:, :], top[0][:, :], ALU.subtract))
            dve.sem_inc(differ, 1)
            st.then(dve.tensor_tensor(R.onehot[:, :, :], hot[0][:, :, :].rearrange("p b e -> p e b"), hot[1][:, :, :].rearrange("p b e -> p e b"), ALU.add))
            R.vector(dve, st)
            for k in range(TOPK):
                ep = place[:, :, :].rearrange("p b e -> p e b")
                hotk = hot[k][:, :, :].rearrange("p b e -> p e b")
                st.then(dve.tensor_tensor(ep, R.rank[:, :, :], over_last(R.base[:, :], NT), ALU.add))
                st.then(dve.tensor_tensor(ep, ep, hotk, ALU.mult))
                st.then(dve.tensor_reduce(posf[:, :], place[:, :, :], X, ALU.add))
                st.then(dve.tensor_copy(pos32[:, k, :], posf[:, :]))
            st.then(dve.tensor_scalar(part32[:, :], flat(pos32[:, :, :]), P - 1, None, ALU.bitwise_and))
            st.then(dve.tensor_copy(flat(lane[:, :, :]), part32[:, :]))
            st.then(dve.tensor_scalar(part32[:, :], flat(pos32[:, :, :]), P.bit_length() - 1, None, ALU.logical_shift_right))
            st.then(dve.tensor_copy(slot[:, :], part32[:, :]))
            st.then(dve.tensor_scalar(lane[:, :, NT - 1], lane[:, :, NT - 1], -1000.0, c["valid"][:, :], ALU.add, ALU.mult))
            st.then(dve.tensor_scalar(lane[:, :, NT - 1], lane[:, :, NT - 1], 1000.0, None, ALU.add))
            lanes = flat(lane[:, :, :])

            def masks(n, j):
                at = bass.ds(n, 1)
                dve.tensor_scalar(in_lane[:, j, :], c["iota16"][:, 0:P], lanes[:, at], pair[:, at], ALU.is_equal, ALU.mult)
                dve.tensor_scalar(in_slot[:, j, :], c["iota16"][:, 0:XSLOTS], slot[:, at], None, ALU.is_equal).then_inc(made, 1)
            for j in range(B):
                masks(j, j)
            with dve.Fori(1, PAIRED // B) as it:
                for j in range(B):
                    dve.wait_ge(used, (it - 1) * B + j + 1)
                    masks(it * B + j, j)
            st.then(dve.tensor_scalar(g["expert32"][:, :], R.kind[:, :], float(NE - 1), None, ALU.min))
            dve.wait_ge(expd, 1)
            st.then(dve.tensor_scalar(posf[:, :], ratio[:, :], 1.0, None, ALU.add))
            st.then(dve.reciprocal(g["weight"][:, 0, :], posf[:, :]))
            st.then(dve.tensor_tensor(g["weight"][:, 1, :], g["weight"][:, 0, :], ratio[:, :], ALU.mult))
            dve.wait_ge(put, 1)
            st.done(dve.tensor_scalar(empty[:, :], p_slot[:, :], 0.0, None, ALU.is_equal))
            st.done(dve.tensor_scalar(holds[:, :], p_slot[:, :], -1.0, None, ALU.add))
            st.then(dve.tensor_scalar(token[:, :], p_slot[:, :], float(NT * P), -float(NT * P), ALU.is_gt, ALU.mult))
            st.done(dve.tensor_tensor(token[:, :], token[:, :], holds[:, :], ALU.add))
            st.then(dve.tensor_tensor(empty[:, :], empty[:, :], spare[:, :], ALU.mult))
            st.done(dve.tensor_scalar(g["take"][:, :], token[:, :], 0.0, None, ALU.max))
            st.then(dve.tensor_tensor(g["give"][:, :], empty[:, :], holds[:, :], ALU.add))


def experts(nc, c, g, big, spare_at, xn_rows, ys, w1h, w1l, w2h, w2l, b1, b2):
    ctx = ExitStack()
    with ctx:
        sb = lambda n, s, d=FP32: ctx.enter_context(nc.sbuf_tensor(f"e_{n}", s, d))
        ps = lambda n, s, d=FP32: ctx.enter_context(nc.psum_tensor(f"e_{n}", s, d))
        sem = lambda n: ctx.enter_context(nc.semaphore(f"e_{n}"))
        T = XG * P
        b1c = sb("b1c", [P, NE, HC])
        b2b = carve(big, spare_at, (NE, F), FP32)
        b1r = sb("b1r", [NE * HC, P])
        xt = sb("xt", [P, 2, XG, F])
        xh, xl = sb("xh", [P, 2, KT, T], BF16), sb("xl", [P, 2, KT, T], BF16)
        hf = sb("hf", [P, 2, HC, T])
        hh, hl = sb("hh", [P, 2, HC, T], BF16), sb("hl", [P, 2, HC, T], BF16)
        yt = sb("yt", [P, 2, XG, F])
        BANKS = 4
        HPB = HC // BANKS
        pT = ps("pT", [P, KT, T])
        pH = [ps(f"pH{j}", [P, HPB, T]) for j in range(BANKS)]
        pY = [ps(f"pY{i}", [P, XG, F]) for i in range(2)]
        biases, b1turned, b1kept = (sem(n) for n in ("biases", "b1turned", "b1kept"))
        take, give = sb("take", [P, 2, XG], I32), sb("give", [P, 2, XG], I32)
        xload = [sem(f"xload{i}") for i in range(2)]
        staged, issued = sem("staged"), sem("issued")
        turned, xhigh, xrest, hidden, gelued, hhigh, hrest, out_s, biased = (sem(n) for n in (
            "turned", "xhigh", "xrest", "hidden", "gelued", "hhigh", "hrest", "out", "biased"))
        stored = [sem(f"stored{i}") for i in range(2)]
        block = ctx.enter_context(nc.Block())

        @block.gpsimd
        def _(pool):
            def stage(to, table, t):
                nonlocal copies
                pool.tensor_copy(to, g[table][:, bass.ds(t * XG, XG)]).then_inc(staged, 1)
                copies = copies + 1
                pool.wait_ge(staged, copies)
                pool.sem_inc(issued, 1)

            def gather(it, i):
                t = it * 2 + i
                wait(pool, xload[i], it * 16 * XG)
                wait(pool, turned, t - 1)
                pool.nop()
                stage(take[:, i, :], "take", t)
                for a in range(XG):
                    pool.indirect_dma_start(xt[:, i, a, :], None, xn_rows, bass.IndirectOffsetOnAxis(ap=take[:, i, a:a + 1], axis=0)
                                            ).then_inc(xload[i], 16)

            def scatter(it, i):
                t = it * 2 + i
                wait(pool, stored[i], it * 16 * XG)
                pool.wait_ge(biased, t + 1)
                pool.nop()
                stage(give[:, i, :], "give", t)
                for a in range(XG):
                    pool.indirect_dma_start(ys, bass.IndirectOffsetOnAxis(ap=give[:, i, a:a + 1], axis=0), yt[:, i, a, :], None
                                            ).then_inc(stored[i], 16)
            copies = 0
            for t in range(4):
                gather(t // 2, t % 2)
            with pool.Fori(2, XT // 2) as it:
                copies = it * 4 - 4
                for i in range(2):
                    gather(it, i)
                    scatter(it - 2, i)
            copies = XT * 2 - 4
            for t in range(XT - 4, XT):
                scatter(t // 2, t % 2)
            for i in range(2):
                pool.wait_ge(stored[i], 16 * XG * (XT // 2))

        @block.scalar
        def _(act):
            act.dma_start(b1r[:, :], b1.rearrange("e (k p) -> (e k) p", p=P)).then_inc(biases, 16)
            act.dma_start(b2b[:, :, :], b2.rearrange("(a e) f -> a e f", a=1).partition_broadcast(P).rearrange("p a e f -> p (a e) f")).then_inc(biases, 16)
            act.wait_ge(b1turned, 1)
            act.activation(flat(b1c[:, :, :]), pY[0][:, 0, 0:NE * HC], ACT.Copy).then_inc(b1kept, 1)

            def x_high(t, i, first):
                act.wait_ge(turned, t + 1)
                if not first:
                    act.wait_ge(hidden, (t - 1) * BANKS)
                act.activation(xh[:, i, :, :], pT[:, :, :], ACT.Copy).then_inc(xhigh, 1)

            def gelu(t, i, first):
                e = act.value_load(g["expert32"][0:1, bass.ds(t, 1)], min_val=0, max_val=NE - 1)
                if not first:
                    act.wait_ge(hrest, (t - 1) * BANKS)
                for m in range(HC):
                    if m % HPB == 0:
                        act.wait_ge(hidden, t * BANKS + m // HPB + 1)
                        act.nop()
                    act.activation(hf[:, i, m, :], pH[m // HPB][:, m % HPB, :], ACT.Gelu,
                                   bias=b1c[:, bass.ds(e, 1), m]).then_inc(gelued, 1)
            act.wait_ge(b1kept, 1)
            x_high(0, 0, True)
            x_high(1, 1, True)
            gelu(0, 0, True)
            x_high(2, 0, False)
            gelu(1, 1, True)
            with act.Fori(1, XT // 2 - 1) as it:
                for i in range(2):
                    x_high(it * 2 + i + 1, 1 - i, False)
                    gelu(it * 2 + i, i, False)
            x_high(XT - 1, 1, False)
            gelu(XT - 2, 0, False)
            gelu(XT - 1, 1, False)

        @block.vector
        def _(dve):
            dve.wait_ge(biases, 32)

            def x_rest(t, i, first):
                dve.wait_ge(xhigh, t + 1)
                if not first:
                    dve.wait_ge(hidden, (t - 1) * BANKS)
                dve.tensor_tensor(xl[:, i, :, :], pT[:, :, :], xh[:, i, :, :], ALU.subtract).then_inc(xrest, 1)

            def split(t, i, first):
                if not first:
                    dve.wait_ge(out_s, t - 1)
                for j in range(BANKS):
                    ms = slice(j * HPB, (j + 1) * HPB)
                    dve.wait_ge(gelued, t * HC + (j + 1) * HPB)
                    dve.tensor_copy(hh[:, i, ms, :], hf[:, i, ms, :]).then_inc(hhigh, 1)
                    dve.wait_ge(hhigh, t * BANKS + j + 1)
                    dve.tensor_tensor(hl[:, i, ms, :], hf[:, i, ms, :], hh[:, i, ms, :], ALU.subtract).then_inc(hrest, 1)

            def add_bias(t, it, i, first):
                e = dve.value_load(g["expert32"][0:1, bass.ds(t, 1)], min_val=0, max_val=NE - 1)
                dve.wait_ge(out_s, t + 1)
                if not first:
                    dve.wait_ge(stored[i], it * 16 * XG)
                bias = b2b[:, bass.ds(e, 1), :].rearrange("p a f -> p (a f)")
                dve.tensor_tensor(yt[:, i, :, :], pY[i][:, :, :], over_middle(bias, XG), ALU.add).then_inc(biased, 1)
            x_rest(0, 0, True)
            x_rest(1, 1, True)
            split(0, 0, True)
            x_rest(2, 0, False)
            split(1, 1, True)
            add_bias(0, 0, 0, True)
            x_rest(3, 1, False)
            split(2, 0, False)
            add_bias(1, 0, 1, True)
            with dve.Fori(1, XT // 2 - 1) as it:
                for i in range(2):
                    if i == 0:
                        x_rest(it * 2 + 2, 0, False)
                        split(it * 2 + 1, 1, False)
                    else:
                        x_rest(it * 2 + 3, 1, False)
                        split(it * 2 + 2, 0, False)
                    add_bias(it * 2 + i, it, i, False)
            split(XT - 1, 1, False)
            add_bias(XT - 2, XT // 2 - 1, 0, False)
            add_bias(XT - 1, XT // 2 - 1, 1, False)

        @block.tensor
        def _(pe):
            pe.wait_ge(biases, 32)
            pe.transpose(pY[0][:, 0, 0:NE * HC], b1r[:, :], c["ident"][0:NE * HC, 0:NE * HC]).then_inc(b1turned, 1)
            pe.wait_ge(b1kept, 1)

            def turn(t, it, i, first):
                pe.wait_ge(xload[i], (it + 1) * 16 * XG)
                if not first:
                    pe.wait_ge(xrest, t)
                for a in range(XG):
                    for k in range(KT):
                        ins = pe.transpose(pT[:, k, a * P:(a + 1) * P], xt[:, i, a, k * P:(k + 1) * P], c["ident"][:, :])
                ins.then_inc(turned, 1)

            def layer1(t, i, first):
                e = pe.value_load(g["expert32"][0:1, bass.ds(t, 1)], min_val=0, max_val=NE - 1)
                pe.wait_ge(xrest, t + 1)
                for m in range(HC):
                    cols = slice(m * P, (m + 1) * P)
                    if m % HPB == 0 and not first:
                        pe.wait_ge(gelued, (t - 1) * HC + m + HPB)
                    for k in range(KT):
                        wh = w1h[:, bass.ds(e * KT + k, 1), cols].rearrange("p a f -> p (a f)")
                        wl = w1l[:, bass.ds(e * KT + k, 1), cols].rearrange("p a f -> p (a f)")
                        to = pH[m // HPB][:, m % HPB, :]
                        pe.matmul(to, wh, xh[:, i, k, :], start=k == 0, stop=False)
                        pe.matmul(to, wh, xl[:, i, k, :], start=False, stop=False)
                        ins = pe.matmul(to, wl, xh[:, i, k, :], start=False, stop=k == KT - 1)
                    if m % HPB == HPB - 1:
                        ins.then_inc(hidden, 1)

            def layer2(t, i, first):
                e = pe.value_load(g["expert32"][0:1, bass.ds(t, 1)], min_val=0, max_val=NE - 1)
                if not first:
                    pe.wait_ge(biased, t - 1)
                for m in range(HC):
                    if m % HPB == 0:
                        pe.wait_ge(hrest, t * BANKS + m // HPB + 1)
                    wh = w2h[:, bass.ds(e * HC + m, 1), :].rearrange("p a f -> p (a f)")
                    wl = w2l[:, bass.ds(e * HC + m, 1), :].rearrange("p a f -> p (a f)")
                    for a in range(XG):
                        rows = slice(a * P, (a + 1) * P)
                        pe.matmul(pY[i][:, a, :], hh[:, i, m, rows], wh, start=m == 0 and a == 0, stop=False, skip_group_check=True)
                        pe.matmul(pY[i][:, a, :], hh[:, i, m, rows], wl, start=False, stop=False, skip_group_check=True)
                        ins = pe.matmul(pY[i][:, a, :], hl[:, i, m, rows], wh, start=False, stop=m == HC - 1, skip_group_check=True)
                ins.then_inc(out_s, 1)
            turn(0, 0, 0, True)
            turn(1, 0, 1, False)
            layer1(0, 0, True)
            turn(2, 1, 0, False)
            layer1(1, 1, False)
            layer2(0, 0, True)
            turn(3, 1, 1, False)
            layer1(2, 0, False)
            layer2(1, 1, True)
            with pe.Fori(2, XT // 2) as it:
                for i in range(2):
                    turn(it * 2 + i, it, i, False)
                    layer1(it * 2 + i - 1, 1 - i, False)
                    layer2(it * 2 + i - 2, i, False)
            layer1(XT - 1, 1, False)
            layer2(XT - 2, 0, False)
            layer2(XT - 1, 1, False)


def combine(nc, g, x1, ys, out):
    ctx = ExitStack()
    with ctx:
        sb = lambda n, s, d=FP32: ctx.enter_context(nc.sbuf_tensor(f"c_{n}", s, d))
        sem = lambda n: ctx.enter_context(nc.semaphore(f"c_{n}"))
        CHUNKS = NT // U
        xr = sb("x", [P, NT, F])
        y = [sb(f"y{k}", [P, NT, F]) for k in range(TOPK)]
        xload = [sem(f"xload{k}") for k in range(CHUNKS)]
        vec, mixed, stored = sem("vec"), sem("mixed"), sem("stored")
        block = ctx.enter_context(nc.Block())

        def parts(k):
            whole = [(k * U, min((k + 1) * U, NT - 1), P)]
            return whole + ([(NT - 1, NT, LAST)] if k == CHUNKS - 1 else [])

        def rows_of(dram, first, b0, b1, n):
            return dram[first + b0 * P:first + (b1 - 1) * P + n, :].rearrange("(b p) f -> p b f", p=n)

        def load(eng, to, dram, first, k):
            for b0, b1, n in parts(k):
                eng.dma_start(to[0:n, b0:b1, :], rows_of(dram, first, b0, b1, n)).then_inc(xload[k], 16)

        @block.sync
        def _(sp):
            for k in range(CHUNKS):
                load(sp, y[0], ys, 0, k)
                load(sp, xr, x1, 0, k)

        @block.scalar
        def _(act):
            for k in range(CHUNKS):
                load(act, y[1], ys, NT * P, k)
            for k in range(CHUNKS):
                act.wait_ge(mixed, k + 1)
                for b0, b1, n in parts(k):
                    act.dma_start(rows_of(out, 0, b0, b1, n), xr[0:n, b0:b1, :]).then_inc(stored, 16)
            act.wait_ge(stored, 16 * (CHUNKS + 1))

        @block.vector
        def _(dve):
            st = Steps(dve, vec)
            for k in range(CHUNKS):
                dve.wait_ge(xload[k], 16 * 3 * len(parts(k)))
                for i in range(TOPK):
                    for b0, b1, n in parts(k):
                        for b in range(b0, b1):
                            here = xr[0:n, b, :]
                            st.done(dve.scalar_tensor_tensor(here, y[i][0:n, b, :], g["weight"][0:n, i, b:b + 1], here, ALU.mult, ALU.add))
                    st.settle()
                dve.sem_inc(mixed, 1)


_INS = ["x", "src", "dst", "L0_gnn_W_w", "L0_gnn_W_b", "L0_gnn_a_w", "L0_gnn_a_b", "L0_ffn_Wg", "L0_ffn_bg",
        "L0_ffn_W1", "L0_ffn_b1", "L0_ffn_W2", "L0_ffn_b2"]


def kernel(**inputs):
    import concourse.bacc as _bacc
    from concourse.bass_utils import run_bass_kernel_spmd as _run

    nc = _bacc.Bacc("TRN2", target_bir_lowering=False, num_devices=1)
    arrays, args = {}, []
    for name in _INS:
        a = np.ascontiguousarray(inputs[name])
        arrays[f"in_{name}_dram"] = a
        args.append(nc.dram_tensor(f"in_{name}_dram", a.shape, mybir.dt.from_np(a.dtype), kind="ExternalInput").ap())
    args.append(nc.dram_tensor("out_0_dram", (N, F), FP32, kind="ExternalOutput").ap())
    gnn_moe_kernel(nc, *args)
    return _run(nc, [arrays], core_ids=[0]).results[0]["out_0_dram"]
```
